# Optimizing a Trainium2 kernel written in Bass

```python
import numpy as np
import jax
import jax.numpy as jnp

def _softmax(x, axis=-1):
    return jax.nn.softmax(x, axis=axis)

def _gelu(x):
    return jax.nn.gelu(x, approximate=True)

def _silu(x):
    return jax.nn.silu(x)

def _sigmoid(x):
    return jax.nn.sigmoid(x)

def _layernorm(x, axis=-1, eps=1e-05):
    m = jnp.mean(x, axis=axis, keepdims=True)
    v = jnp.var(x, axis=axis, keepdims=True)
    return (x - m) / jnp.sqrt(v + eps)

def _scatter_add(tgt, idx, src, axis=0):
    return tgt.at[idx].add(src)

def _segment_sum(src, seg, n):
    return jax.ops.segment_sum(src, seg, n)
kernel_name = 'mk_gnn_resnorm_d4_gnn_r64_9a6757'

def setup_inputs(seed: int=0):
    np.random.seed(seed)
    _w = jnp.asarray

    def _rec_inputs():
        import jax
        import jax.numpy as jnp
        _gk = jax.random.key(seed)
        x = -0.000202 + 1 * jax.random.normal(jax.random.fold_in(_gk, 1), (50000, 128), jnp.float32)
        src = jax.random.randint(jax.random.fold_in(_gk, 2), (12500,), 0, 50000, jnp.int32)
        dst = jnp.minimum((50000 * jax.random.uniform(jax.random.fold_in(_gk, 3), (12500,)) ** 2.0).astype(jnp.int32), 49999)
        _o = jnp.argsort(dst, stable=True)
        src = src[_o]
        dst = dst[_o]
        edge_attr_9 = 0.000458729 + 1.00015 * jax.random.normal(jax.random.fold_in(_gk, 11), (12500, 9), jnp.float32)
        return (x, src, dst, edge_attr_9)
    x, src, dst, edge_attr_9 = _rec_inputs()

    def _L0_gnn_setup():
        import jax, jax.numpy as jnp
        import numpy as np
        N_NODES = 50000

        def _sage_layer(x, src, dst, W_l, b_l, W_r, n_nodes):
            msgs = x[src]
            agg = jax.ops.segment_sum(msgs, dst, num_segments=n_nodes)
            deg = jax.ops.segment_sum(jnp.ones((src.shape[0],), x.dtype), dst, num_segments=n_nodes)
            mean = agg / jnp.maximum(deg, 1.0)[:, None]
            return mean @ W_l + b_l + x @ W_r
        key = jax.random.key(seed)
        ks = jax.random.split(key, 8)
        d_in, d_out, n_edges = (128, 128, 10000)
        s = 1.0 / np.sqrt(d_in)
        x = jax.random.normal(ks[0], (N_NODES, d_in), dtype=jnp.float32)
        edge_index = jax.random.randint(ks[1], (2, n_edges), 0, N_NODES, dtype=jnp.int64)
        return {'x': x, 'edge_index': edge_index, 'W1_l': jax.random.normal(ks[2], (d_in, d_out), dtype=jnp.float32) * s, 'b1': jnp.zeros((d_out,), dtype=jnp.float32), 'W1_r': jax.random.normal(ks[3], (d_in, d_out), dtype=jnp.float32) * s, 'W2_l': jax.random.normal(ks[4], (d_out, d_out), dtype=jnp.float32) * s, 'b2': jnp.zeros((d_out,), dtype=jnp.float32), 'W2_r': jax.random.normal(ks[5], (d_out, d_out), dtype=jnp.float32) * s}
    _L0_gnn_all = _L0_gnn_setup()
    _L0_gnn_in = {k: v for k, v in _L0_gnn_all.items() if k in ('W1_l', 'b1', 'W1_r', 'W2_l', 'b2', 'W2_r')}
    del _L0_gnn_all

    def _L1_gnn_setup():
        import jax, jax.numpy as jnp
        import numpy as np
        from fractions import Fraction
        from math import factorial

        def _su2_cg_coeff(j1, m1, j2, m2, j3, m3):
            if m3 != m1 + m2:
                return 0.0
            vmin = int(max(-j1 + j2 + m3, -j1 + m1, 0))
            vmax = int(min(j2 + j3 + m1, j3 - j1 + j2, j3 + m3))
            f = lambda n: factorial(round(n))
            C = ((2.0 * j3 + 1.0) * Fraction(f(j3 + j1 - j2) * f(j3 - j1 + j2) * f(j1 + j2 - j3) * f(j3 + m3) * f(j3 - m3), f(j1 + j2 + j3 + 1) * f(j1 - m1) * f(j1 + m1) * f(j2 - m2) * f(j2 + m2))) ** 0.5
            S = 0
            for v in range(vmin, vmax + 1):
                S += (-1) ** (v + j2 + m2) * Fraction(f(j2 + j3 + m1 - v) * f(j1 - m1 + v), f(v) * f(j3 - j1 + j2 - v) * f(j3 + m3 - v) * f(v + j1 - j2 - m3))
            return float(C * S)

        def _change_basis_real_to_complex(l):
            q = np.zeros((2 * l + 1, 2 * l + 1), dtype=np.complex128)
            for m in range(-l, 0):
                q[l + m, l + abs(m)] = 1 / np.sqrt(2)
                q[l + m, l - abs(m)] = -1j / np.sqrt(2)
            q[l, l] = 1
            for m in range(1, l + 1):
                q[l + m, l + abs(m)] = (-1) ** m / np.sqrt(2)
                q[l + m, l - abs(m)] = 1j * (-1) ** m / np.sqrt(2)
            return (-1j) ** l * q

        def wigner_3j(l1, l2, l3):
            C = np.zeros((2 * l1 + 1, 2 * l2 + 1, 2 * l3 + 1))
            for m1 in range(-l1, l1 + 1):
                for m2 in range(-l2, l2 + 1):
                    m3 = m1 + m2
                    if abs(m3) <= l3:
                        C[l1 + m1, l2 + m2, l3 + m3] = _su2_cg_coeff(l1, m1, l2, m2, l3, m3)
            Q1 = _change_basis_real_to_complex(l1)
            Q2 = _change_basis_real_to_complex(l2)
            Q3 = _change_basis_real_to_complex(l3)
            Cc = np.einsum('ij,kl,mn,ikn->jlm', Q1, Q2, np.conj(Q3.T), C.astype(np.complex128))
            Cr = np.real(Cc)
            return Cr / np.linalg.norm(Cr)
        MUL = 32
        IRREPS_IN = [(MUL, 0, 1), (MUL, 1, -1)]
        IRREPS_SH = [(1, 0, 1), (1, 1, -1), (1, 2, 1)]
        IRREPS_OUT = [(MUL, 0, 1), (MUL, 1, -1)]
        NUM_NEIGHBORS = 10.0
        N_NODES, N_EDGES = (10000, 100000)

        def _dim(irreps):
            return sum((m * (2 * l + 1) for m, l, _ in irreps))

        def _slices(irreps):
            s, out = (0, [])
            for m, l, _ in irreps:
                d = m * (2 * l + 1)
                out.append((s, s + d))
                s += d
            return out

        def _instructions():
            ins = []
            for i1, (m1, l1, p1) in enumerate(IRREPS_IN):
                for i2, (m2, l2, p2) in enumerate(IRREPS_SH):
                    for io, (mo, lo, po) in enumerate(IRREPS_OUT):
                        if abs(l1 - l2) <= lo <= l1 + l2 and p1 * p2 == po:
                            ins.append((i1, i2, io))
            return ins
        _INSTR = _instructions()
        _SL_IN, _SL_SH, _SL_OUT = (_slices(IRREPS_IN), _slices(IRREPS_SH), _slices(IRREPS_OUT))
        _W3J = [jnp.asarray(wigner_3j(IRREPS_IN[i1][1], IRREPS_SH[i2][1], IRREPS_OUT[io][1]), dtype=jnp.float32) for i1, i2, io in _INSTR]
        _NORM = []
        for _i1, _i2, _io in _INSTR:
            _alpha = 2 * IRREPS_OUT[_io][1] + 1
            _x = sum((IRREPS_IN[j1][0] * IRREPS_SH[j2][0] for j1, j2, jo in _INSTR if jo == _io))
            _NORM.append(float(np.sqrt(_alpha / _x)))

        def _tensor_product(x1, x2, weights):
            E = x1.shape[0]
            out = jnp.zeros((E, _dim(IRREPS_OUT)), dtype=x1.dtype)
            for k, (i1, i2, io) in enumerate(_INSTR):
                m1, l1, _ = IRREPS_IN[i1]
                m2, l2, _ = IRREPS_SH[i2]
                mo, lo, _ = IRREPS_OUT[io]
                a, b = _SL_IN[i1]
                c, d = _SL_SH[i2]
                e, f = _SL_OUT[io]
                x1s = x1[:, a:b].reshape(E, m1, 2 * l1 + 1)
                x2s = x2[:, c:d].reshape(E, m2, 2 * l2 + 1)
                seg = jnp.einsum('uvw,ijk,eui,evj->ewk', weights[k], _W3J[k], x1s, x2s, optimize='optimal') * _NORM[k]
                out = out.at[:, e:f].add(seg.reshape(E, mo * (2 * lo + 1)))
            return out
        key = jax.random.key(seed)
        ks = jax.random.split(key, 8)
        x = jax.random.normal(ks[0], (N_NODES, _dim(IRREPS_IN)), dtype=jnp.float32)
        edge_index = jax.random.randint(ks[1], (2, N_EDGES), 0, N_NODES)
        edge_attr = jax.random.normal(ks[2], (N_EDGES, _dim(IRREPS_SH)), dtype=jnp.float32)
        ws = {f'w{k}': jax.random.normal(ks[3 + k], (MUL, 1, MUL), dtype=jnp.float32) for k in range(len(_INSTR))}
        return {'x': x, 'edge_index': edge_index, 'edge_attr': edge_attr, **ws}
    _L1_gnn_all = _L1_gnn_setup()
    _L1_gnn_in = {k: v for k, v in _L1_gnn_all.items() if k in ('w0', 'w1', 'w2', 'w3', 'w4')}
    del _L1_gnn_all

    def _L2_gnn_setup():
        import jax, jax.numpy as jnp
        import numpy as np
        N, E, D, H, L, FF = (50000, 500000, 128, 8, 2, 512)
        HD = D // H

        def _layernorm(x, g, b):
            mu = jnp.mean(x, axis=-1, keepdims=True)
            var = jnp.mean(jnp.square(x - mu), axis=-1, keepdims=True)
            return (x - mu) * jax.lax.rsqrt(var + 1e-05) * g + b

        def _forward(edge_index, x, Wq, bq, Wk, bk, Wv, bv, Wo, bo, Wpos, bpos, Wdeg, bdeg, ln1_g, ln1_b, ln2_g, ln2_b, W1, b1, W2, b2):
            n = x.shape[0]
            loops = jnp.arange(n, dtype=edge_index.dtype)
            src = jnp.concatenate([edge_index[0], loops])
            dst = jnp.concatenate([edge_index[1], loops])
            scale = np.float32(np.sqrt(HD))
            for l in range(L):
                xn = _layernorm(x, ln1_g[l], ln1_b[l])
                deg = jax.ops.segment_sum(jnp.ones_like(src, dtype=x.dtype), src, num_segments=n)
                deg = (deg - deg.mean()) / (jnp.std(deg, ddof=1) + 1e-06)
                pos = xn @ Wpos[l] + bpos[l] + deg[:, None] * Wdeg[l][0] + bdeg[l]
                xp = xn + pos
                q = (xp @ Wq[l] + bq[l]).reshape(n, H, HD)
                k = (xp @ Wk[l] + bk[l]).reshape(n, H, HD)
                v = (xp @ Wv[l] + bv[l]).reshape(n, H, HD)
                att = jnp.einsum('ehd,ehd->eh', q[dst], k[src]) / scale
                att = jnp.nan_to_num(jnp.clip(att, -50.0, 50.0), nan=0.0, posinf=50.0, neginf=-50.0)
                m = jax.ops.segment_max(att, dst, num_segments=n)
                ex = jnp.exp(att - m[dst])
                s = jax.ops.segment_sum(ex, dst, num_segments=n)
                alpha = ex / (s[dst] + 1e-16)
                msg = (v[src] * alpha[:, :, None]).reshape(-1, D)
                aggr = jax.ops.segment_sum(msg, dst, num_segments=n)
                x = x + (aggr @ Wo[l] + bo[l])
                h = jax.nn.gelu(_layernorm(x, ln2_g[l], ln2_b[l]) @ W1[l] + b1[l], approximate=False)
                x = x + (h @ W2[l] + b2[l])
            return x
        key = jax.random.key(seed)
        ks = jax.random.split(key, 16)
        inp = {'x': jax.random.normal(ks[0], (N, D), jnp.float32), 'edge_index': jax.random.randint(ks[1], (2, E), 0, N, jnp.int32)}

        def w(k, shape, fan_in):
            return jax.random.normal(k, shape, jnp.float32) / np.float32(np.sqrt(fan_in))
        inp['Wq'] = w(ks[2], (L, D, D), D)
        inp['Wk'] = w(ks[3], (L, D, D), D)
        inp['Wv'] = w(ks[4], (L, D, D), D)
        inp['Wo'] = w(ks[5], (L, D, D), D)
        inp['Wpos'] = w(ks[6], (L, D, D), D)
        inp['Wdeg'] = w(ks[7], (L, 1, D), 1)
        inp['W1'] = w(ks[8], (L, D, FF), D)
        inp['W2'] = w(ks[9], (L, FF, D), FF)
        for name, shape in [('bq', (L, D)), ('bk', (L, D)), ('bv', (L, D)), ('bo', (L, D)), ('bpos', (L, D)), ('bdeg', (L, D)), ('ln1_b', (L, D)), ('ln2_b', (L, D)), ('b1', (L, FF)), ('b2', (L, D))]:
            inp[name] = jnp.zeros(shape, jnp.float32)
        inp['ln1_g'] = jnp.ones((L, D), jnp.float32)
        inp['ln2_g'] = jnp.ones((L, D), jnp.float32)
        return inp
    _L2_gnn_all = _L2_gnn_setup()
    _L2_gnn_in = {k: v for k, v in _L2_gnn_all.items() if k in ('Wq', 'bq', 'Wk', 'bk', 'Wv', 'bv', 'Wo', 'bo', 'Wpos', 'bpos', 'Wdeg', 'bdeg', 'ln1_g', 'ln1_b', 'ln2_g', 'ln2_b', 'W1', 'b1', 'W2', 'b2')}
    del _L2_gnn_all

    def _L3_gnn_setup():
        import jax, jax.numpy as jnp
        import numpy as np
        N = 50000
        E = 9375
        D = 128
        L = 4
        key = jax.random.key(seed)
        k0, k1, k2, k3 = jax.random.split(key, 4)
        scale = 1.0 / np.sqrt(D)
        node_embedding = jax.random.normal(k0, (N, D), jnp.float32)
        edge_index = jax.random.randint(k1, (2, E), 0, N, dtype=jnp.int32)
        Ws_rel = jax.random.normal(k2, (L, D, D), jnp.float32) * scale
        bs_rel = jnp.zeros((L, D), jnp.float32)
        Ws_root = jax.random.normal(k3, (L, D, D), jnp.float32) * scale
        return {'node_embedding': node_embedding, 'edge_index': edge_index, 'Ws_rel': Ws_rel, 'bs_rel': bs_rel, 'Ws_root': Ws_root}
    _L3_gnn_all = _L3_gnn_setup()
    _L3_gnn_in = {k: v for k, v in _L3_gnn_all.items() if k in ('Ws_rel', 'bs_rel', 'Ws_root')}
    del _L3_gnn_all
    return {'x': x, 'src': src, 'dst': dst, 'edge_attr_9': edge_attr_9, 'L0_gnn_W1_l': _L0_gnn_in['W1_l'], 'L0_gnn_b1': _L0_gnn_in['b1'], 'L0_gnn_W1_r': _L0_gnn_in['W1_r'], 'L0_gnn_W2_l': _L0_gnn_in['W2_l'], 'L0_gnn_b2': _L0_gnn_in['b2'], 'L0_gnn_W2_r': _L0_gnn_in['W2_r'], 'L1_gnn_w0': _L1_gnn_in['w0'], 'L1_gnn_w1': _L1_gnn_in['w1'], 'L1_gnn_w2': _L1_gnn_in['w2'], 'L1_gnn_w3': _L1_gnn_in['w3'], 'L1_gnn_w4': _L1_gnn_in['w4'], 'L2_gnn_Wq': _L2_gnn_in['Wq'], 'L2_gnn_bq': _L2_gnn_in['bq'], 'L2_gnn_Wk': _L2_gnn_in['Wk'], 'L2_gnn_bk': _L2_gnn_in['bk'], 'L2_gnn_Wv': _L2_gnn_in['Wv'], 'L2_gnn_bv': _L2_gnn_in['bv'], 'L2_gnn_Wo': _L2_gnn_in['Wo'], 'L2_gnn_bo': _L2_gnn_in['bo'], 'L2_gnn_Wpos': _L2_gnn_in['Wpos'], 'L2_gnn_bpos': _L2_gnn_in['bpos'], 'L2_gnn_Wdeg': _L2_gnn_in['Wdeg'], 'L2_gnn_bdeg': _L2_gnn_in['bdeg'], 'L2_gnn_ln1_g': _L2_gnn_in['ln1_g'], 'L2_gnn_ln1_b': _L2_gnn_in['ln1_b'], 'L2_gnn_ln2_g': _L2_gnn_in['ln2_g'], 'L2_gnn_ln2_b': _L2_gnn_in['ln2_b'], 'L2_gnn_W1': _L2_gnn_in['W1'], 'L2_gnn_b1': _L2_gnn_in['b1'], 'L2_gnn_W2': _L2_gnn_in['W2'], 'L2_gnn_b2': _L2_gnn_in['b2'], 'L3_gnn_Ws_rel': _L3_gnn_in['Ws_rel'], 'L3_gnn_bs_rel': _L3_gnn_in['bs_rel'], 'L3_gnn_Ws_root': _L3_gnn_in['Ws_root']}

def reference(x, src, dst, edge_attr_9, L0_gnn_W1_l, L0_gnn_b1, L0_gnn_W1_r, L0_gnn_W2_l, L0_gnn_b2, L0_gnn_W2_r, L1_gnn_w0, L1_gnn_w1, L1_gnn_w2, L1_gnn_w3, L1_gnn_w4, L2_gnn_Wq, L2_gnn_bq, L2_gnn_Wk, L2_gnn_bk, L2_gnn_Wv, L2_gnn_bv, L2_gnn_Wo, L2_gnn_bo, L2_gnn_Wpos, L2_gnn_bpos, L2_gnn_Wdeg, L2_gnn_bdeg, L2_gnn_ln1_g, L2_gnn_ln1_b, L2_gnn_ln2_g, L2_gnn_ln2_b, L2_gnn_W1, L2_gnn_b1, L2_gnn_W2, L2_gnn_b2, L3_gnn_Ws_rel, L3_gnn_bs_rel, L3_gnn_Ws_root):
    import jax
    import jax.numpy as jnp

    def _L0_gnn_ref(x, edge_index, W1_l, b1, W1_r, W2_l, b2, W2_r):
        import jax, jax.numpy as jnp
        import numpy as np
        N_NODES = 50000

        def _sage_layer(x, src, dst, W_l, b_l, W_r, n_nodes):
            msgs = x[src]
            agg = jax.ops.segment_sum(msgs, dst, num_segments=n_nodes)
            deg = jax.ops.segment_sum(jnp.ones((src.shape[0],), x.dtype), dst, num_segments=n_nodes)
            mean = agg / jnp.maximum(deg, 1.0)[:, None]
            return mean @ W_l + b_l + x @ W_r
        src, dst = (edge_index[0], edge_index[1])
        h = jax.nn.relu(_sage_layer(x, src, dst, W1_l, b1, W1_r, N_NODES))
        h = jax.nn.relu(_sage_layer(h, src, dst, W2_l, b2, W2_r, N_NODES))
        return h

    def _L1_gnn_ref(x, edge_index, edge_attr, w0, w1, w2, w3, w4):
        import jax, jax.numpy as jnp
        import numpy as np
        from fractions import Fraction
        from math import factorial

        def _su2_cg_coeff(j1, m1, j2, m2, j3, m3):
            if m3 != m1 + m2:
                return 0.0
            vmin = int(max(-j1 + j2 + m3, -j1 + m1, 0))
            vmax = int(min(j2 + j3 + m1, j3 - j1 + j2, j3 + m3))
            f = lambda n: factorial(round(n))
            C = ((2.0 * j3 + 1.0) * Fraction(f(j3 + j1 - j2) * f(j3 - j1 + j2) * f(j1 + j2 - j3) * f(j3 + m3) * f(j3 - m3), f(j1 + j2 + j3 + 1) * f(j1 - m1) * f(j1 + m1) * f(j2 - m2) * f(j2 + m2))) ** 0.5
            S = 0
            for v in range(vmin, vmax + 1):
                S += (-1) ** (v + j2 + m2) * Fraction(f(j2 + j3 + m1 - v) * f(j1 - m1 + v), f(v) * f(j3 - j1 + j2 - v) * f(j3 + m3 - v) * f(v + j1 - j2 - m3))
            return float(C * S)

        def _change_basis_real_to_complex(l):
            q = np.zeros((2 * l + 1, 2 * l + 1), dtype=np.complex128)
            for m in range(-l, 0):
                q[l + m, l + abs(m)] = 1 / np.sqrt(2)
                q[l + m, l - abs(m)] = -1j / np.sqrt(2)
            q[l, l] = 1
            for m in range(1, l + 1):
                q[l + m, l + abs(m)] = (-1) ** m / np.sqrt(2)
                q[l + m, l - abs(m)] = 1j * (-1) ** m / np.sqrt(2)
            return (-1j) ** l * q

        def wigner_3j(l1, l2, l3):
            C = np.zeros((2 * l1 + 1, 2 * l2 + 1, 2 * l3 + 1))
            for m1 in range(-l1, l1 + 1):
                for m2 in range(-l2, l2 + 1):
                    m3 = m1 + m2
                    if abs(m3) <= l3:
                        C[l1 + m1, l2 + m2, l3 + m3] = _su2_cg_coeff(l1, m1, l2, m2, l3, m3)
            Q1 = _change_basis_real_to_complex(l1)
            Q2 = _change_basis_real_to_complex(l2)
            Q3 = _change_basis_real_to_complex(l3)
            Cc = np.einsum('ij,kl,mn,ikn->jlm', Q1, Q2, np.conj(Q3.T), C.astype(np.complex128))
            Cr = np.real(Cc)
            return Cr / np.linalg.norm(Cr)
        MUL = 32
        IRREPS_IN = [(MUL, 0, 1), (MUL, 1, -1)]
        IRREPS_SH = [(1, 0, 1), (1, 1, -1), (1, 2, 1)]
        IRREPS_OUT = [(MUL, 0, 1), (MUL, 1, -1)]
        NUM_NEIGHBORS = 10.0
        N_NODES, N_EDGES = (10000, 100000)

        def _dim(irreps):
            return sum((m * (2 * l + 1) for m, l, _ in irreps))

        def _slices(irreps):
            s, out = (0, [])
            for m, l, _ in irreps:
                d = m * (2 * l + 1)
                out.append((s, s + d))
                s += d
            return out

        def _instructions():
            ins = []
            for i1, (m1, l1, p1) in enumerate(IRREPS_IN):
                for i2, (m2, l2, p2) in enumerate(IRREPS_SH):
                    for io, (mo, lo, po) in enumerate(IRREPS_OUT):
                        if abs(l1 - l2) <= lo <= l1 + l2 and p1 * p2 == po:
                            ins.append((i1, i2, io))
            return ins
        _INSTR = _instructions()
        _SL_IN, _SL_SH, _SL_OUT = (_slices(IRREPS_IN), _slices(IRREPS_SH), _slices(IRREPS_OUT))
        _W3J = [jnp.asarray(wigner_3j(IRREPS_IN[i1][1], IRREPS_SH[i2][1], IRREPS_OUT[io][1]), dtype=jnp.float32) for i1, i2, io in _INSTR]
        _NORM = []
        for _i1, _i2, _io in _INSTR:
            _alpha = 2 * IRREPS_OUT[_io][1] + 1
            _x = sum((IRREPS_IN[j1][0] * IRREPS_SH[j2][0] for j1, j2, jo in _INSTR if jo == _io))
            _NORM.append(float(np.sqrt(_alpha / _x)))

        def _tensor_product(x1, x2, weights):
            E = x1.shape[0]
            out = jnp.zeros((E, _dim(IRREPS_OUT)), dtype=x1.dtype)
            for k, (i1, i2, io) in enumerate(_INSTR):
                m1, l1, _ = IRREPS_IN[i1]
                m2, l2, _ = IRREPS_SH[i2]
                mo, lo, _ = IRREPS_OUT[io]
                a, b = _SL_IN[i1]
                c, d = _SL_SH[i2]
                e, f = _SL_OUT[io]
                x1s = x1[:, a:b].reshape(E, m1, 2 * l1 + 1)
                x2s = x2[:, c:d].reshape(E, m2, 2 * l2 + 1)
                seg = jnp.einsum('uvw,ijk,eui,evj->ewk', weights[k], _W3J[k], x1s, x2s, optimize='optimal') * _NORM[k]
                out = out.at[:, e:f].add(seg.reshape(E, mo * (2 * lo + 1)))
            return out
        i, j = (edge_index[0], edge_index[1])
        summand = _tensor_product(x[i], edge_attr, [w0, w1, w2, w3, w4])
        out = jax.ops.segment_sum(summand, j, num_segments=x.shape[0])
        return out / float(np.sqrt(NUM_NEIGHBORS))

    def _L2_gnn_ref(x, edge_index, Wq, bq, Wk, bk, Wv, bv, Wo, bo, Wpos, bpos, Wdeg, bdeg, ln1_g, ln1_b, ln2_g, ln2_b, W1, b1, W2, b2):
        import jax, jax.numpy as jnp
        import numpy as np
        N, E, D, H, L, FF = (50000, 500000, 128, 8, 2, 512)
        HD = D // H

        def _layernorm(x, g, b):
            mu = jnp.mean(x, axis=-1, keepdims=True)
            var = jnp.mean(jnp.square(x - mu), axis=-1, keepdims=True)
            return (x - mu) * jax.lax.rsqrt(var + 1e-05) * g + b

        def _forward(edge_index, x, Wq, bq, Wk, bk, Wv, bv, Wo, bo, Wpos, bpos, Wdeg, bdeg, ln1_g, ln1_b, ln2_g, ln2_b, W1, b1, W2, b2):
            n = x.shape[0]
            loops = jnp.arange(n, dtype=edge_index.dtype)
            src = jnp.concatenate([edge_index[0], loops])
            dst = jnp.concatenate([edge_index[1], loops])
            scale = np.float32(np.sqrt(HD))
            for l in range(L):
                xn = _layernorm(x, ln1_g[l], ln1_b[l])
                deg = jax.ops.segment_sum(jnp.ones_like(src, dtype=x.dtype), src, num_segments=n)
                deg = (deg - deg.mean()) / (jnp.std(deg, ddof=1) + 1e-06)
                pos = xn @ Wpos[l] + bpos[l] + deg[:, None] * Wdeg[l][0] + bdeg[l]
                xp = xn + pos
                q = (xp @ Wq[l] + bq[l]).reshape(n, H, HD)
                k = (xp @ Wk[l] + bk[l]).reshape(n, H, HD)
                v = (xp @ Wv[l] + bv[l]).reshape(n, H, HD)
                att = jnp.einsum('ehd,ehd->eh', q[dst], k[src]) / scale
                att = jnp.nan_to_num(jnp.clip(att, -50.0, 50.0), nan=0.0, posinf=50.0, neginf=-50.0)
                m = jax.ops.segment_max(att, dst, num_segments=n)
                ex = jnp.exp(att - m[dst])
                s = jax.ops.segment_sum(ex, dst, num_segments=n)
                alpha = ex / (s[dst] + 1e-16)
                msg = (v[src] * alpha[:, :, None]).reshape(-1, D)
                aggr = jax.ops.segment_sum(msg, dst, num_segments=n)
                x = x + (aggr @ Wo[l] + bo[l])
                h = jax.nn.gelu(_layernorm(x, ln2_g[l], ln2_b[l]) @ W1[l] + b1[l], approximate=False)
                x = x + (h @ W2[l] + b2[l])
            return x
        return _forward(edge_index, x, Wq, bq, Wk, bk, Wv, bv, Wo, bo, Wpos, bpos, Wdeg, bdeg, ln1_g, ln1_b, ln2_g, ln2_b, W1, b1, W2, b2)

    def _L3_gnn_ref(node_embedding, edge_index, Ws_rel, bs_rel, Ws_root):
        import jax, jax.numpy as jnp
        import numpy as np
        N = 50000
        E = 9375
        D = 128
        L = 4
        n = node_embedding.shape[0]
        src, dst = (edge_index[0], edge_index[1])
        ones = jnp.ones((edge_index.shape[1],), node_embedding.dtype)
        deg = jax.ops.segment_sum(ones, dst, num_segments=n)
        inv_deg = (1.0 / jnp.maximum(deg, 1.0))[:, None]
        X = node_embedding
        for l in range(Ws_rel.shape[0]):
            agg = jax.ops.segment_sum(X[src], dst, num_segments=n) * inv_deg
            out = agg @ Ws_rel[l] + bs_rel[l] + X @ Ws_root[l]
            X = jax.nn.elu(out)
        return X
    edge_index = jnp.stack([src, dst])
    x = _layernorm(x + _L0_gnn_ref(x, edge_index, L0_gnn_W1_l, L0_gnn_b1, L0_gnn_W1_r, L0_gnn_W2_l, L0_gnn_b2, L0_gnn_W2_r), axis=-1)
    x = _layernorm(x + _L1_gnn_ref(x, edge_index, edge_attr_9, L1_gnn_w0, L1_gnn_w1, L1_gnn_w2, L1_gnn_w3, L1_gnn_w4), axis=-1)
    x = _layernorm(x + _L2_gnn_ref(x, edge_index, L2_gnn_Wq, L2_gnn_bq, L2_gnn_Wk, L2_gnn_bk, L2_gnn_Wv, L2_gnn_bv, L2_gnn_Wo, L2_gnn_bo, L2_gnn_Wpos, L2_gnn_bpos, L2_gnn_Wdeg, L2_gnn_bdeg, L2_gnn_ln1_g, L2_gnn_ln1_b, L2_gnn_ln2_g, L2_gnn_ln2_b, L2_gnn_W1, L2_gnn_b1, L2_gnn_W2, L2_gnn_b2), axis=-1)
    x = _layernorm(x + _L3_gnn_ref(x, edge_index, L3_gnn_Ws_rel, L3_gnn_bs_rel, L3_gnn_Ws_root), axis=-1)
    return x

_drawn_inputs = setup_inputs


def setup_inputs(seed=0):
    import zlib

    import numpy as np

    out = dict(_drawn_inputs(seed))
    spreads = {'L0_gnn_b1': (0.0, 0.1),
     'L0_gnn_b2': (0.0, 0.1),
     'L2_gnn_bq': (0.0, 0.427),
     'L2_gnn_bk': (0.0, 0.8),
     'L2_gnn_bv': (0.0, 0.1),
     'L2_gnn_bo': (0.0, 0.1),
     'L2_gnn_bpos': (0.0, 0.1),
     'L2_gnn_bdeg': (0.0, 0.1),
     'L2_gnn_ln1_g': (1.0, 0.2),
     'L2_gnn_ln1_b': (0.0, 0.1),
     'L2_gnn_ln2_g': (1.0, 0.2),
     'L2_gnn_ln2_b': (0.0, 0.1),
     'L2_gnn_b1': (0.0, 0.1),
     'L2_gnn_b2': (0.0, 0.1),
     'L3_gnn_bs_rel': (0.0, 0.1)}
    factors = {}
    for name, (base, spread) in spreads.items():
        noise = np.random.default_rng([zlib.crc32(name.encode()), seed]).standard_normal(out[name].shape)
        drawn = base * np.exp(spread * noise) if base else spread * noise
        out[name] = jnp.asarray(drawn.astype(out[name].dtype))
    for name, factor in factors.items():
        out[name] = (out[name] * factor).astype(out[name].dtype)
    return out
```

```python
import concourse.bass as bass
from concourse import mybir
from contextlib import ExitStack, contextmanager
from math import factorial, sqrt
import numpy as np

F32 = mybir.dt.float32
BF16 = mybir.dt.bfloat16
I32 = mybir.dt.int32
ALU = mybir.AluOpType
ACT = mybir.ActivationFunctionType
AX = mybir.AxisListType

D = 128
TPC = 4
CH = TPC * D
H, HD = 8, 16
FF = 512
FJ = FF // D
MUL = 32
EPS = 1e-5
STD_EPS = 1e-6
ATT_CLIP = 50.0
ea_n = 9


def wigner_3j(l1, l2, l3):
    def f(n):
        return factorial(round(n))

    def cg(j1, m1, j2, m2, j3, m3):
        if m3 != m1 + m2:
            return 0.0
        vmin = int(max(-j1 + j2 + m3, -j1 + m1, 0))
        vmax = int(min(j2 + j3 + m1, j3 - j1 + j2, j3 + m3))
        c = ((2.0 * j3 + 1.0) * f(j3 + j1 - j2) * f(j3 - j1 + j2) * f(j1 + j2 - j3) * f(j3 + m3) * f(j3 - m3)
             / (f(j1 + j2 + j3 + 1) * f(j1 - m1) * f(j1 + m1) * f(j2 - m2) * f(j2 + m2))) ** 0.5
        s = 0
        for v in range(vmin, vmax + 1):
            s += (-1) ** (v + j2 + m2) * f(j2 + j3 + m1 - v) * f(j1 - m1 + v) / (
                f(v) * f(j3 - j1 + j2 - v) * f(j3 + m3 - v) * f(v + j1 - j2 - m3))
        return float(c * s)

    def basis(l):
        q = np.zeros((2 * l + 1, 2 * l + 1), dtype=np.complex128)
        for m in range(-l, 0):
            q[l + m, l + abs(m)] = 1 / np.sqrt(2)
            q[l + m, l - abs(m)] = -1j / np.sqrt(2)
        q[l, l] = 1
        for m in range(1, l + 1):
            q[l + m, l + abs(m)] = (-1) ** m / np.sqrt(2)
            q[l + m, l - abs(m)] = 1j * (-1) ** m / np.sqrt(2)
        return (-1j) ** l * q

    c = np.zeros((2 * l1 + 1, 2 * l2 + 1, 2 * l3 + 1))
    for m1 in range(-l1, l1 + 1):
        for m2 in range(-l2, l2 + 1):
            if abs(m1 + m2) <= l3:
                c[l1 + m1, l2 + m2, l3 + m1 + m2] = cg(l1, m1, l2, m2, l3, m1 + m2)
    out = np.real(np.einsum("ij,kl,mn,ikn->jlm", basis(l1), basis(l2), np.conj(basis(l3).T),
                            c.astype(np.complex128)))
    return out / np.linalg.norm(out)


@contextmanager
def pairs(eng, steps):
    with eng.Fori(0, steps // 2) as j:
        yield j * 2


def gnn_stack(nc, t):
    N = t["x"].shape[0]
    E = t["src"].shape[0]
    CN = -(-N // CH)
    NP = CN * CH
    ET = -(-E // D)
    EP = ET * D
    TAIL_P = (N - (CN - 1) * CH) // TPC
    TAIL_E = E - (ET - 1) * D
    HC = CN * TPC
    assert N % TPC == 0 and N < NP and E < EP and ET % 2 == 0 and CN % 2 == 0 and HC <= 512

    ctx = ExitStack()
    with ctx:
        def sb(name, shape, dt=F32):
            return ctx.enter_context(nc.sbuf_tensor("sb_" + name, shape, dt))

        def sem(name):
            return ctx.enter_context(nc.semaphore(name))

        def dram(name, rows, cols, dt=F32):
            return nc.dram_tensor("scratch_" + name, [rows, cols], dt).ap()

        XD0 = dram("x_of_targets", EP, D)
        T1, T2, T3, T4, T5, T6, T7, T8 = [dram(f"table{n}", NP + EP, D) for n in range(1, 9)]
        INFO = dram("node_info", NP, 4)

        bank = [ctx.enter_context(nc.psum_tensor(f"bank{n}", [D, 512], F32)) for n in range(8)]
        banks = [b[:, :] for b in bank]

        ident = sb("ident", [D, D])
        ones = sb("ones", [D, D])
        dst_all = sb("dst_all", [D, EP + 1])
        dst_col = sb("dst_col", [D, ET])
        x_src = sb("x_src", [D, ET], I32)
        x_dst = sb("x_dst", [D, ET], I32)
        g_dst0 = sb("g_dst0", [D, ET], I32)
        g_src = sb("g_src", [D, ET], I32)
        g_dst = sb("g_dst", [D, ET], I32)
        put_row = sb("put_row", [D, ET], I32)
        inv_in = sb("inv_in", [D, ET])
        deg_src = sb("deg_src", [D, ET])
        deg_dst = sb("deg_dst", [D, ET])
        deg_node = sb("deg_node", [D, HC])
        ea = sb("ea", [D, ET, ea_n])
        coef = sb("coef", [D, ET, 3, 3])
        minus_half = sb("minus_half", [D, 8])
        cnt = sb("cnt", [D, ET])
        seg = sb("seg", [D, 2, D])
        cont = sb("cont", [1, 2, D])
        idx2 = sb("idx2", [D, 2, 2], I32)
        carry = sb("carry", [1, 2, 3 * D])
        W = {}
        for n in ("L0_gnn_W1_l", "L0_gnn_W1_r", "L0_gnn_W2_l", "L0_gnn_W2_r"):
            W[n] = sb("w_" + n, [D, D])
        w_rel = sb("w_rel", [D, 4, D])
        w_root = sb("w_root", [D, 4, D])
        b1_col, b2_col = sb("b1_col", [D, 1]), sb("b2_col", [D, 1])
        b1_row, b2_row = sb("b1_row", [D, D]), sb("b2_row", [D, D])
        rel_col, rel_row = sb("rel_col", [D, 4]), sb("rel_row", [D, 4, D])
        tp0, tp1 = sb("tp0", [2 * MUL, MUL]), sb("tp1", [3 * MUL, MUL])
        w_qkv = sb("w_qkv", [D, 2, 3 * D])
        c_qkv = sb("c_qkv", [D, 2, 3 * D])
        u_qkv = sb("u_qkv", [D, 2, 3 * D])
        w_o = sb("w_o", [D, 2, D])
        bo_row = sb("bo_row", [D, 2, D])
        w_vo = sb("w_vo", [D, 2, D])
        c_vo = sb("c_vo", [D, 2, D])
        u_vo = sb("u_vo", [D, 2, D])
        w_up = sb("w_up", [D, 2, FF])
        b_up = sb("b_up", [D, 2, FJ])
        w_down = sb("w_down", [D, 2, FJ, D])
        b_down = sb("b_down", [D, 2, D])

        s_tmp = sem("setup_done")
        s_ld = sem("setup_loaded")
        s_ldc = sem("setup_cast_loaded")
        s_pre = sem("setup_pool")

        class Chain:
            def __init__(self, name):
                self.sem, self.n = sem(name), 0

            def __call__(self, eng, ins):
                self.n += 1
                ins.then_inc(self.sem, 1)
                eng.wait_ge(self.sem, self.n)

        signals, started = [], []

        class Signal:
            def __init__(self, name):
                self.raw, self.n, self.touched = sem(name), 0, False
                signals.append(self)

            @property
            def sem(self):
                self.touched = True
                return self.raw

            def now(self, i, u):
                return i + (self.n + u + 3)

            def last(self, i, u):
                return i + (self.n + u + 2)

            def old(self, i, u):
                return i + (self.n + u + 1)

        class Transfer:
            def __init__(self, name, start=1):
                self.start = start
                self.raw, self.n, self.touched = [sem(name + "_0"), sem(name + "_1")], 0, False
                signals.append(self)

            @property
            def sem(self):
                self.touched = True
                return self.raw

            def now(self, i):
                return i * 8 + (self.n * 8 + self.start + 16)

            def old(self, i):
                return i * 8 + (self.n * 8 + self.start)

            def end(self, steps):
                return 8 * (self.n + steps) + self.start

        def start_signals():
            with nc.Block() as block:
                @block.vector
                def _(dve):
                    for s in signals[len(started):]:
                        if isinstance(s, Signal):
                            dve.sem_inc(s.raw, 2)
                        elif s.start == 1:
                            dve.sem_inc(s.raw[0], 1)
                            dve.sem_inc(s.raw[1], 1)
                        started.append(s)

        def end_phase(steps):
            for s in signals:
                if s.touched:
                    s.n, s.touched = s.n + steps, False

        setup = ExitStack()

        def tmp(name, shape, dt=F32):
            return setup.enter_context(nc.sbuf_tensor("sb_" + name, shape, dt))

        stage = tmp("stage", [D, 6, D])
        lay = tmp("lay", [ET, 3, D])
        wpos = tmp("wpos", [D, 2, D])
        wqkv_raw = tmp("wqkv_raw", [D, 2, 3 * D])
        cols = tmp("cols", [D, 2, 8])
        bqkv = tmp("bqkv", [D, 2, 3 * D])
        aposT = tmp("aposT", [D, D])
        m1 = tmp("m1", [D, 3 * D])
        spread = tmp("spread", [D, 3, D])
        b_up_raw = tmp("b_up_raw", [D, 2, FJ])
        n_ld = [0]
        s_ea, s_pad = sem("ea_cleared"), sem("pads_set")

        def row_bc(v):
            return v.rearrange("(a n) -> a n", a=1).broadcast_to([D, v.shape[0]])

        def col_of(v):
            return v.rearrange("(n a) -> n a", a=1)

        with nc.Block() as block:
            @block.sync
            def _(sp):
                def ld(out, in_):
                    sp.dma_start(out, in_).then_inc(s_ld, 16)
                    n_ld[0] += 16
                for n in ("L0_gnn_W1_l", "L0_gnn_W1_r", "L0_gnn_W2_l", "L0_gnn_W2_r"):
                    ld(W[n][:, :], t[n])
                ld(b1_col[:, :], col_of(t["L0_gnn_b1"]))
                ld(b2_col[:, :], col_of(t["L0_gnn_b2"]))
                ld(b1_row[:, :], row_bc(t["L0_gnn_b1"]))
                ld(b2_row[:, :], row_bc(t["L0_gnn_b2"]))
                ld(w_rel[:, :, :], t["L3_gnn_Ws_rel"].rearrange("l a b -> a l b"))
                ld(w_root[:, :, :], t["L3_gnn_Ws_root"].rearrange("l a b -> a l b"))
                for l in range(4):
                    ld(rel_col[:, l:l + 1], col_of(t["L3_gnn_bs_rel"][l, :]))
                    ld(rel_row[:, l, :], row_bc(t["L3_gnn_bs_rel"][l, :]))
                for k, (tile, at) in enumerate([(tp0, 0), (tp1, 0), (tp1, MUL), (tp0, MUL), (tp1, 2 * MUL)]):
                    ld(tile[at:at + MUL, :], t[f"L1_gnn_w{k}"].rearrange("u a w -> u (a w)"))
                for l in range(2):
                    ld(wpos[:, l, :], t["L2_gnn_Wpos"][l, :, :])
                    for j, n in enumerate("qkv"):
                        ld(wqkv_raw[:, l, j * D:(j + 1) * D], t[f"L2_gnn_W{n}"][l, :, :])
                        ld(bqkv[:, l, j * D:(j + 1) * D], row_bc(t[f"L2_gnn_b{n}"][l, :]))
                    for j, v in enumerate([t["L2_gnn_ln1_g"][l, :], t["L2_gnn_ln1_b"][l, :], t["L2_gnn_bpos"][l, :],
                                           t["L2_gnn_bdeg"][l, :], t["L2_gnn_Wdeg"][l, 0, :],
                                           t["L2_gnn_ln2_g"][l, :], t["L2_gnn_ln2_b"][l, :]]):
                        ld(cols[:, l, j:j + 1], col_of(v))
                    ld(w_o[:, l, :], t["L2_gnn_Wo"][l, :, :])
                    ld(bo_row[:, l, :], row_bc(t["L2_gnn_bo"][l, :]))
                    ld(w_up[:, l, :], t["L2_gnn_W1"][l, :, :])
                    ld(w_down[:, l, :, :], t["L2_gnn_W2"][l, :, :].rearrange("(j p) n -> p j n", p=D))
                    for j in range(FJ):
                        ld(b_up_raw[:, l, j:j + 1], col_of(t["L2_gnn_b1"][l, j * D:(j + 1) * D]))
                    ld(b_down[:, l, :], row_bc(t["L2_gnn_b2"][l, :]))
                sp.wait_ge(s_ea, 1)
                ld(ea[:, 0:ET - 1, :], t["edge_attr_9"][0:(ET - 1) * D, :].rearrange("(s p) c -> p s c", p=D))
                ld(ea[0:TAIL_E, ET - 1, :], t["edge_attr_9"][(ET - 1) * D:E, :])
                sp.wait_ge(s_ld, n_ld[0])

            @block.gpsimd
            def _(pool):
                ch = Chain("setup_pool_chain")
                pool.memset(ident[:, :], 0.0).then_inc(s_pre, 1)
                pool.wait_ge(s_pre, 1)
                pool.affine_select(out=ident[:, :], in_=ident[:, :], compare_op=ALU.not_equal, fill=1.0,
                                   base=0, pattern=[[-1, D]], channel_multiplier=1).then_inc(s_pre, 1)
                pool.memset(ones[:, :], 1.0).then_inc(s_pre, 1)
                pool.memset(minus_half[:, :], -0.5).then_inc(s_pre, 1)
                pool.wait_ge(s_pad, 1)
                n = 0
                for j, (v, o) in enumerate([(t["src"], 0), (t["dst"], 0), (t["dst"], 1)]):
                    full = (ET - 1) * D
                    pool.dma_start(lay[0:ET - 1, j, :], v[o:o + full].rearrange("(s p) -> s p", p=D)).then_inc(s_ldc, 16)
                    pool.dma_start(lay[ET - 1:ET, j, 0:TAIL_E - o],
                                   v[full + o:E].rearrange("(s p) -> s p", s=1)).then_inc(s_ldc, 16)
                    n += 32
                pool.dma_start(dst_all[:, 1:1 + E], row_bc(t["dst"])).then_inc(s_ldc, 16)
                pool.wait_ge(s_ldc, n + 16)

            @block.vector
            def _(dve):
                dve.memset(ea[:, ET - 1, :], 0.0).then_inc(s_ea, 1)
                dve.memset(lay[:, 0, :], float(NP))
                dve.memset(lay[:, 1, :], float(NP - 1))
                dve.memset(lay[:, 2, :], float(NP - 1))
                dve.memset(dst_all[:, 0:1], -1.0)
                dve.memset(dst_all[:, 1 + E:], float(NP - 1)).then_inc(s_pad, 1)

        s1, s2, s3, s4 = sem("su_pe"), sem("su_dve"), sem("su_act"), sem("su_pool2")
        srcf = tmp("srcf", [D, ET])
        nxtf = tmp("nxtf", [D, ET])
        lo_f, hi_f = tmp("lo_f", [D, ET]), tmp("hi_f", [D, ET])
        wi = tmp("wi", [D, 3, ET], I32)
        wf = tmp("wf", [D, 3, ET])
        iota_lo, iota_hi = tmp("iota_lo", [D, D]), tmp("iota_hi", [D, HC])
        w121 = wigner_3j(1, 2, 1)

        with nc.Block() as block:
            @block.gpsimd
            def _(pool):
                pool.iota(iota_lo[:, :], [[1, D]], base=0, channel_multiplier=0,
                          allow_small_or_imprecise_dtypes=True)
                pool.iota(iota_hi[:, :], [[1, HC]], base=0, channel_multiplier=0,
                          allow_small_or_imprecise_dtypes=True)

            @block.tensor
            def _(pe):
                ch = [0]

                def done(ins):
                    ch[0] += 1
                    ins.then_inc(s1, 1)
                for j in range(3):
                    last = pe.transpose(banks[0][:, j * ET:(j + 1) * ET], lay[:, j, :], ident[0:ET, 0:ET])
                done(last)
                for l in range(2):
                    v = 8 * l
                    pe.wait_ge(s2, v + 1)
                    done(pe.transpose(banks[1][:, 0:D], stage[:, 0, :], ident[:, :]))
                    pe.wait_ge(s2, v + 2)
                    done(pe.matmul(banks[2][:, 0:3 * D], aposT[:, :], wqkv_raw[:, l, :], start=True, stop=True))
                    pe.wait_ge(s2, v + 3)
                    pe.matmul(banks[3][:, 0:3 * D], spread[:, 0, :], m1[:, :], start=True, stop=False)
                    done(pe.matmul(banks[3][:, 0:3 * D], spread[:, 1, :], wqkv_raw[:, l, :], start=False, stop=True))
                    done(pe.matmul(banks[4][:, 0:3 * D], spread[:, 2, :], wqkv_raw[:, l, :], start=True, stop=True))
                    pe.wait_ge(s2, v + 4)
                    for j, src_ in enumerate([w_qkv[:, l, 2 * D:3 * D], c_qkv[:, l, 2 * D:3 * D], u_qkv[:, l, 2 * D:3 * D]]):
                        last = pe.transpose(banks[5][:, j * D:(j + 1) * D], src_, ident[:, :])
                    done(last)
                    pe.wait_ge(s2, v + 5)
                    for j in range(3):
                        last = pe.matmul(banks[6][:, j * D:(j + 1) * D], stage[:, 1 + j, :], w_o[:, l, :], start=True, stop=True)
                    done(last)
                    for j in range(FJ):
                        last = pe.matmul(banks[7][:, j:j + 1], w_up[:, l, j * D:(j + 1) * D], cols[:, l, 6:7], start=True, stop=True)
                    done(last)

            @block.vector
            def _(dve):
                ch = Chain("su_dve_chain")

                def go(ins):
                    ch(dve, ins)
                dve.wait_ge(s1, 1)
                go(dve.tensor_copy(srcf[:, :], banks[0][:, 0:ET]))
                go(dve.tensor_copy(dst_col[:, :], banks[0][:, ET:2 * ET]))
                go(dve.tensor_copy(nxtf[:, :], banks[0][:, 2 * ET:3 * ET]))
                go(dve.tensor_scalar(x_src[:, :], srcf[:, :], float(N - 1), None, ALU.min))
                go(dve.tensor_scalar(x_dst[:, :], dst_col[:, :], float(N - 1), None, ALU.min))
                go(dve.tensor_copy(g_dst0[:, :], dst_col[:, :]))
                go(dve.tensor_tensor(wf[:, 0, :], dst_col[:, :], nxtf[:, :], ALU.is_equal))
                go(dve.tensor_scalar(wf[:, 1, :], wf[:, 0, :], float(2 * NP), None, ALU.mult))
                go(dve.tensor_tensor(put_row[:, :], wf[:, 1, :], dst_col[:, :], ALU.add))
                go(dve.tensor_copy(wi[:, 0, :], srcf[:, :]))
                go(dve.tensor_scalar(wi[:, 1, :], wi[:, 0, :], 2, 127, ALU.logical_shift_right, ALU.bitwise_and))
                go(dve.tensor_copy(lo_f[:, :], wi[:, 1, :]))
                go(dve.tensor_scalar(wi[:, 1, :], wi[:, 0, :], 9, 2, ALU.logical_shift_right, ALU.logical_shift_left))
                go(dve.tensor_copy(wf[:, 0, :], wi[:, 1, :]))
                go(dve.tensor_scalar(wi[:, 2, :], wi[:, 0, :], 3, None, ALU.bitwise_and))
                go(dve.tensor_copy(wf[:, 1, :], wi[:, 2, :]))
                go(dve.tensor_tensor(hi_f[:, :], wf[:, 0, :], wf[:, 1, :], ALU.add))
                for k in range(3):
                    for i in range(3):
                        first = True
                        for j in range(5):
                            c = float(w121[i, j, k])
                            if abs(c) < 1e-12:
                                continue
                            if first:
                                go(dve.tensor_scalar(coef[:, :, k, i], ea[:, :, 4 + j], c, None, ALU.mult))
                            else:
                                go(dve.scalar_tensor_tensor(coef[:, :, k, i], ea[:, :, 4 + j], c, coef[:, :, k, i],
                                                            ALU.mult, ALU.add))
                            first = False
                        if first:
                            go(dve.memset(coef[:, :, k, i], 0.0))
                fan0, fan1, nb = 2 * MUL, 3 * MUL, sqrt(10.0)
                n0, n1 = sqrt(1.0 / fan0) / nb, sqrt(3.0 / fan1) / nb
                r3 = 1.0 / sqrt(3.0)
                go(dve.tensor_scalar(tp0[0:MUL, :], tp0[0:MUL, :], n0, None, ALU.mult))
                go(dve.tensor_scalar(tp0[MUL:2 * MUL, :], tp0[MUL:2 * MUL, :], n0 * r3, None, ALU.mult))
                go(dve.tensor_scalar(tp1[0:MUL, :], tp1[0:MUL, :], n1 * r3, None, ALU.mult))
                go(dve.tensor_scalar(tp1[MUL:2 * MUL, :], tp1[MUL:2 * MUL, :], n1 * r3, None, ALU.mult))
                go(dve.tensor_scalar(tp1[2 * MUL:3 * MUL, :], tp1[2 * MUL:3 * MUL, :], n1, None, ALU.mult))
                for l in range(2):
                    p = 1 + 7 * l
                    go(dve.tensor_tensor(stage[:, 0, :], wpos[:, l, :], ident[:, :], ALU.add))
                    dve.sem_inc(s2, 1)
                    dve.wait_ge(s1, p + 1)
                    go(dve.tensor_copy(aposT[:, :], banks[1][:, 0:D]))
                    dve.sem_inc(s2, 1)
                    dve.wait_ge(s1, p + 2)
                    go(dve.tensor_copy(m1[:, :], banks[2][:, 0:3 * D]))
                    go(dve.tensor_scalar(w_qkv[:, l, :], m1[:, :], cols[:, l, 0:1], None, ALU.mult))
                    go(dve.tensor_scalar(spread[:, 0, :], ones[:, :], cols[:, l, 1:2], None, ALU.mult))
                    go(dve.tensor_scalar(spread[:, 1, :], ones[:, :], cols[:, l, 2:3], cols[:, l, 3:4], ALU.mult, ALU.add))
                    go(dve.tensor_scalar(spread[:, 2, :], ones[:, :], cols[:, l, 4:5], None, ALU.mult))
                    dve.sem_inc(s2, 1)
                    dve.wait_ge(s1, p + 4)
                    go(dve.tensor_tensor(c_qkv[:, l, :], banks[3][:, 0:3 * D], bqkv[:, l, :], ALU.add))
                    go(dve.tensor_copy(u_qkv[:, l, :], banks[4][:, 0:3 * D]))
                    dve.sem_inc(s2, 1)
                    dve.wait_ge(s1, p + 5)
                    go(dve.tensor_copy(stage[:, 1:4, :], banks[5][:, 0:3 * D].rearrange("p (j d) -> p j d", j=3)))
                    dve.sem_inc(s2, 1)
                    dve.wait_ge(s1, p + 6)
                    go(dve.tensor_copy(w_vo[:, l, :], banks[6][:, 0:D]))
                    go(dve.tensor_tensor(c_vo[:, l, :], banks[6][:, D:2 * D], bo_row[:, l, :], ALU.add))
                    go(dve.tensor_copy(u_vo[:, l, :], banks[6][:, 2 * D:3 * D]))
                    dve.wait_ge(s1, p + 7)
                    go(dve.tensor_tensor(b_up[:, l, :], banks[7][:, 0:FJ], b_up_raw[:, l, :], ALU.add))
                    go(dve.tensor_scalar(w_up[:, l, :], w_up[:, l, :], cols[:, l, 5:6], None, ALU.mult))
                    dve.sem_inc(s2, 3)

        deg_seg, deg_pe = Signal("deg_seg"), Signal("deg_pe")
        deg_carry, deg_cnt = Signal("deg_carry"), Signal("deg_cnt")
        idx_set = [Signal("src_rows_set"), Signal("dst_rows_set")]

        def edge_signal(name):
            return Signal("edge_" + name)
        seg_set, agg_done, carry_set, at_set, mm_done = map(
            edge_signal, ("seg_set", "agg_done", "carry_set", "at_set", "mm_done"))
        z_set, e_set, c_set, y_set = map(edge_signal, ("z_set", "e_set", "c_set", "y_set"))
        st_set, v_set, rs_set, ln_set = map(edge_signal, ("st_set", "v_set", "rs_set", "ln_set"))
        row_set = edge_signal("row_set")
        got_src, got_dst = Transfer("edge_got_src", 0), Transfer("edge_got_dst", 0)
        put_rows = Transfer("edge_put_rows", 16)
        got_own, got_res, put_out, put_x = [Transfer("edge_" + x) for x in ("got_own", "got_res", "put_out", "put_x")]

        def p_wait(pool, s, v):
            pool.wait_ge(s, v)
            pool.nop(nofuse=True)

        def gather(pool, i, u, out, table, rows, j, free):
            p_wait(pool, *free)
            pool.tensor_copy(idx2[:, u, j:j + 1], rows[:, bass.ds(i + u, 1)]).then_inc(idx_set[j].sem, 1)
            p_wait(pool, idx_set[j].sem, idx_set[j].now(i, u))
            return pool.indirect_dma_start(
                out, None, table, bass.IndirectOffsetOnAxis(ap=idx2[:, u, j:j + 1], axis=0))

        def same_target(dve, i, u, scale):
            at = (i + u) * D
            if scale:
                dve.tensor_scalar(seg[:, u, :], dst_all[:, bass.ds(at + 1, D)], dst_col[:, bass.ds(i + u, 1)],
                                  inv_in[:, bass.ds(i + u, 1)], ALU.is_equal, ALU.mult)
            else:
                dve.tensor_scalar(seg[:, u, :], dst_all[:, bass.ds(at + 1, D)], dst_col[:, bass.ds(i + u, 1)],
                                  None, ALU.is_equal)
            return dve.tensor_scalar(cont[0:1, u, :], dst_all[0:1, bass.ds(at + 1, D)],
                                     dst_all[0:1, bass.ds(at, 1)], None, ALU.is_equal)

        one_lo = tmp("one_lo", [D, 2, D], BF16)
        one_hi = tmp("one_hi", [D, 2, HC], BF16)
        zero_b = tmp("zero_b", [D, max(HC, D)], BF16)
        carry_n = tmp("carry_n", [1, 2, 1])

        start_signals()
        with nc.Block() as block:
            @block.vector
            def _(dve):
                dve.memset(zero_b[:, :], 0.0)
                dve.memset(carry[:, :, :], 0.0)
                dve.memset(carry_n[:, :, :], 0.0)
                dve.drain()

        with nc.Block() as block:
            @block.vector
            def _(dve):
                with pairs(dve, ET) as i:
                    for u in range(2):
                        dve.wait_ge(deg_pe.sem, deg_pe.old(i, u))
                        same_target(dve, i, u, False)
                        dve.tensor_scalar(one_lo[:, u, :], iota_lo[:, :], lo_f[:, bass.ds(i + u, 1)], None, ALU.is_equal)
                        dve.tensor_scalar(one_hi[:, u, :], iota_hi[:, :], hi_f[:, bass.ds(i + u, 1)], None,
                                          ALU.is_equal).then_inc(deg_seg.sem, 1)

            @block.tensor
            def _(pe):
                hist = banks[4][:, 0:HC]
                pe.matmul(hist, zero_b[:, 0:D], zero_b[:, 0:HC], start=True, stop=False, skip_group_check=True)
                with pairs(pe, ET) as i:
                    for u in range(2):
                        pe.wait_ge(deg_seg.sem, deg_seg.now(i, u))
                        pe.wait_ge(deg_cnt.sem, deg_cnt.old(i, u))
                        pe.wait_ge(deg_carry.sem, deg_carry.last(i, u))
                        pe.matmul(hist, one_lo[:, u, :], one_hi[:, u, :], start=False, stop=False, skip_group_check=True)
                        pe.matmul(banks[u][:, 0:1], seg[:, u, :], ones[:, 0:1], start=True, stop=False)
                        pe.matmul(banks[u][:, 0:1], cont[0:1, u, :], carry_n[0:1, 1 - u, :], start=False, stop=True)
                        pe.matmul(banks[2 + u][0:1, 0:1], seg[:, u, D - 1:D], ones[:, 0:1], start=True, stop=False)
                        pe.matmul(banks[2 + u][0:1, 0:1], cont[0:1, u, D - 1:D], carry_n[0:1, 1 - u, :],
                                  start=False, stop=True).then_inc(deg_pe.sem, 1)
                pe.matmul(hist, zero_b[:, 0:D], zero_b[:, 0:HC], start=False, stop=True, skip_group_check=True)

            @block.scalar
            def _(act):
                with pairs(act, ET) as i:
                    for u in range(2):
                        act.wait_ge(deg_pe.sem, deg_pe.now(i, u))
                        act.copy(carry_n[0:1, u, :], banks[2 + u][0:1, 0:1]).then_inc(deg_carry.sem, 1)
                        act.copy(cnt[:, bass.ds(i + u, 1)], banks[u][:, 0:1]).then_inc(deg_cnt.sem, 1)
        end_phase(ET)

        sq, colsum = tmp("sq", [D, HC]), tmp("colsum", [D, 4])
        info = tmp("info", [D, CN, TPC, 4])
        info_d, info_s = tmp("info_d", [D, 2, 4]), tmp("info_s", [D, 2, 4])
        slot_row = tmp("slot_row", [D, ET])
        t1, t2, t3, t4 = sem("tab_sq"), sem("tab_total"), sem("tab_var"), sem("tab_info")
        t5, t6, t7 = sem("tab_std"), sem("tab_iota"), sem("tab_stored")
        mean_out = (E + N) / N
        primer = tmp("primer", [1, 2])
        half = tmp("half", [D, 1])
        with nc.Block() as block:
            @block.gpsimd
            def _(pool):
                for u in range(2):
                    pool.dma_start(primer[0:1, u:u + 1], t["x"][0:1, 0:1]).then_inc(put_rows.raw[u], 16)
                    pool.wait_ge(put_rows.raw[u], 16)
                pool.memset(half[:, :], 0.5)
                pool.iota(info[:, :, :, 0], [[CH, CN], [1, TPC]], base=0, channel_multiplier=TPC,
                          allow_small_or_imprecise_dtypes=True)
                pool.iota(slot_row[:, :], [[D, ET]], base=NP, channel_multiplier=1,
                          allow_small_or_imprecise_dtypes=True)
                pool.memset(info[:, :, :, 1], 1.0)
                pool.memset(info[:, :, :, 3], 0.0).then_inc(t6, 1)
                pool.wait_ge(t6, 1)
                pool.wait_ge(t3, 1)
                pool.tensor_tensor(colsum[:, 2:3], colsum[:, 1:2], half[:, :], ALU.pow).then_inc(t5, 1)

            @block.tensor
            def _(pe):
                pe.wait_ge(t1, 1)
                pe.matmul(banks[0][:, 0:1], ones[:, :], colsum[:, 0:1], start=True, stop=True).then_inc(t2, 1)

            @block.vector
            def _(dve):
                ch = Chain("tab_chain")

                def go(ins):
                    ch(dve, ins)
                go(dve.tensor_scalar(deg_node[:, :], banks[4][:, 0:HC], 1.0 - mean_out, None, ALU.add))
                go(dve.tensor_tensor(sq[:, :], deg_node[:, :], deg_node[:, :], ALU.mult))
                dve.tensor_reduce(colsum[:, 0:1], sq[:, :], AX.X, ALU.add).then_inc(t1, 1)
                dve.wait_ge(t2, 1)
                dve.tensor_scalar(colsum[:, 1:2], banks[0][:, 0:1], -(NP - N) * (1.0 - mean_out) ** 2, 1.0 / (N - 1),
                                  ALU.add, ALU.mult).then_inc(t3, 1)
                dve.wait_ge(t5, 1)
                go(dve.tensor_scalar(colsum[:, 0:1], colsum[:, 2:3], STD_EPS, None, ALU.add))
                go(dve.reciprocal(colsum[:, 3:4], colsum[:, 0:1]))
                go(dve.tensor_scalar(deg_node[:, :], deg_node[:, :], colsum[:, 3:4], None, ALU.mult))
                dve.wait_ge(t6, 1)
                dve.tensor_copy(info[:, :, :, 2], deg_node[:, :].rearrange("p (c t) -> p c t", t=TPC)).then_inc(t4, 1)

            @block.sync
            def _(sp):
                sp.wait_ge(t4, 1)
                sp.dma_start(INFO.rearrange("(c p t) f -> p c (t f)", p=D, t=TPC),
                             info[:, :, :, :].rearrange("p c t f -> p c (t f)")).then_inc(t7, 16)
                sp.wait_ge(t7, 16)

        new_info = tmp("new_info", [D, 2, 4])
        put2 = tmp("put2", [D, 2], I32)
        with nc.Block() as block:
            @block.gpsimd
            def _(pool):
                with pairs(pool, ET) as i:
                    for u in range(2):
                        gather(pool, i, u, info_d[:, u, :], INFO, g_dst0, 1,
                               (row_set.sem, row_set.old(i, u))).then_inc(got_dst.sem[u], 16)

            @block.vector
            def _(dve):
                with pairs(dve, ET) as i:
                    for u in range(2):
                        dve.wait_ge(got_dst.sem[u], got_dst.now(i))
                        dve.tensor_copy(deg_dst[:, bass.ds(i + u, 1)], info_d[:, u, 2:3]).then_inc(row_set.sem, 1)
        end_phase(ET)
        with nc.Block() as block:
            @block.vector
            def _(dve):
                with pairs(dve, ET) as i:
                    for u in range(2):
                        dve.wait_ge(put_rows.sem[u], put_rows.old(i))
                        dve.tensor_copy(new_info[:, u, 0:1], slot_row[:, bass.ds(i + u, 1)])
                        dve.tensor_copy(new_info[:, u, 1:2], cnt[:, bass.ds(i + u, 1)])
                        dve.tensor_copy(new_info[:, u, 2:3], deg_dst[:, bass.ds(i + u, 1)])
                        dve.tensor_copy(new_info[:, u, 3:4], cnt[:, bass.ds(i + u, 1)])
                        dve.tensor_copy(put2[:, u:u + 1], put_row[:, bass.ds(i + u, 1)]).then_inc(row_set.sem, 1)

            @block.gpsimd
            def _(pool):
                with pairs(pool, ET) as i:
                    for u in range(2):
                        p_wait(pool, row_set.sem, row_set.now(i, u))
                        pool.indirect_dma_start(INFO, bass.IndirectOffsetOnAxis(ap=put2[:, u:u + 1], axis=0),
                                                new_info[:, u, :], None, bounds_check=NP - 1,
                                                oob_is_err=False).then_inc(put_rows.sem[u], 16)
                for u in range(2):
                    pool.wait_ge(put_rows.sem[u], put_rows.end(ET))
        end_phase(ET)
        with nc.Block() as block:
            @block.gpsimd
            def _(pool):
                with pairs(pool, ET) as i:
                    for u in range(2):
                        free = (row_set.sem, row_set.old(i, u))
                        gather(pool, i, u, info_s[:, u, :], INFO, x_src, 0, free).then_inc(got_src.sem[u], 16)
                        gather(pool, i, u, info_d[:, u, :], INFO, g_dst0, 1, free).then_inc(got_dst.sem[u], 16)

            @block.vector
            def _(dve):
                with pairs(dve, ET) as i:
                    for u in range(2):
                        dve.wait_ge(got_src.sem[u], got_src.now(i))
                        dve.wait_ge(got_dst.sem[u], got_dst.now(i))
                        dve.tensor_copy(g_src[:, bass.ds(i + u, 1)], info_s[:, u, 0:1])
                        dve.tensor_copy(deg_src[:, bass.ds(i + u, 1)], info_s[:, u, 2:3])
                        dve.tensor_copy(g_dst[:, bass.ds(i + u, 1)], info_d[:, u, 0:1])
                        dve.tensor_copy(cnt[:, bass.ds(i + u, 1)], info_d[:, u, 1:2]).then_inc(row_set.sem, 1)
                dve.wait_ge(row_set.sem, row_set.n + ET + 2)
                dve.reciprocal(inv_in[:, :], cnt[:, :])
        end_phase(ET)

        setup.close()

        nodes = ExitStack()

        def nsb(name, shape, dt=F32):
            return nodes.enter_context(nc.sbuf_tensor("sb_" + name, shape, dt))

        def node_signal(name):
            return Signal("node_" + name)
        n_pe = [node_signal(f"pe_{x}") for x in range(9)]
        n_act = [node_signal(f"act_{x}") for x in range(9)]
        n_dve = [node_signal(f"dve_{x}") for x in range(12)]
        n_pool = [node_signal(f"pool_{x}") for x in range(8)]
        n_in, n_in2 = Transfer("node_in"), Transfer("node_in2")
        n_out = [Transfer(f"node_out{x}") for x in range(4)]
        nb = [nsb(f"node_buf{x}", [D, 2, TPC, D]) for x in range(9)]
        hT = nsb("hT", [D, 2, FJ, CH])
        nst = [nsb(f"node_stats{x}", [D, 2, TPC, 3]) for x in range(3)]
        nv = [nsb(f"node_var{x}", [D, 2, TPC]) for x in range(3)]
        nrs = [nsb(f"node_rstd{x}", [D, 2, TPC]) for x in range(3)]

        start_signals()

        def rows_of(table, c, tail=False):
            if tail:
                return table[(CN - 1) * CH:(CN - 1) * CH + TAIL_P * TPC, :].rearrange("(p t) d -> p t d", t=TPC)
            return table[bass.ds(c * CH, CH), :].rearrange("(p t) d -> p t d", t=TPC)

        def node_sync(sp, loads, stores, ragged_in, ragged_out):
            def load(c, u, tail):
                for table, buf, tr in loads:
                    if tail and ragged_in:
                        sp.dma_start(buf[0:TAIL_P, u], rows_of(table, c, True)).then_inc(tr.sem[u], 16)
                    else:
                        sp.dma_start(buf[:, u], rows_of(table, c)).then_inc(tr.sem[u], 16)

            def store(i, u, c, tail):
                for table, buf, tr, sig in stores:
                    sp.wait_ge(sig.sem, sig.now(i, u))
                    if tail and table is ragged_out:
                        sp.dma_start(rows_of(table, c, True), buf[0:TAIL_P, u]).then_inc(tr.sem[u], 16)
                    else:
                        sp.dma_start(rows_of(table, c), buf[:, u]).then_inc(tr.sem[u], 16)
            load(0, 0, False)
            load(1, 1, False)
            if CN > 4:
                with pairs(sp, CN - 4) as i:
                    for u in range(2):
                        store(i, u, i + u, False)
                        load(i + (u + 2), u, False)
            for c in range(CN - 4, CN):
                store(c - c % 2, c % 2, c, c == CN - 1)
                if c + 2 < CN:
                    load(c + 2, c % 2, c + 2 == CN - 1)
            for _, _, tr, _ in stores:
                for u in range(2):
                    sp.wait_ge(tr.sem[u], tr.end(CN))

        def tiles_T(pe, out, src_, u):
            for k in range(TPC):
                last = pe.transpose(out[:, k * D:(k + 1) * D], src_(k), ident[:, :])
            return last

        def stats(dve, st, x, u):
            for q in range(TPC // 2):
                last = dve.bn_stats(st[:, u, 2 * q:2 * q + 2, :].rearrange("p e f -> p (e f)"),
                                    x[:, u, 2 * q:2 * q + 2, :].rearrange("p t d -> p d t"))
            return last

        def rstd(pool, i, u, st, v, r, ready, v_done, r_done):
            p_wait(pool, ready.sem, ready.now(i, u))
            pool.tensor_scalar(v[:, u, :], st[:, u, :, 2], 1.0 / D, EPS, ALU.mult, ALU.add).then_inc(v_done.sem, 1)
            p_wait(pool, v_done.sem, v_done.now(i, u))
            pool.tensor_tensor(r[:, u, :], v[:, u, :], minus_half[:, 0:TPC], ALU.pow).then_inc(r_done.sem, 1)

        def normalise(dve, out, x, st, r, u):
            for k in range(TPC):
                last = dve.tensor_scalar(out[:, u, k, :], x[:, u, k, :], st[:, u, k, 1:2], r[:, u, k:k + 1],
                                         ALU.subtract, ALU.mult)
            return last

        def flat(buf, u):
            return buf[:, u].rearrange("p t d -> p (t d)")

        with nc.Block() as block:
            @block.vector
            def _(dve):
                dve.memset(nb[0][:, :, :, :], 0.0)
                dve.memset(nb[8][:, :, :, :], 0.0)

        xin, xT, h1T, h1n, h2T, y, x1n, x2n = nb[0:8]
        with nc.Block() as block:
            @block.sync
            def _(sp):
                node_sync(sp, [(t["x"], xin, n_in)],
                          [(T1, h1n, n_out[0], n_act[3]), (T2, x1n, n_out[1], n_dve[2]), (T3, x2n, n_out[2], n_pool[4])],
                          True, None)

            @block.tensor
            def _(pe):
                with pairs(pe, CN) as i:
                    for u in range(2):
                        pe.wait_ge(n_in.sem[u], n_in.now(i))
                        pe.wait_ge(n_dve[0].sem, n_dve[0].old(i, u))
                        tiles_T(pe, banks[u], lambda k: xin[:, u, k, :], u).then_inc(n_pe[0].sem, 1)
                    for u in range(2):
                        pe.wait_ge(n_act[0].sem, n_act[0].now(i, u))
                        pe.wait_ge(n_act[1].sem, n_act[1].old(i, u))
                        pe.matmul(banks[2 + u], W["L0_gnn_W1_r"][:, :], flat(xT, u), start=True, stop=True).then_inc(n_pe[1].sem, 1)
                    for u in range(2):
                        pe.wait_ge(n_act[1].sem, n_act[1].now(i, u))
                        pe.wait_ge(n_act[2].sem, n_act[2].old(i, u))
                        pe.matmul(banks[6 + u], W["L0_gnn_W2_r"][:, :], flat(h1T, u), start=True, stop=True).then_inc(n_pe[2].sem, 1)
                        pe.wait_ge(n_act[3].sem, n_act[3].old(i, u))
                        tiles_T(pe, banks[4 + u], lambda k: h1T[:, u, k, :], u).then_inc(n_pe[3].sem, 1)
                    for u in range(2):
                        pe.wait_ge(n_act[2].sem, n_act[2].now(i, u))
                        tiles_T(pe, banks[u], lambda k: h2T[:, u, k, :], u).then_inc(n_pe[4].sem, 1)

            @block.scalar
            def _(act):
                with pairs(act, CN) as i:
                    for u in range(2):
                        act.wait_ge(n_pe[0].sem, n_pe[0].now(i, u))
                        act.wait_ge(n_pe[1].sem, n_pe[1].old(i, u))
                        act.copy(flat(xT, u), banks[u]).then_inc(n_act[0].sem, 1)
                    for u in range(2):
                        act.wait_ge(n_pe[1].sem, n_pe[1].now(i, u))
                        act.wait_ge(n_pe[3].sem, n_pe[3].old(i, u))
                        act.activation(flat(h1T, u), banks[2 + u], ACT.Relu, bias=b1_col[:, :]).then_inc(n_act[1].sem, 1)
                    for u in range(2):
                        act.wait_ge(n_pe[2].sem, n_pe[2].now(i, u))
                        act.wait_ge(n_pe[4].sem, n_pe[4].old(i, u))
                        act.activation(flat(h2T, u), banks[6 + u], ACT.Relu, bias=b2_col[:, :]).then_inc(n_act[2].sem, 1)
                    for u in range(2):
                        act.wait_ge(n_pe[3].sem, n_pe[3].now(i, u))
                        act.wait_ge(n_out[0].sem[u], n_out[0].old(i))
                        act.copy(flat(h1n, u), banks[4 + u]).then_inc(n_act[3].sem, 1)

            @block.vector
            def _(dve):
                with pairs(dve, CN) as i:
                    for u in range(2):
                        dve.wait_ge(n_pe[4].sem, n_pe[4].now(i, u))
                        dve.wait_ge(n_dve[2].sem, n_dve[2].old(i, u))
                        dve.tensor_tensor(flat(y, u), banks[u], flat(xin, u), ALU.add).then_inc(n_dve[0].sem, 1)
                    for u in range(2):
                        dve.wait_ge(n_dve[0].sem, n_dve[0].now(i, u))
                        dve.wait_ge(n_pool[6].sem, n_pool[6].old(i, u))
                        stats(dve, nst[0], y, u).then_inc(n_dve[1].sem, 1)
                    for u in range(2):
                        dve.wait_ge(n_pool[1].sem, n_pool[1].now(i, u))
                        dve.wait_ge(n_out[1].sem[u], n_out[1].old(i))
                        dve.wait_ge(n_pool[4].sem, n_pool[4].old(i, u))
                        normalise(dve, x1n, y, nst[0], nrs[0], u).then_inc(n_dve[2].sem, 1)

            @block.gpsimd
            def _(pool):
                with pairs(pool, CN) as i:
                    for u in range(2):
                        p_wait(pool, n_dve[2].sem, n_dve[2].old(i, u))
                        rstd(pool, i, u, nst[0], nv[0], nrs[0], n_dve[1], n_pool[0], n_pool[1])
                    for u in range(2):
                        p_wait(pool, n_pool[1].sem, n_pool[1].now(i, u))
                        pool.tensor_tensor(nv[1][:, u, :], nrs[0][:, u, :], nrs[0][:, u, :], ALU.mult).then_inc(n_pool[5].sem, 1)
                        p_wait(pool, n_pool[5].sem, n_pool[5].now(i, u))
                        pool.tensor_tensor(nv[2][:, u, :], nv[1][:, u, :], nst[0][:, u, :, 2], ALU.mult).then_inc(n_pool[6].sem, 1)
                        p_wait(pool, n_pool[6].sem, n_pool[6].now(i, u))
                        pool.tensor_scalar(nv[1][:, u, :], nv[2][:, u, :], 1.0 / D, EPS, ALU.mult, ALU.add).then_inc(n_pool[2].sem, 1)
                        p_wait(pool, n_pool[2].sem, n_pool[2].now(i, u))
                        pool.tensor_tensor(nrs[1][:, u, :], nv[1][:, u, :], minus_half[:, 0:TPC], ALU.pow).then_inc(n_pool[3].sem, 1)
                        p_wait(pool, n_pool[3].sem, n_pool[3].now(i, u))
                        p_wait(pool, n_dve[2].sem, n_dve[2].now(i, u))
                        p_wait(pool, n_out[2].sem[u], n_out[2].old(i))
                        for k in range(TPC):
                            last = pool.tensor_scalar(x2n[:, u, k, :], x1n[:, u, k, :], nrs[1][:, u, k:k + 1], None, ALU.mult)
                        last.then_inc(n_pool[4].sem, 1)
        end_phase(CN)

        def node_transformer(l):
            src_t, dst_t = (T3, T4) if l == 0 else (T4, T5)
            xin, xh, xhT, xc, tmp, yy, yb, zz, res = nb
            out_b = zz if l == 0 else tmp
            with nc.Block() as block:
                @block.sync
                def _(sp):
                    loads = [(src_t, xin, n_in)] + ([(T3, res, n_in2)] if l else [])
                    node_sync(sp, loads, [(dst_t, out_b, n_out[0], n_dve[11] if l else n_dve[7])], False, None)

                @block.tensor
                def _(pe):
                    with pairs(pe, CN) as i:
                        for u in range(2):
                            pe.wait_ge(n_dve[1].sem, n_dve[1].now(i, u))
                            pe.wait_ge(n_act[1].sem, n_act[1].old(i, u))
                            tiles_T(pe, banks[u], lambda k: xh[:, u, k, :], u).then_inc(n_pe[0].sem, 1)
                        for u in range(2):
                            pe.wait_ge(n_act[0].sem, n_act[0].now(i, u))
                            pe.wait_ge(n_dve[7].sem, n_dve[7].old(i, u))
                            for k in range(TPC):
                                last = pe.matmul(banks[2 + u][:, k * D:(k + 1) * D], xhT[:, u, k, :], w_vo[:, l, :], start=True, stop=True)
                            last.then_inc(n_pe[1].sem, 1)
                        for u in range(2):
                            pe.wait_ge(n_dve[5].sem, n_dve[5].now(i, u))
                            tiles_T(pe, banks[u], lambda k: xh[:, u, k, :], u).then_inc(n_pe[2].sem, 1)
                        for u in range(2):
                            pe.wait_ge(n_act[1].sem, n_act[1].now(i, u))
                            for j in range(FJ):
                                pe.wait_ge(n_act[3 + j].sem, n_act[3 + j].last(i, u))
                                pe.matmul(banks[4 + j], w_up[:, l, j * D:(j + 1) * D], flat(xhT, u), start=True,
                                          stop=True).then_inc(n_pe[4 + j].sem, 1)
                        for u in range(2):
                            pe.wait_ge(n_act[6].sem, n_act[6].now(i, u))
                            pe.wait_ge(n_dve[6].sem, n_dve[6].now(i, u))
                            for k in range(TPC):
                                for j in range(FJ):
                                    last = pe.matmul(banks[2 + u][:, k * D:(k + 1) * D], hT[:, u, j, k * D:(k + 1) * D],
                                                     w_down[:, l, j, :], start=(j == 0), stop=(j == FJ - 1))
                            last.then_inc(n_pe[8].sem, 1)

                @block.scalar
                def _(act):
                    with pairs(act, CN) as i:
                        for u in range(2):
                            act.wait_ge(n_pe[0].sem, n_pe[0].now(i, u))
                            act.wait_ge(n_pe[7].sem, n_pe[7].old(i, u))
                            act.copy(flat(xhT, u), banks[u]).then_inc(n_act[0].sem, 1)
                        for u in range(2):
                            act.wait_ge(n_pe[2].sem, n_pe[2].now(i, u))
                            act.copy(flat(xhT, u), banks[u]).then_inc(n_act[1].sem, 1)
                        for u in range(2):
                            for j in range(FJ):
                                act.wait_ge(n_pe[4 + j].sem, n_pe[4 + j].now(i, u))
                                if j == 0:
                                    act.wait_ge(n_pe[8].sem, n_pe[8].old(i, u))
                                act.activation(hT[:, u, j, :], banks[4 + j], ACT.Gelu,
                                               bias=b_up[:, l, j:j + 1]).then_inc(n_act[3 + j].sem, 1)

                @block.vector
                def _(dve):
                    with pairs(dve, CN) as i:
                        for u in range(2):
                            dve.wait_ge(n_in.sem[u], n_in.now(i))
                            dve.wait_ge(n_dve[1].sem, n_dve[1].old(i, u))
                            stats(dve, nst[0], xin, u).then_inc(n_dve[0].sem, 1)
                        for u in range(2):
                            dve.wait_ge(n_pool[1].sem, n_pool[1].now(i, u))
                            dve.wait_ge(n_pe[2].sem, n_pe[2].old(i, u))
                            normalise(dve, xh, xin, nst[0], nrs[0], u).then_inc(n_dve[1].sem, 1)
                        for u in range(2):
                            dve.wait_ge(n_pe[1].sem, n_pe[1].now(i, u))
                            dve.wait_ge((n_dve[11] if l else n_dve[3]).sem, (n_dve[11] if l else n_dve[3]).old(i, u))
                            if l:
                                dve.wait_ge(n_out[0].sem[u], n_out[0].old(i))
                            for k in range(TPC):
                                last = dve.scalar_tensor_tensor(tmp[:, u, k, :], u_vo[:, l, :], deg_node[:, bass.ds(i * TPC + (u * TPC + k), 1)],
                                                                banks[2 + u][:, k * D:(k + 1) * D], ALU.mult, ALU.add)
                            last.then_inc(n_dve[6].sem, 1)
                            dve.wait_ge(n_dve[6].sem, n_dve[6].now(i, u))
                            dve.wait_ge(n_pool[4].sem, n_pool[4].now(i, u))
                            dve.wait_ge(n_pool[5].sem, n_pool[5].old(i, u))
                            dve.wait_ge(n_dve[5].sem, n_dve[5].old(i, u))
                            dve.tensor_tensor(flat(yy, u), flat(tmp, u), flat(xc, u), ALU.add).then_inc(n_dve[3].sem, 1)
                        for u in range(2):
                            dve.wait_ge(n_dve[3].sem, n_dve[3].now(i, u))
                            stats(dve, nst[1], yy, u).then_inc(n_dve[4].sem, 1)
                        for u in range(2):
                            dve.wait_ge(n_pool[3].sem, n_pool[3].now(i, u))
                            dve.wait_ge(n_pe[0].sem, n_pe[0].now(i, u))
                            normalise(dve, xh, yy, nst[1], nrs[1], u).then_inc(n_dve[5].sem, 1)
                        for u in range(2):
                            dve.wait_ge(n_pe[8].sem, n_pe[8].now(i, u))
                            dve.wait_ge(n_pool[5].sem, n_pool[5].now(i, u))
                            if l == 0:
                                dve.wait_ge(n_out[0].sem[u], n_out[0].old(i))
                            else:
                                dve.wait_ge(n_dve[8].sem, n_dve[8].old(i, u))
                            dve.tensor_tensor(flat(zz, u), banks[2 + u], flat(yb, u), ALU.add).then_inc(n_dve[7].sem, 1)
                        if l:
                            for u in range(2):
                                dve.wait_ge(n_dve[7].sem, n_dve[7].now(i, u))
                                dve.wait_ge(n_in2.sem[u], n_in2.now(i))
                                dve.wait_ge(n_dve[11].sem, n_dve[11].old(i, u))
                                dve.tensor_tensor(flat(xc, u), flat(zz, u), flat(res, u), ALU.add).then_inc(n_dve[8].sem, 1)
                            for u in range(2):
                                dve.wait_ge(n_dve[8].sem, n_dve[8].now(i, u))
                                stats(dve, nst[2], xc, u).then_inc(n_dve[9].sem, 1)
                            for u in range(2):
                                dve.wait_ge(n_pool[7].sem, n_pool[7].now(i, u))
                                normalise(dve, tmp, xc, nst[2], nrs[2], u).then_inc(n_dve[11].sem, 1)

                @block.gpsimd
                def _(pool):
                    with pairs(pool, CN) as i:
                        for u in range(2):
                            p_wait(pool, n_dve[1].sem, n_dve[1].old(i, u))
                            rstd(pool, i, u, nst[0], nv[0], nrs[0], n_dve[0], n_pool[0], n_pool[1])
                        for u in range(2):
                            s = n_dve[11] if l else n_dve[3]
                            p_wait(pool, s.sem, s.old(i, u))
                            pool.tensor_tensor(xc[:, u, :, :], xin[:, u, :, :],
                                               c_vo[:, l, :].unsqueeze(1).broadcast_to([D, TPC, D]), ALU.add).then_inc(n_pool[4].sem, 1)
                        for u in range(2):
                            p_wait(pool, n_dve[3].sem, n_dve[3].now(i, u))
                            p_wait(pool, n_dve[7].sem, n_dve[7].old(i, u))
                            pool.tensor_tensor(yb[:, u, :, :], yy[:, u, :, :],
                                               b_down[:, l, :].unsqueeze(1).broadcast_to([D, TPC, D]), ALU.add).then_inc(n_pool[5].sem, 1)
                        for u in range(2):
                            p_wait(pool, n_dve[5].sem, n_dve[5].old(i, u))
                            rstd(pool, i, u, nst[1], nv[1], nrs[1], n_dve[4], n_pool[2], n_pool[3])
                        if l:
                            for u in range(2):
                                p_wait(pool, n_dve[11].sem, n_dve[11].old(i, u))
                                rstd(pool, i, u, nst[2], nv[2], nrs[2], n_dve[9], n_pool[6], n_pool[7])
            end_phase(CN)

        node_transformer(0)
        node_transformer(1)

        xin, xa, xb_, ee, tt, nn, yy, oo, _x = nb
        y3 = nsb("node_y3", [D, 2, TPC, D])
        e1 = yy
        yy = nsb("node_yy", [D, 2, TPC, D])
        tabs = [T6, T7, T8]
        with nc.Block() as block:
            @block.sync
            def _(sp):
                node_sync(sp, [(T5, xin, n_in)],
                          [(T6, nn, n_out[0], n_act[4]), (T7, y3, n_out[1], n_act[5]), (T8, tt, n_out[2], n_act[6]),
                           (t["out"], oo, n_out[3], n_dve[11])], False, t["out"])

            @block.tensor
            def _(pe):
                with pairs(pe, CN) as i:
                    for u in range(2):
                        pe.wait_ge(n_in.sem[u], n_in.now(i))
                        pe.wait_ge(n_dve[8].sem, n_dve[8].old(i, u))
                        tiles_T(pe, banks[u], lambda k: xin[:, u, k, :], u).then_inc(n_pe[0].sem, 1)
                    for r in range(4):
                        for u in range(2):
                            if r == 0:
                                pe.wait_ge(n_act[0].sem, n_act[0].now(i, u))
                                pe.wait_ge(n_dve[3].sem, n_dve[3].old(i, u))
                            else:
                                pe.wait_ge(n_dve[r - 1].sem, n_dve[r - 1].now(i, u))
                            pe.matmul(banks[2 + u], w_root[:, r, :], flat(xa if r % 2 == 0 else xb_, u), start=True,
                                      stop=True).then_inc(n_pe[1 + r].sem, 1)
                            if r > 0:
                                if r == 1:
                                    pe.wait_ge(n_act[6].sem, n_act[6].old(i, u))
                                else:
                                    pe.wait_ge(n_act[4 + r - 2].sem, n_act[4 + r - 2].now(i, u))
                                src_ = xa if r % 2 == 0 else xb_
                                tiles_T(pe, banks[4 + u], lambda k: src_[:, u, k, :], u).then_inc(n_pe[4 + r].sem, 1)
                    for u in range(2):
                        pe.wait_ge(n_dve[3].sem, n_dve[3].now(i, u))
                        tiles_T(pe, banks[u], lambda k: xa[:, u, k, :], u).then_inc(n_pe[8].sem, 1)

            @block.scalar
            def _(act):
                with pairs(act, CN) as i:
                    for u in range(2):
                        act.wait_ge(n_pe[0].sem, n_pe[0].now(i, u))
                        act.wait_ge(n_pe[8].sem, n_pe[8].old(i, u))
                        act.copy(flat(xa, u), banks[u]).then_inc(n_act[0].sem, 1)
                    for r in range(4):
                        for u in range(2):
                            act.wait_ge(n_pe[1 + r].sem, n_pe[1 + r].now(i, u))
                            if r == 0:
                                act.wait_ge(n_dve[7].sem, n_dve[7].old(i, u))
                            else:
                                act.wait_ge(n_dve[4 + r - 1].sem, n_dve[4 + r - 1].now(i, u))
                            act.activation(flat(ee, u), banks[2 + u], ACT.Exp, bias=rel_col[:, r:r + 1]).then_inc(
                                (n_act[1], n_act[2], n_act[3], n_act[7])[r].sem, 1)
                        if r > 0:
                            for u in range(2):
                                act.wait_ge(n_pe[4 + r].sem, n_pe[4 + r].now(i, u))
                                act.wait_ge(n_out[r - 1].sem[u], n_out[r - 1].old(i))
                                act.copy(flat((nn, y3, tt)[r - 1], u), banks[4 + u]).then_inc(n_act[3 + r].sem, 1)

            @block.vector
            def _(dve):
                with pairs(dve, CN) as i:
                    for r in range(4):
                        for u in range(2):
                            g = (n_act[1], n_act[2], n_act[3], n_act[7])[r]
                            dve.wait_ge(g.sem, g.now(i, u))
                            if r == 0:
                                dve.wait_ge(n_dve[3].sem, n_dve[3].old(i, u))
                            else:
                                dve.wait_ge(n_dve[r - 1].sem, n_dve[r - 1].now(i, u))
                            dve.tensor_scalar(flat(e1, u), flat(ee, u), 1.0, -1.0, ALU.min, ALU.add).then_inc(n_dve[4 + r].sem, 1)
                            dve.wait_ge(n_dve[4 + r].sem, n_dve[4 + r].now(i, u))
                            if r == 0:
                                dve.wait_ge(n_pe[7].sem, n_pe[7].old(i, u))
                            elif r == 1:
                                dve.wait_ge(n_pe[1].sem, n_pe[1].now(i, u))
                            elif r == 2:
                                dve.wait_ge(n_pe[5].sem, n_pe[5].now(i, u))
                            else:
                                dve.wait_ge(n_pe[6].sem, n_pe[6].now(i, u))
                            dve.scalar_tensor_tensor(flat(xb_ if r % 2 == 0 else xa, u), banks[2 + u], rel_col[:, r:r + 1],
                                                     flat(e1, u), ALU.add, ALU.max).then_inc(n_dve[r].sem, 1)
                    for u in range(2):
                        dve.wait_ge(n_pe[8].sem, n_pe[8].now(i, u))
                        dve.wait_ge(n_dve[11].sem, n_dve[11].old(i, u))
                        dve.tensor_tensor(flat(yy, u), banks[u], flat(xin, u), ALU.add).then_inc(n_dve[8].sem, 1)
                        dve.wait_ge(n_dve[8].sem, n_dve[8].now(i, u))
                        stats(dve, nst[0], yy, u).then_inc(n_dve[9].sem, 1)
                    for u in range(2):
                        dve.wait_ge(n_pool[1].sem, n_pool[1].now(i, u))
                        dve.wait_ge(n_out[3].sem[u], n_out[3].old(i))
                        normalise(dve, oo, yy, nst[0], nrs[0], u).then_inc(n_dve[11].sem, 1)

            @block.gpsimd
            def _(pool):
                with pairs(pool, CN) as i:
                    for u in range(2):
                        p_wait(pool, n_dve[11].sem, n_dve[11].old(i, u))
                        rstd(pool, i, u, nst[0], nv[0], nrs[0], n_dve[9], n_pool[0], n_pool[1])
        end_phase(CN)
        nodes.close()

        msg = sb("msg", [D, 2, D])
        xd = sb("xd", [D, 2, D])
        res_e = sb("res_e", [D, 2, D])
        aT = sb("aT", [D, 2, 2 * D])
        z = sb("z", [D, 2, D])
        ex = sb("ex", [D, 2, D])
        em = sb("em", [D, 2, D])
        ye = sb("ye", [D, 2, D])
        yo = sb("yo", [D, 2, D])
        est = sb("est", [D, 2, 6])
        eag = sb("eag", [D, 2, 2])
        ev = sb("ev", [D, 2, 2])
        ers = sb("ers", [D, 2, 2])

        def slot_rows(table, c, base):
            return table[bass.ds(c * D + base, D), :]

        def edge_sync(sp, loads, stores):
            def load(c, u):
                for table, base, buf, tr in loads:
                    sp.dma_start(buf[:, u, :], slot_rows(table, c, base)).then_inc(tr.sem[u], 16)

            def store(i, u):
                for table, base, buf, tr, sig in stores:
                    sp.wait_ge(sig.sem, sig.now(i, u))
                    sp.dma_start(slot_rows(table, i + u, base), buf[:, u, :]).then_inc(tr.sem[u], 16)
            load(0, 0)
            load(1, 1)
            if ET > 2:
                with pairs(sp, ET - 2) as i:
                    for u in range(2):
                        store(i, u)
                        load(i + (u + 2), u)
            for u in range(2):
                store(ET - 2, u)
            for _, _, _, tr, _ in stores:
                for u in range(2):
                    sp.wait_ge(tr.sem[u], tr.end(ET))

        def layer_norm_stats(dve, i, u, x, made):
            dve.wait_ge(made.sem, made.now(i, u))
            dve.bn_stats(est[:, u, :], x[:, u, :]).then_inc(st_set.sem, 1)
            dve.wait_ge(st_set.sem, st_set.now(i, u))
            dve.wait_ge(ln_set.sem, ln_set.old(i, u))
            dve.nop(nofuse=True)
            dve.bn_aggr(eag[:, u, :], est[:, u, :]).then_inc(c_set.sem, 1)

        def layer_norm_rstd(pool, i, u):
            p_wait(pool, c_set.sem, c_set.now(i, u))
            p_wait(pool, ln_set.sem, ln_set.old(i, u))
            pool.tensor_scalar(ev[:, u, 0:1], eag[:, u, 1:2], EPS, None, ALU.add).then_inc(v_set.sem, 1)
            p_wait(pool, v_set.sem, v_set.now(i, u))
            pool.tensor_tensor(ers[:, u, 0:1], ev[:, u, 0:1], minus_half[:, 0:1], ALU.pow).then_inc(rs_set.sem, 1)

        def layer_norm_out(dve, i, u, x, out):
            dve.wait_ge(rs_set.sem, rs_set.now(i, u))
            return dve.tensor_scalar(out[:, u, :], x[:, u, :], eag[:, u, 0:1], ers[:, u, 0:1], ALU.subtract, ALU.mult)

        def mean_round(table, wl, wr, bias, out_t, elu, norm, residual=None, first=False, final=False):
            res_t = {"x": (XD0, 0), "t5": (T5, NP)}.get(residual)
            made = ln_set if norm else y_set
            made_buf = yo if norm else ye
            own_in = got_dst if first else got_own
            put = put_rows if final else put_out
            with nc.Block() as block:
                @block.gpsimd
                def _(pool):
                    with pairs(pool, ET) as i:
                        for u in range(2):
                            gather(pool, i, u, msg[:, u, :], table, x_src if first else g_src, 0,
                                   (agg_done.sem, agg_done.old(i, u))).then_inc(got_src.sem[u], 16)
                            if first:
                                p_wait(pool, put_x.sem[u], put_x.old(i))
                                gather(pool, i, u, xd[:, u, :], table, x_dst, 1,
                                       (agg_done.sem, agg_done.old(i, u))).then_inc(got_dst.sem[u], 16)
                        for u in range(2):
                            if norm:
                                layer_norm_rstd(pool, i, u)
                        if final:
                            for u in range(2):
                                p_wait(pool, put_rows.sem[u], put_rows.old(i))
                            pool.tensor_copy(idx2f[:, :], put_row[:, bass.ds(i, 2)]).then_inc(row_set.sem, 2)
                            p_wait(pool, row_set.sem, row_set.now(i, 1))
                            for u in range(2):
                                p_wait(pool, ln_set.sem, ln_set.now(i, u))
                                pool.indirect_dma_start(t["out"], bass.IndirectOffsetOnAxis(ap=idx2f[:, u:u + 1], axis=0),
                                                        yo[:, u, :], None, bounds_check=N - 1,
                                                        oob_is_err=False).then_inc(put_rows.sem[u], 16)
                    if final:
                        for u in range(2):
                            pool.wait_ge(put_rows.sem[u], put_rows.end(ET))

                @block.sync
                def _(sp):
                    if first:
                        with pairs(sp, ET) as i:
                            for u in range(2):
                                sp.wait_ge(got_dst.sem[u], got_dst.now(i))
                                sp.dma_start(slot_rows(XD0, i + u, 0), xd[:, u, :]).then_inc(put_x.sem[u], 16)
                                sp.wait_ge(made.sem, made.now(i, u))
                                sp.dma_start(slot_rows(out_t, i + u, NP), made_buf[:, u, :]).then_inc(put_out.sem[u], 16)
                        for u in range(2):
                            sp.wait_ge(put_out.sem[u], put_out.end(ET))
                            sp.wait_ge(put_x.sem[u], put_x.end(ET))
                    else:
                        loads = [(table, NP, xd, got_own)]
                        if residual:
                            loads.append((res_t[0], res_t[1], res_e, got_res))
                        if not final:
                            edge_sync(sp, loads, [(out_t, NP, made_buf, put_out, made)])
                        else:
                            for c in range(2):
                                for tb, base, buf, tr in loads:
                                    sp.dma_start(buf[:, c, :], slot_rows(tb, c, base)).then_inc(tr.sem[c], 16)
                            with pairs(sp, ET - 2) as i:
                                for u in range(2):
                                    sp.wait_ge(ln_set.sem, ln_set.now(i, u))
                                    for tb, base, buf, tr in loads:
                                        sp.dma_start(buf[:, u, :], slot_rows(tb, i + (u + 2), base)).then_inc(tr.sem[u], 16)

                @block.tensor
                def _(pe):
                    with pairs(pe, ET) as i:
                        for u in range(2):
                            pe.wait_ge(seg_set.sem, seg_set.now(i, u))
                            pe.wait_ge(got_src.sem[u], got_src.now(i))
                            pe.wait_ge(own_in.sem[u], own_in.now(i))
                            pe.wait_ge(at_set.sem, at_set.old(i, u))
                            pe.wait_ge(carry_set.sem, carry_set.last(i, u))
                            pe.matmul(banks[2 + u][0:1, 0:D], seg[:, u, D - 1:D], msg[:, u, :], start=True, stop=False)
                            pe.matmul(banks[2 + u][0:1, 0:D], cont[0:1, u, D - 1:D], carry[0:1, 1 - u, 0:D], start=False, stop=True)
                            pe.matmul(banks[u][:, 0:D], msg[:, u, :], seg[:, u, :], start=True, stop=False)
                            pe.matmul(banks[u][:, 0:D], carry[0:1, 1 - u, 0:D], cont[0:1, u, :], start=False, stop=True)
                            pe.transpose(banks[u][:, D:2 * D], xd[:, u, :], ident[:, :]).then_inc(agg_done.sem, 1)
                        for u in range(2):
                            pe.wait_ge(at_set.sem, at_set.now(i, u))
                            pe.wait_ge(z_set.sem, z_set.old(i, u))
                            pe.matmul(banks[4 + u][:, 0:D], aT[:, u, 0:D], wl, start=True, stop=False)
                            pe.matmul(banks[4 + u][:, 0:D], aT[:, u, D:2 * D], wr, start=False, stop=True).then_inc(mm_done.sem, 1)

                @block.scalar
                def _(act):
                    with pairs(act, ET) as i:
                        for u in range(2):
                            act.wait_ge(agg_done.sem, agg_done.now(i, u))
                            act.copy(carry[0:1, u, 0:D], banks[2 + u][0:1, 0:D]).then_inc(carry_set.sem, 1)
                            act.wait_ge(mm_done.sem, mm_done.old(i, u))
                            act.copy(aT[:, u, :], banks[u][:, 0:2 * D]).then_inc(at_set.sem, 1)
                        for u in range(2):
                            if elu:
                                act.wait_ge(row_set2.sem, row_set2.now(i, u))
                                act.wait_ge(y_set.sem, y_set.old(i, u))
                                act.activation(ex[:, u, :], em[:, u, :], ACT.Exp).then_inc(e_set.sem, 1)
                            elif not norm:
                                act.wait_ge(z_set.sem, z_set.now(i, u))
                                act.wait_ge(put_out.sem[u], put_out.old(i))
                                act.activation(ye[:, u, :], z[:, u, :], ACT.Relu).then_inc(y_set.sem, 1)

                @block.vector
                def _(dve):
                    with pairs(dve, ET) as i:
                        for u in range(2):
                            dve.wait_ge(agg_done.sem, agg_done.old(i, u))
                            same_target(dve, i, u, True).then_inc(seg_set.sem, 1)
                        for u in range(2):
                            dve.wait_ge(mm_done.sem, mm_done.now(i, u))
                            dve.wait_ge(y_set.sem, y_set.old(i, u))
                            dve.tensor_tensor(z[:, u, :], banks[4 + u][:, 0:D], bias, ALU.add).then_inc(z_set.sem, 1)
                            if elu:
                                dve.wait_ge(z_set.sem, z_set.now(i, u))
                                dve.tensor_scalar(em[:, u, :], z[:, u, :], 0.0, None, ALU.min).then_inc(row_set2.sem, 1)
                        for u in range(2):
                            if elu:
                                dve.wait_ge(e_set.sem, e_set.now(i, u))
                                if norm:
                                    dve.scalar_tensor_tensor(em2[:, u, :], ex[:, u, :], -1.0, z[:, u, :], ALU.add, ALU.max).then_inc(elu_set.sem, 1)
                                    dve.wait_ge(elu_set.sem, elu_set.now(i, u))
                                    dve.wait_ge(got_res.sem[u], got_res.now(i))
                                    dve.wait_ge(ln_set.sem, ln_set.old(i, u))
                                    dve.tensor_tensor(ye[:, u, :], em2[:, u, :], res_e[:, u, :], ALU.add).then_inc(y_set.sem, 1)
                                else:
                                    dve.wait_ge(put.sem[u], put.old(i))
                                    dve.scalar_tensor_tensor(ye[:, u, :], ex[:, u, :], -1.0, z[:, u, :], ALU.add, ALU.max).then_inc(y_set.sem, 1)
                            elif norm:
                                dve.wait_ge(z_set.sem, z_set.now(i, u))
                                dve.wait_ge(got_res.sem[u], got_res.now(i))
                                dve.wait_ge(ln_set.sem, ln_set.old(i, u))
                                dve.scalar_tensor_tensor(ye[:, u, :], z[:, u, :], 0.0, res_e[:, u, :], ALU.max, ALU.add).then_inc(y_set.sem, 1)
                        if norm:
                            for u in range(2):
                                layer_norm_stats(dve, i, u, ye, y_set)
                            for u in range(2):
                                dve.wait_ge(put.sem[u], put.old(i))
                                layer_norm_out(dve, i, u, ye, yo).then_inc(ln_set.sem, 1)
            end_phase(ET)

        row_set2, elu_set = edge_signal("min_set"), edge_signal("elu_set")
        em2 = sb("em2", [D, 2, D])
        idx2f = sb("idx2f", [D, 2], I32)
        E3 = [edge_signal(f"more_{x}") for x in range(22)]
        start_signals()

        mean_round(t["x"], W["L0_gnn_W1_l"][:, :], W["L0_gnn_W1_r"][:, :], b1_row[:, :], T1, elu=False, norm=False, first=True)
        mean_round(T1, W["L0_gnn_W2_l"][:, :], W["L0_gnn_W2_r"][:, :], b2_row[:, :], T2, elu=False, norm=True, residual="x")

        zp = sb("zp", [D, 2, 2 * MUL + 9 * MUL])
        prod = sb("prod", [D, 2, 3, MUL, 3])
        pr1 = sb("pr1", [D, 2, MUL, 3])
        zT = sb("zT", [3 * MUL, 2, 4, D])
        (zp_done, zagg_done, zcarry, zT_set, w_done, l1_sum, prod_set) = E3[0:7]
        G0, G1 = 2 * MUL, 3 * MUL
        NZ = G0 + 3 * G1
        with nc.Block() as block:
            @block.gpsimd
            def _(pool):
                with pairs(pool, ET) as i:
                    for u in range(2):
                        gather(pool, i, u, msg[:, u, :], T2, g_src, 0,
                               (zp_done.sem, zp_done.old(i, u))).then_inc(got_src.sem[u], 16)
                    for u in range(2):
                        layer_norm_rstd(pool, i, u)

            @block.sync
            def _(sp):
                edge_sync(sp, [(T2, NP, res_e, got_res)], [(T3, NP, yo, put_out, ln_set)])

            @block.vector
            def _(dve):
                with pairs(dve, ET) as i:
                    for u in range(2):
                        dve.wait_ge(zagg_done.sem, zagg_done.old(i, u))
                        same_target(dve, i, u, False).then_inc(seg_set.sem, 1)
                    for u in range(2):
                        a = ea[:, bass.ds(i + u, 1), :].rearrange("p o c -> p (o c)")
                        m = coef[:, bass.ds(i + u, 1), :, :].rearrange("p o k i -> p (o k) i")
                        s = msg[:, u, 0:MUL]
                        v = msg[:, u, MUL:].rearrange("p (u i) -> p u i", i=3)
                        zk = zp[:, u, G0:].rearrange("p (k g w) -> p k g w", k=3, g=3)
                        dve.wait_ge(got_src.sem[u], got_src.now(i))
                        dve.tensor_tensor(pr1[:, u, :, :], v, a[:, 1:4].unsqueeze(1).broadcast_to([D, MUL, 3]), ALU.mult)
                        for k in range(3):
                            last = dve.tensor_tensor(prod[:, u, k, :, :], v, m[:, k, :].unsqueeze(1).broadcast_to([D, MUL, 3]), ALU.mult)
                        last.then_inc(prod_set.sem, 1)
                        dve.tensor_scalar(zp[:, u, 0:MUL], s, a[:, 0:1], None, ALU.mult)
                        for k in range(3):
                            dve.tensor_scalar(zk[:, k, 0, :], s, a[:, 1 + k:2 + k], None, ALU.mult)
                            dve.tensor_scalar(zk[:, k, 1, :], v[:, :, k], a[:, 0:1], None, ALU.mult)
                        dve.wait_ge(prod_set.sem, prod_set.now(i, u))
                        dve.tensor_reduce(zp[:, u, MUL:2 * MUL], pr1[:, u, :, :], AX.X, ALU.add)
                        dve.tensor_reduce(zk[:, :, 2, :], prod[:, u, :, :, :], AX.X, ALU.add).then_inc(zp_done.sem, 1)
                    for u in range(2):
                        dve.wait_ge(w_done.sem, w_done.now(i, u))
                        dve.wait_ge(got_res.sem[u], got_res.now(i))
                        dve.wait_ge(ln_set.sem, ln_set.old(i, u))
                        dve.tensor_tensor(ye[:, u, 0:MUL], banks[6 + u][:, 0:MUL], res_e[:, u, 0:MUL], ALU.add)
                        dve.tensor_tensor(ye[:, u, MUL:].rearrange("p (w k) -> p w k", k=3),
                                          banks[6 + u][:, MUL:4 * MUL].rearrange("p (k w) -> p w k", k=3),
                                          res_e[:, u, MUL:].rearrange("p (w k) -> p w k", k=3), ALU.add).then_inc(l1_sum.sem, 1)
                    for u in range(2):
                        layer_norm_stats(dve, i, u, ye, l1_sum)
                    for u in range(2):
                        dve.wait_ge(put_out.sem[u], put_out.old(i))
                        layer_norm_out(dve, i, u, ye, yo).then_inc(ln_set.sem, 1)

            @block.tensor
            def _(pe):
                def group(k):
                    return (0, G0) if k == 0 else (G0 + (k - 1) * G1, G1)
                with pairs(pe, ET) as i:
                    for u in range(2):
                        pe.wait_ge(zp_done.sem, zp_done.now(i, u))
                        pe.wait_ge(seg_set.sem, seg_set.now(i, u))
                        pe.wait_ge(zT_set.sem, zT_set.old(i, u))
                        pe.wait_ge(zcarry.sem, zcarry.last(i, u))
                        pe.matmul(banks[2 + u][0:1, 0:NZ], seg[:, u, D - 1:D], zp[:, u, :], start=True, stop=False)
                        pe.matmul(banks[2 + u][0:1, 0:NZ], cont[0:1, u, D - 1:D], carry[0:1, 1 - u, 0:NZ], start=False, stop=True)
                        for k in range(4):
                            at, n = group(k)
                            pe.matmul(banks[u][0:n, k * D:(k + 1) * D], zp[:, u, at:at + n], seg[:, u, :], start=True, stop=False)
                            last = pe.matmul(banks[u][0:n, k * D:(k + 1) * D], carry[0:1, 1 - u, at:at + n], cont[0:1, u, :],
                                             start=False, stop=True)
                        last.then_inc(zagg_done.sem, 1)
                    for u in range(2):
                        pe.wait_ge(zT_set.sem, zT_set.now(i, u))
                        pe.wait_ge(l1_sum.sem, l1_sum.old(i, u))
                        for k in range(4):
                            n = group(k)[1]
                            last = pe.matmul(banks[6 + u][:, k * MUL:(k + 1) * MUL], zT[0:n, u, k, :],
                                             (tp0 if k == 0 else tp1)[:, :], start=True, stop=True)
                        last.then_inc(w_done.sem, 1)

            @block.scalar
            def _(act):
                with pairs(act, ET) as i:
                    for u in range(2):
                        act.wait_ge(zagg_done.sem, zagg_done.now(i, u))
                        act.copy(carry[0:1, u, 0:NZ], banks[2 + u][0:1, 0:NZ]).then_inc(zcarry.sem, 1)
                        act.wait_ge(w_done.sem, w_done.old(i, u))
                        act.copy(zT[0:G0, u, 0, :], banks[u][0:G0, 0:D])
                        act.copy(zT[:, u, 1:4, :], banks[u][0:G1, D:4 * D].rearrange("p (k e) -> p k e", k=3)).then_inc(zT_set.sem, 1)
        end_phase(ET)

        xp = sb("xp", [D, 2, 2, D])
        raw2 = sb("raw2", [D, 2, 2, D])
        xpT = sb("xpT", [D, 2, 2, D])
        add_s = sb("add_s", [D, 2, 2 * D])
        add_d = sb("add_d", [D, 2, 3 * D])
        kv_s = sb("kv_s", [D, 2, 2 * D])
        qkv_d = sb("qkv_d", [D, 2, 3 * D])
        qk = sb("qk", [D, 2, 2, H, HD])
        att = sb("att", [D, 2, 2, H])
        att2 = sb("att2", [D, 2, 2, H])
        exa = sb("exa", [D, 2, 2, H])
        NM = D + H
        am = sb("am", [D, 2, NM])
        own = sb("own", [D, 2, NM])
        num = sb("num", [D, 2, NM])
        rden = sb("rden", [D, 2, H])
        ag = sb("ag", [D, 2, D])
        agT = sb("agT", [D, 2, D])
        xo = sb("xo", [D, 2, D])
        x2 = sb("x2", [D, 2, D])
        hE = sb("hE", [D, 2, FJ, D])
        z2 = sb("z2", [D, 2, D])
        ast2 = sb("ast2", [D, 2, 2, 3])

        def attention_round(l):
            src_t, dst_t = (T3, T4) if l == 0 else (T4, T5)
            (a_st, a_v, a_rs, a_ln, a_T, a_xT, a_mm, a_qkv, a_qk, a_att, a_exp, a_am, a_agg, a_num, a_ag, a_agt) = E3[0:16]
            (a_agT, a_wo, a_x2, a_ln2, a_t2, a_t2s) = E3[16:22]
            with nc.Block() as block:
                @block.gpsimd
                def _(pool):
                    with pairs(pool, ET) as i:
                        for u in range(2):
                            free = (a_x2.sem, a_x2.old(i, u))
                            gather(pool, i, u, raw2[:, u, 0, :], src_t, g_src, 0, free).then_inc(got_src.sem[u], 16)
                            gather(pool, i, u, raw2[:, u, 1, :], src_t, g_dst, 1, free).then_inc(got_dst.sem[u], 16)
                        for u in range(2):
                            p_wait(pool, a_st.sem, a_st.now(i, u))
                            p_wait(pool, a_ln.sem, a_ln.old(i, u))
                            pool.tensor_scalar(ev[:, u, :], ast2[:, u, :, 2], 1.0 / D, EPS, ALU.mult, ALU.add).then_inc(a_v.sem, 1)
                            p_wait(pool, a_v.sem, a_v.now(i, u))
                            pool.tensor_tensor(ers2[:, u, :], ev[:, u, :], minus_half[:, 0:2], ALU.pow).then_inc(a_rs.sem, 1)
                        for u in range(2):
                            layer_norm_rstd(pool, i, u)
                        if l:
                            for u in range(2):
                                p_wait(pool, f_st.sem, f_st.now(i, u))
                                p_wait(pool, f_ln.sem, f_ln.old(i, u))
                                pool.tensor_scalar(fv[:, u, :], fag[:, u, 1:2], EPS, None, ALU.add).then_inc(f_v.sem, 1)
                                p_wait(pool, f_v.sem, f_v.now(i, u))
                                pool.tensor_tensor(frs[:, u, :], fv[:, u, :], minus_half[:, 0:1], ALU.pow).then_inc(f_rs.sem, 1)

                @block.sync
                def _(sp):
                    if l == 0:
                        edge_sync(sp, [], [(dst_t, NP, z2, put_out, y_set)])
                    else:
                        edge_sync(sp, [(T3, NP, res_e, got_res)], [(dst_t, NP, yo, put_out, f_ln)])

                @block.vector
                def _(dve):
                    with pairs(dve, ET) as i:
                        for u in range(2):
                            dve.wait_ge(a_agg.sem, a_agg.old(i, u))
                            same_target(dve, i, u, False).then_inc(seg_set.sem, 1)
                            dve.wait_ge(got_src.sem[u], got_src.now(i))
                            dve.wait_ge(got_dst.sem[u], got_dst.now(i))
                            dve.bn_stats(ast2[:, u, :, :].rearrange("p e f -> p (e f)"),
                                         raw2[:, u, :, :].rearrange("p e d -> p d e")).then_inc(a_st.sem, 1)
                        for u in range(2):
                            dve.wait_ge(a_qkv.sem, a_qkv.old(i, u))
                            dve.scalar_tensor_tensor(add_s[:, u, :], u_qkv[:, l, D:], deg_src[:, bass.ds(i + u, 1)],
                                                     c_qkv[:, l, D:], ALU.mult, ALU.add)
                            dve.scalar_tensor_tensor(add_d[:, u, :], u_qkv[:, l, :], deg_dst[:, bass.ds(i + u, 1)],
                                                     c_qkv[:, l, :], ALU.mult, ALU.add).then_inc(add_set.sem, 1)
                        for u in range(2):
                            dve.wait_ge(a_rs.sem, a_rs.now(i, u))
                            dve.wait_ge(a_T.sem, a_T.old(i, u))
                            for j in range(2):
                                last = dve.tensor_scalar(xp[:, u, j, :], raw2[:, u, j, :], ast2[:, u, j, 1:2], ers2[:, u, j:j + 1],
                                                         ALU.subtract, ALU.mult)
                            last.then_inc(a_ln.sem, 1)
                        for u in range(2):
                            dve.wait_ge(a_mm.sem, a_mm.now(i, u))
                            dve.wait_ge(add_set.sem, add_set.now(i, u))
                            dve.wait_ge(a_am.sem, a_am.old(i, u))
                            dve.tensor_tensor(kv_s[:, u, :], banks[2 + u][:, 0:2 * D], add_s[:, u, :], ALU.add)
                            dve.tensor_tensor(qkv_d[:, u, :], banks[4 + u][:, 0:3 * D], add_d[:, u, :], ALU.add).then_inc(a_qkv.sem, 1)
                        for u in range(2):
                            dve.wait_ge(a_qkv.sem, a_qkv.now(i, u))
                            q = qkv_d[:, u, 0:D]
                            dve.tensor_tensor(qk[:, u, 0].rearrange("p h d -> p (h d)"), q, kv_s[:, u, 0:D], ALU.mult)
                            dve.tensor_tensor(qk[:, u, 1].rearrange("p h d -> p (h d)"), q, qkv_d[:, u, D:2 * D], ALU.mult).then_inc(a_qk.sem, 1)
                            dve.wait_ge(a_qk.sem, a_qk.now(i, u))
                            dve.tensor_reduce(att[:, u, :, :], qk[:, u, :, :, :], AX.X, ALU.add).then_inc(att_sum.sem, 1)
                            dve.wait_ge(att_sum.sem, att_sum.now(i, u))
                            dve.tensor_scalar(att2[:, u, :, :], att[:, u, :, :], HD ** -0.5, ATT_CLIP, ALU.mult, ALU.min).then_inc(att_min.sem, 1)
                            dve.wait_ge(att_min.sem, att_min.now(i, u))
                            dve.wait_ge(a_exp.sem, a_exp.old(i, u))
                            dve.tensor_scalar(att3[:, u, :, :], att2[:, u, :, :], -ATT_CLIP, None, ALU.max).then_inc(a_att.sem, 1)
                        for u in range(2):
                            dve.wait_ge(a_exp.sem, a_exp.now(i, u))
                            dve.wait_ge(a_num.sem, a_num.old(i, u))
                            for j, (to, v) in enumerate([(am, kv_s[:, u, D:2 * D]), (own, qkv_d[:, u, 2 * D:3 * D])]):
                                dve.tensor_tensor(to[:, u, 0:D].rearrange("p (h d) -> p h d", d=HD),
                                                  v.rearrange("p (h d) -> p h d", d=HD),
                                                  exa[:, u, j, :].unsqueeze(2).broadcast_to([D, H, HD]), ALU.mult)
                                last = dve.tensor_copy(to[:, u, D:NM], exa[:, u, j, :])
                            last.then_inc(a_am.sem, 1)
                        for u in range(2):
                            dve.wait_ge(a_agg.sem, a_agg.now(i, u))
                            dve.wait_ge(a_am.sem, a_am.now(i, u))
                            dve.wait_ge(carry_set.sem, carry_set.now(i, u))
                            dve.wait_ge(a_ag.sem, a_ag.old(i, u))
                            dve.tensor_tensor(num[:, u, :], banks[6 + u][:, 0:NM], own[:, u, :], ALU.add).then_inc(a_num.sem, 1)
                            dve.wait_ge(a_num.sem, a_num.now(i, u))
                            dve.reciprocal(rden[:, u, :], num[:, u, D:NM]).then_inc(rden_set.sem, 1)
                            dve.wait_ge(rden_set.sem, rden_set.now(i, u))
                            dve.wait_ge(a_agt.sem, a_agt.old(i, u))
                            dve.tensor_tensor(ag[:, u, :].rearrange("p (h d) -> p h d", d=HD),
                                              num[:, u, 0:D].rearrange("p (h d) -> p h d", d=HD),
                                              rden[:, u, :].unsqueeze(2).broadcast_to([D, H, HD]), ALU.mult).then_inc(a_ag.sem, 1)
                        for u in range(2):
                            dve.wait_ge(c_set.sem, c_set.old(i, u))
                            dve.wait_ge(a_x2.sem, a_x2.old(i, u))
                            dve.tensor_tensor(xo[:, u, :], raw2[:, u, 1, :], bo_row[:, l, :], ALU.add).then_inc(xo_set.sem, 1)
                            dve.wait_ge(xo_set.sem, xo_set.now(i, u))
                            dve.wait_ge(a_wo.sem, a_wo.now(i, u))
                            dve.wait_ge(z_set.sem, z_set.old(i, u))
                            dve.tensor_tensor(x2[:, u, :], banks[2 + u][:, 256:384], xo[:, u, :], ALU.add).then_inc(a_x2.sem, 1)
                        for u in range(2):
                            layer_norm_stats(dve, i, u, x2, a_x2)
                        for u in range(2):
                            dve.wait_ge(a_t2.sem, a_t2.old(i, u))
                            layer_norm_out(dve, i, u, x2, yln).then_inc(ln_set.sem, 1)
                            dve.tensor_tensor(z[:, u, :], x2[:, u, :], b_down[:, l, :], ALU.add).then_inc(z_set.sem, 1)
                        for u in range(2):
                            dve.wait_ge(mm_done.sem, mm_done.now(i, u))
                            dve.wait_ge(z_set.sem, z_set.now(i, u))
                            if l == 0:
                                dve.wait_ge(put_out.sem[u], put_out.old(i))
                            else:
                                dve.wait_ge(f_sum.sem, f_sum.old(i, u))
                            dve.tensor_tensor(z2[:, u, :], banks[6 + u][:, 384:512], z[:, u, :], ALU.add).then_inc(y_set.sem, 1)
                        if l:
                            for u in range(2):
                                dve.wait_ge(y_set.sem, y_set.now(i, u))
                                dve.wait_ge(got_res.sem[u], got_res.now(i))
                                dve.wait_ge(f_ln.sem, f_ln.old(i, u))
                                dve.tensor_tensor(ye[:, u, :], z2[:, u, :], res_e[:, u, :], ALU.add).then_inc(f_sum.sem, 1)
                                dve.wait_ge(f_sum.sem, f_sum.now(i, u))
                                dve.bn_stats(fst[:, u, :], ye[:, u, :]).then_inc(f_bn.sem, 1)
                                dve.wait_ge(f_bn.sem, f_bn.now(i, u))
                                dve.nop(nofuse=True)
                                dve.bn_aggr(fag[:, u, :], fst[:, u, :]).then_inc(f_st.sem, 1)
                            for u in range(2):
                                dve.wait_ge(f_rs.sem, f_rs.now(i, u))
                                dve.wait_ge(put_out.sem[u], put_out.old(i))
                                dve.tensor_scalar(yo[:, u, :], ye[:, u, :], fag[:, u, 0:1], frs[:, u, :], ALU.subtract,
                                                  ALU.mult).then_inc(f_ln.sem, 1)

                @block.tensor
                def _(pe):
                    with pairs(pe, ET) as i:
                        for u in range(2):
                            pe.wait_ge(a_ln.sem, a_ln.now(i, u))
                            pe.wait_ge(a_t2s.sem, a_t2s.old(i, u))
                            for j in range(2):
                                last = pe.transpose(banks[u][:, j * D:(j + 1) * D], xp[:, u, j, :], ident[:, :])
                            last.then_inc(a_T.sem, 1)
                        for u in range(2):
                            pe.wait_ge(a_xT.sem, a_xT.now(i, u))
                            pe.wait_ge(a_x2.sem, a_x2.old(i, u))
                            pe.matmul(banks[2 + u][:, 0:2 * D], xpT[:, u, 0, :], w_qkv[:, l, D:3 * D], start=True, stop=True)
                            pe.wait_ge(g_last.sem, g_last.old(i, u))
                            pe.matmul(banks[4 + u][:, 0:3 * D], xpT[:, u, 1, :], w_qkv[:, l, :], start=True, stop=True).then_inc(a_mm.sem, 1)
                        for u in range(2):
                            pe.wait_ge(a_am.sem, a_am.now(i, u))
                            pe.wait_ge(seg_set.sem, seg_set.now(i, u))
                            pe.wait_ge(y_set.sem, y_set.old(i, u))
                            pe.wait_ge(carry_set.sem, carry_set.last(i, u))
                            pe.matmul(banks[6 + u][0:1, NM:2 * NM], seg[:, u, D - 1:D], am[:, u, :], start=True, stop=False)
                            pe.matmul(banks[6 + u][0:1, NM:2 * NM], cont[0:1, u, D - 1:D], carry[0:1, 1 - u, 0:NM], start=False, stop=True)
                            pe.matmul(banks[6 + u][:, 0:NM], seg[:, u, :], am[:, u, :], start=True, stop=False)
                            pe.matmul(banks[6 + u][:, 0:NM], cont[0:1, u, :], carry[0:1, 1 - u, 0:NM], start=False, stop=True).then_inc(a_agg.sem, 1)
                        for u in range(2):
                            pe.wait_ge(a_ag.sem, a_ag.now(i, u))
                            pe.transpose(banks[u][:, 256:384], ag[:, u, :], ident[:, :]).then_inc(a_agt.sem, 1)
                        for u in range(2):
                            pe.wait_ge(a_agT.sem, a_agT.now(i, u))
                            pe.wait_ge(a_qkv.sem, a_qkv.now(i, u))
                            pe.matmul(banks[2 + u][:, 256:384], agT[:, u, :], w_o[:, l, :], start=True, stop=True).then_inc(a_wo.sem, 1)
                        for u in range(2):
                            pe.wait_ge(ln_set.sem, ln_set.now(i, u))
                            pe.transpose(banks[u][:, 384:512], yln[:, u, :], ident[:, :]).then_inc(a_t2.sem, 1)
                        for u in range(2):
                            pe.wait_ge(a_t2s.sem, a_t2s.now(i, u))
                            for j in range(FJ):
                                last = pe.matmul(banks[4 + u][:, j * D:(j + 1) * D], w_up[:, l, j * D:(j + 1) * D], yT[:, u, :], start=True, stop=True)
                            last.then_inc(up_done.sem, 1)
                        for u in range(2):
                            pe.wait_ge(g_last.sem, g_last.now(i, u))
                            pe.wait_ge(y_set.sem, y_set.old(i, u))
                            for j in range(FJ):
                                last = pe.matmul(banks[6 + u][:, 384:512], hE[:, u, j, :], w_down[:, l, j, :], start=(j == 0), stop=(j == FJ - 1))
                            last.then_inc(mm_done.sem, 1)

                @block.scalar
                def _(act):
                    with pairs(act, ET) as i:
                        for u in range(2):
                            act.wait_ge(a_T.sem, a_T.now(i, u))
                            act.wait_ge(a_mm.sem, a_mm.old(i, u))
                            act.copy(xpT[:, u].rearrange("p e d -> p (e d)"), banks[u][:, 0:2 * D]).then_inc(a_xT.sem, 1)
                        for u in range(2):
                            act.wait_ge(a_att.sem, a_att.now(i, u))
                            act.wait_ge(a_am.sem, a_am.old(i, u))
                            act.activation(exa[:, u, :, :], att3[:, u, :, :], ACT.Exp).then_inc(a_exp.sem, 1)
                        for u in range(2):
                            act.wait_ge(a_agg.sem, a_agg.now(i, u))
                            act.copy(carry[0:1, u, 0:NM], banks[6 + u][0:1, NM:2 * NM]).then_inc(carry_set.sem, 1)
                        for u in range(2):
                            act.wait_ge(a_agt.sem, a_agt.now(i, u))
                            act.wait_ge(a_wo.sem, a_wo.old(i, u))
                            act.copy(agT[:, u, :], banks[u][:, 256:384]).then_inc(a_agT.sem, 1)
                        for u in range(2):
                            act.wait_ge(a_t2.sem, a_t2.now(i, u))
                            act.wait_ge(up_done.sem, up_done.old(i, u))
                            act.copy(yT[:, u, :], banks[u][:, 384:512]).then_inc(a_t2s.sem, 1)
                        for u in range(2):
                            act.wait_ge(up_done.sem, up_done.now(i, u))
                            act.wait_ge(mm_done.sem, mm_done.old(i, u))
                            for j in range(FJ):
                                last = act.activation(hE[:, u, j, :], banks[4 + u][:, j * D:(j + 1) * D], ACT.Gelu, bias=b_up[:, l, j:j + 1])
                            last.then_inc(g_last.sem, 1)
            end_phase(ET)

        ers2 = sb("ers2", [D, 2, 2])
        att3 = sb("att3", [D, 2, 2, H])
        yln, yT = sb("yln", [D, 2, D]), sb("yT", [D, 2, D])
        fst, fag, fv, frs = sb("fst", [D, 2, 6]), sb("fag", [D, 2, 2]), sb("fv", [D, 2, 1]), sb("frs", [D, 2, 1])
        names = ("add_set", "att_sum", "att_min", "rden_set", "xo_set", "g_last", "up_done", "f_sum", "f_bn", "f_st", "f_v", "f_rs", "f_ln")
        (add_set, att_sum, att_min, rden_set, xo_set, g_last, up_done, f_sum, f_bn, f_st, f_v, f_rs, f_ln) = map(edge_signal, names)
        start_signals()
        with nc.Block() as block:
            @block.vector
            def _(dve):
                dve.memset(carry[:, :, :], 0.0)
                dve.drain()
        attention_round(0)
        attention_round(1)

        def root(l):
            return w_rel[:, l, :], w_root[:, l, :], rel_row[:, l, :]
        mean_round(T5, *root(0), T6, elu=True, norm=False)
        mean_round(T6, *root(1), T7, elu=True, norm=False)
        mean_round(T7, *root(2), T8, elu=True, norm=False)
        mean_round(T8, *root(3), None, elu=True, norm=True, residual="t5", final=True)


_INS = ['x',
        'src',
        'dst',
        'edge_attr_9',
        'L0_gnn_W1_l',
        'L0_gnn_b1',
        'L0_gnn_W1_r',
        'L0_gnn_W2_l',
        'L0_gnn_b2',
        'L0_gnn_W2_r',
        'L1_gnn_w0',
        'L1_gnn_w1',
        'L1_gnn_w2',
        'L1_gnn_w3',
        'L1_gnn_w4',
        'L2_gnn_Wq',
        'L2_gnn_bq',
        'L2_gnn_Wk',
        'L2_gnn_bk',
        'L2_gnn_Wv',
        'L2_gnn_bv',
        'L2_gnn_Wo',
        'L2_gnn_bo',
        'L2_gnn_Wpos',
        'L2_gnn_bpos',
        'L2_gnn_Wdeg',
        'L2_gnn_bdeg',
        'L2_gnn_ln1_g',
        'L2_gnn_ln1_b',
        'L2_gnn_ln2_g',
        'L2_gnn_ln2_b',
        'L2_gnn_W1',
        'L2_gnn_b1',
        'L2_gnn_W2',
        'L2_gnn_b2',
        'L3_gnn_Ws_rel',
        'L3_gnn_bs_rel',
        'L3_gnn_Ws_root']


def kernel(**inputs):
    import numpy as _np
    import concourse.bacc as _bacc
    from concourse import mybir as _mybir
    from concourse.bass_utils import run_bass_kernel_spmd as _run

    nc = _bacc.Bacc("TRN2", target_bir_lowering=False, num_devices=1)
    arrays, tensors = {}, {}
    for name in _INS:
        a = _np.ascontiguousarray(inputs[name])
        arrays[f"in_{name}_dram"] = a
        tensors[name] = nc.dram_tensor(f"in_{name}_dram", a.shape, _mybir.dt.from_np(a.dtype), kind="ExternalInput").ap()
    shape = list(inputs["x"].shape)
    tensors["out"] = nc.dram_tensor("out_0_dram", shape, _mybir.dt.from_np(_np.dtype("float32")), kind="ExternalOutput").ap()
    gnn_stack(nc, tensors)
    r = _run(nc, [arrays], core_ids=[0])
    return r.results[0]["out_0_dram"]
```

```python
import concourse.bass as bass
from concourse import mybir
from contextlib import ExitStack, contextmanager
from math import factorial, sqrt
import numpy as np

F32 = mybir.dt.float32
BF16 = mybir.dt.bfloat16
I32 = mybir.dt.int32
ALU = mybir.AluOpType
ACT = mybir.ActivationFunctionType
AX = mybir.AxisListType

D = 128
TPC = 4
CH = TPC * D
H, HD = 8, 16
FF = 512
FJ = FF // D
MUL = 32
EPS = 1e-5
STD_EPS = 1e-6
ATT_CLIP = 50.0
ea_n = 9


def wigner_3j(l1, l2, l3):
    def f(n):
        return factorial(round(n))

    def cg(j1, m1, j2, m2, j3, m3):
        if m3 != m1 + m2:
            return 0.0
        vmin = int(max(-j1 + j2 + m3, -j1 + m1, 0))
        vmax = int(min(j2 + j3 + m1, j3 - j1 + j2, j3 + m3))
        c = ((2.0 * j3 + 1.0) * f(j3 + j1 - j2) * f(j3 - j1 + j2) * f(j1 + j2 - j3) * f(j3 + m3) * f(j3 - m3)
             / (f(j1 + j2 + j3 + 1) * f(j1 - m1) * f(j1 + m1) * f(j2 - m2) * f(j2 + m2))) ** 0.5
        s = 0
        for v in range(vmin, vmax + 1):
            s += (-1) ** (v + j2 + m2) * f(j2 + j3 + m1 - v) * f(j1 - m1 + v) / (
                f(v) * f(j3 - j1 + j2 - v) * f(j3 + m3 - v) * f(v + j1 - j2 - m3))
        return float(c * s)

    def basis(l):
        q = np.zeros((2 * l + 1, 2 * l + 1), dtype=np.complex128)
        for m in range(-l, 0):
            q[l + m, l + abs(m)] = 1 / np.sqrt(2)
            q[l + m, l - abs(m)] = -1j / np.sqrt(2)
        q[l, l] = 1
        for m in range(1, l + 1):
            q[l + m, l + abs(m)] = (-1) ** m / np.sqrt(2)
            q[l + m, l - abs(m)] = 1j * (-1) ** m / np.sqrt(2)
        return (-1j) ** l * q

    c = np.zeros((2 * l1 + 1, 2 * l2 + 1, 2 * l3 + 1))
    for m1 in range(-l1, l1 + 1):
        for m2 in range(-l2, l2 + 1):
            if abs(m1 + m2) <= l3:
                c[l1 + m1, l2 + m2, l3 + m1 + m2] = cg(l1, m1, l2, m2, l3, m1 + m2)
    out = np.real(np.einsum("ij,kl,mn,ikn->jlm", basis(l1), basis(l2), np.conj(basis(l3).T),
                            c.astype(np.complex128)))
    return out / np.linalg.norm(out)


@contextmanager
def pairs(eng, steps):
    with eng.Fori(0, steps // 2) as j:
        yield j * 2


def skewed(eng, steps, step):
    step(-2, True, False)
    with eng.Fori(0, steps // 2 - 1) as j:
        step(j * 2, True, True)
    step(steps - 2, False, True)


def skewed3(eng, steps, step):
    step(-4, True, False, False)
    step(-2, True, True, False)
    with eng.Fori(0, steps // 2 - 2) as j:
        step(j * 2, True, True, True)
    step(steps - 4, False, True, True)
    step(steps - 2, False, False, True)


def skewed5(eng, steps, step):
    for i in (-8, -6, -4, -2):
        step(i, *[i + 8 - 2 * k >= 0 for k in range(5)])
    with eng.Fori(0, steps // 2 - 4) as j:
        step(j * 2, True, True, True, True, True)
    for i in (steps - 8, steps - 6, steps - 4, steps - 2):
        step(i, *[i + 8 - 2 * k < steps for k in range(5)])


def gnn_stack(nc, t):
    N = t["x"].shape[0]
    E = t["src"].shape[0]
    CN = -(-N // CH)
    NP = CN * CH
    ET = -(-E // D)
    EP = ET * D
    TAIL_P = (N - (CN - 1) * CH) // TPC
    TAIL_E = E - (ET - 1) * D
    HC = CN * TPC
    assert N % TPC == 0 and N < NP and E < EP and ET % 2 == 0 and CN % 2 == 0 and CN >= 10 and ET >= 10 and HC <= 512

    ctx = ExitStack()
    with ctx:
        def sb(name, shape, dt=F32):
            return ctx.enter_context(nc.sbuf_tensor("sb_" + name, shape, dt))

        def sem(name):
            return ctx.enter_context(nc.semaphore(name))

        def dram(name, rows, cols, dt=F32):
            return nc.dram_tensor("scratch_" + name, [rows, cols], dt).ap()

        XD0 = dram("x_of_targets", EP, D)
        T1, T2, T3, T4, T5, T6, T7, T8 = [dram(f"table{n}", NP + EP, D) for n in range(1, 9)]
        INFO = dram("node_info", NP, 4)

        bank = [ctx.enter_context(nc.psum_tensor(f"bank{n}", [D, 512], F32)) for n in range(8)]
        banks = [b[:, :] for b in bank]

        ident = sb("ident", [D, D])
        ones = sb("ones", [D, D])
        dst_all = sb("dst_all", [D, EP + 1])
        dst_col = sb("dst_col", [D, ET])
        x_src = sb("x_src", [D, ET], I32)
        x_dst = sb("x_dst", [D, ET], I32)
        g_dst0 = sb("g_dst0", [D, ET], I32)
        g_src = sb("g_src", [D, ET], I32)
        g_dst = sb("g_dst", [D, ET], I32)
        put_row = sb("put_row", [D, ET], I32)
        inv_in = sb("inv_in", [D, ET])
        deg_src = sb("deg_src", [D, ET])
        deg_dst = sb("deg_dst", [D, ET])
        deg_node = sb("deg_node", [D, HC])
        ea = sb("ea", [D, ET, ea_n])
        coef = sb("coef", [D, ET, 3, 3])
        minus_half = sb("minus_half", [D, 8])
        cnt = sb("cnt", [D, ET])
        seg = sb("seg", [D, 2, D])
        cont = sb("cont", [1, 2, D])
        idx2 = sb("idx2", [D, 2, 2], I32)
        carry = sb("carry", [1, 2, 3 * D])
        W = {}
        for n in ("L0_gnn_W1_l", "L0_gnn_W1_r", "L0_gnn_W2_l", "L0_gnn_W2_r"):
            W[n] = sb("w_" + n, [D, D])
        w_rel = sb("w_rel", [D, 4, D])
        w_root = sb("w_root", [D, 4, D])
        b1_col, b2_col = sb("b1_col", [D, 1]), sb("b2_col", [D, 1])
        b1_row, b2_row = sb("b1_row", [D, D]), sb("b2_row", [D, D])
        rel_col, rel_row = sb("rel_col", [D, 4]), sb("rel_row", [D, 4, D])
        tp0, tp1 = sb("tp0", [2 * MUL, MUL]), sb("tp1", [3 * MUL, MUL])
        w_qkv = sb("w_qkv", [D, 2, 3 * D])
        c_qkv = sb("c_qkv", [D, 2, 3 * D])
        u_qkv = sb("u_qkv", [D, 2, 3 * D])
        w_o = sb("w_o", [D, 2, D])
        bo_row = sb("bo_row", [D, 2, D])
        w_vo = sb("w_vo", [D, 2, D])
        c_vo = sb("c_vo", [D, 2, D])
        u_vo = sb("u_vo", [D, 2, D])
        w_up = sb("w_up", [D, 2, FF])
        b_up = sb("b_up", [D, 2, FJ])
        w_down = sb("w_down", [D, 2, FJ, D])
        b_down = sb("b_down", [D, 2, D])

        s_tmp = sem("setup_done")
        s_ld = sem("setup_loaded")
        s_ldc = sem("setup_cast_loaded")
        s_pre = sem("setup_pool")

        class Chain:
            def __init__(self, name):
                self.sem, self.n = sem(name), 0

            def __call__(self, eng, ins):
                self.n += 1
                ins.then_inc(self.sem, 1)
                eng.wait_ge(self.sem, self.n)

        signals, started = [], []

        class Signal:
            def __init__(self, name):
                self.raw, self.n, self.touched = sem(name), 0, False
                signals.append(self)

            @property
            def sem(self):
                self.touched = True
                return self.raw

            def now(self, i, u):
                return i + (self.n + u + 3)

            def last(self, i, u):
                return i + (self.n + u + 2)

            def old(self, i, u):
                return i + (self.n + u + 1)

        class Transfer:
            def __init__(self, name, start=1):
                self.start = start
                self.raw, self.n, self.touched = [sem(name + "_0"), sem(name + "_1")], 0, False
                signals.append(self)

            @property
            def sem(self):
                self.touched = True
                return self.raw

            def now(self, i):
                return i * 8 + (self.n * 8 + self.start + 16)

            def old(self, i):
                return i * 8 + (self.n * 8 + self.start)

            def end(self, steps):
                return 8 * (self.n + steps) + self.start

        def start_signals():
            with nc.Block() as block:
                @block.vector
                def _(dve):
                    for s in signals[len(started):]:
                        if isinstance(s, Signal):
                            dve.sem_inc(s.raw, 2)
                        elif s.start == 1:
                            dve.sem_inc(s.raw[0], 1)
                            dve.sem_inc(s.raw[1], 1)
                        started.append(s)

        def end_phase(steps):
            for s in signals:
                if s.touched:
                    s.n, s.touched = s.n + steps, False

        setup = ExitStack()

        def tmp(name, shape, dt=F32):
            return setup.enter_context(nc.sbuf_tensor("sb_" + name, shape, dt))

        stage = tmp("stage", [D, 6, D])
        lay = tmp("lay", [ET, 3, D])
        wpos = tmp("wpos", [D, 2, D])
        wqkv_raw = tmp("wqkv_raw", [D, 2, 3 * D])
        cols = tmp("cols", [D, 2, 8])
        bqkv = tmp("bqkv", [D, 2, 3 * D])
        aposT = tmp("aposT", [D, D])
        m1 = tmp("m1", [D, 3 * D])
        spread = tmp("spread", [D, 3, D])
        b_up_raw = tmp("b_up_raw", [D, 2, FJ])
        n_ld = [0]
        s_ea, s_pad = sem("ea_cleared"), sem("pads_set")

        def row_bc(v):
            return v.rearrange("(a n) -> a n", a=1).broadcast_to([D, v.shape[0]])

        def col_of(v):
            return v.rearrange("(n a) -> n a", a=1)

        with nc.Block() as block:
            @block.sync
            def _(sp):
                def ld(out, in_):
                    sp.dma_start(out, in_).then_inc(s_ld, 16)
                    n_ld[0] += 16
                for n in ("L0_gnn_W1_l", "L0_gnn_W1_r", "L0_gnn_W2_l", "L0_gnn_W2_r"):
                    ld(W[n][:, :], t[n])
                ld(b1_col[:, :], col_of(t["L0_gnn_b1"]))
                ld(b2_col[:, :], col_of(t["L0_gnn_b2"]))
                ld(b1_row[:, :], row_bc(t["L0_gnn_b1"]))
                ld(b2_row[:, :], row_bc(t["L0_gnn_b2"]))
                ld(w_rel[:, :, :], t["L3_gnn_Ws_rel"].rearrange("l a b -> a l b"))
                ld(w_root[:, :, :], t["L3_gnn_Ws_root"].rearrange("l a b -> a l b"))
                for l in range(4):
                    ld(rel_col[:, l:l + 1], col_of(t["L3_gnn_bs_rel"][l, :]))
                    ld(rel_row[:, l, :], row_bc(t["L3_gnn_bs_rel"][l, :]))
                for k, (tile, at) in enumerate([(tp0, 0), (tp1, 0), (tp1, MUL), (tp0, MUL), (tp1, 2 * MUL)]):
                    ld(tile[at:at + MUL, :], t[f"L1_gnn_w{k}"].rearrange("u a w -> u (a w)"))
                for l in range(2):
                    ld(wpos[:, l, :], t["L2_gnn_Wpos"][l, :, :])
                    for j, n in enumerate("qkv"):
                        ld(wqkv_raw[:, l, j * D:(j + 1) * D], t[f"L2_gnn_W{n}"][l, :, :])
                        ld(bqkv[:, l, j * D:(j + 1) * D], row_bc(t[f"L2_gnn_b{n}"][l, :]))
                    for j, v in enumerate([t["L2_gnn_ln1_g"][l, :], t["L2_gnn_ln1_b"][l, :], t["L2_gnn_bpos"][l, :],
                                           t["L2_gnn_bdeg"][l, :], t["L2_gnn_Wdeg"][l, 0, :],
                                           t["L2_gnn_ln2_g"][l, :], t["L2_gnn_ln2_b"][l, :]]):
                        ld(cols[:, l, j:j + 1], col_of(v))
                    ld(w_o[:, l, :], t["L2_gnn_Wo"][l, :, :])
                    ld(bo_row[:, l, :], row_bc(t["L2_gnn_bo"][l, :]))
                    ld(w_up[:, l, :], t["L2_gnn_W1"][l, :, :])
                    ld(w_down[:, l, :, :], t["L2_gnn_W2"][l, :, :].rearrange("(j p) n -> p j n", p=D))
                    for j in range(FJ):
                        ld(b_up_raw[:, l, j:j + 1], col_of(t["L2_gnn_b1"][l, j * D:(j + 1) * D]))
                    ld(b_down[:, l, :], row_bc(t["L2_gnn_b2"][l, :]))
                sp.wait_ge(s_ea, 1)
                ld(ea[:, 0:ET - 1, :], t["edge_attr_9"][0:(ET - 1) * D, :].rearrange("(s p) c -> p s c", p=D))
                ld(ea[0:TAIL_E, ET - 1, :], t["edge_attr_9"][(ET - 1) * D:E, :])
                sp.wait_ge(s_ld, n_ld[0])

            @block.gpsimd
            def _(pool):
                ch = Chain("setup_pool_chain")
                pool.memset(ident[:, :], 0.0).then_inc(s_pre, 1)
                pool.wait_ge(s_pre, 1)
                pool.affine_select(out=ident[:, :], in_=ident[:, :], compare_op=ALU.not_equal, fill=1.0,
                                   base=0, pattern=[[-1, D]], channel_multiplier=1).then_inc(s_pre, 1)
                pool.memset(ones[:, :], 1.0).then_inc(s_pre, 1)
                pool.memset(minus_half[:, :], -0.5).then_inc(s_pre, 1)
                pool.wait_ge(s_pad, 1)
                n = 0
                for j, (v, o) in enumerate([(t["src"], 0), (t["dst"], 0), (t["dst"], 1)]):
                    full = (ET - 1) * D
                    pool.dma_start(lay[0:ET - 1, j, :], v[o:o + full].rearrange("(s p) -> s p", p=D)).then_inc(s_ldc, 16)
                    pool.dma_start(lay[ET - 1:ET, j, 0:TAIL_E - o],
                                   v[full + o:E].rearrange("(s p) -> s p", s=1)).then_inc(s_ldc, 16)
                    n += 32
                pool.dma_start(dst_all[:, 1:1 + E], row_bc(t["dst"])).then_inc(s_ldc, 16)
                pool.wait_ge(s_ldc, n + 16)

            @block.vector
            def _(dve):
                dve.memset(ea[:, ET - 1, :], 0.0).then_inc(s_ea, 1)
                dve.memset(lay[:, 0, :], float(NP))
                dve.memset(lay[:, 1, :], float(NP - 1))
                dve.memset(lay[:, 2, :], float(NP - 1))
                dve.memset(dst_all[:, 0:1], -1.0)
                dve.memset(dst_all[:, 1 + E:], float(NP - 1)).then_inc(s_pad, 1)

        s1, s2, s3, s4 = sem("su_pe"), sem("su_dve"), sem("su_act"), sem("su_pool2")
        srcf = tmp("srcf", [D, ET])
        nxtf = tmp("nxtf", [D, ET])
        lo_f, hi_f = tmp("lo_f", [D, ET]), tmp("hi_f", [D, ET])
        wi = tmp("wi", [D, 3, ET], I32)
        wf = tmp("wf", [D, 3, ET])
        iota_lo, iota_hi = tmp("iota_lo", [D, D]), tmp("iota_hi", [D, HC])
        w121 = wigner_3j(1, 2, 1)

        with nc.Block() as block:
            @block.gpsimd
            def _(pool):
                pool.iota(iota_lo[:, :], [[1, D]], base=0, channel_multiplier=0,
                          allow_small_or_imprecise_dtypes=True)
                pool.iota(iota_hi[:, :], [[1, HC]], base=0, channel_multiplier=0,
                          allow_small_or_imprecise_dtypes=True)

            @block.tensor
            def _(pe):
                ch = [0]

                def done(ins):
                    ch[0] += 1
                    ins.then_inc(s1, 1)
                for j in range(3):
                    last = pe.transpose(banks[0][:, j * ET:(j + 1) * ET], lay[:, j, :], ident[0:ET, 0:ET])
                done(last)
                for l in range(2):
                    v = 8 * l
                    pe.wait_ge(s2, v + 1)
                    done(pe.transpose(banks[1][:, 0:D], stage[:, 0, :], ident[:, :]))
                    pe.wait_ge(s2, v + 2)
                    done(pe.matmul(banks[2][:, 0:3 * D], aposT[:, :], wqkv_raw[:, l, :], start=True, stop=True))
                    pe.wait_ge(s2, v + 3)
                    pe.matmul(banks[3][:, 0:3 * D], spread[:, 0, :], m1[:, :], start=True, stop=False)
                    done(pe.matmul(banks[3][:, 0:3 * D], spread[:, 1, :], wqkv_raw[:, l, :], start=False, stop=True))
                    done(pe.matmul(banks[4][:, 0:3 * D], spread[:, 2, :], wqkv_raw[:, l, :], start=True, stop=True))
                    pe.wait_ge(s2, v + 4)
                    for j, src_ in enumerate([w_qkv[:, l, 2 * D:3 * D], c_qkv[:, l, 2 * D:3 * D], u_qkv[:, l, 2 * D:3 * D]]):
                        last = pe.transpose(banks[5][:, j * D:(j + 1) * D], src_, ident[:, :])
                    done(last)
                    pe.wait_ge(s2, v + 5)
                    for j in range(3):
                        last = pe.matmul(banks[6][:, j * D:(j + 1) * D], stage[:, 1 + j, :], w_o[:, l, :], start=True, stop=True)
                    done(last)
                    for j in range(FJ):
                        last = pe.matmul(banks[7][:, j:j + 1], w_up[:, l, j * D:(j + 1) * D], cols[:, l, 6:7], start=True, stop=True)
                    done(last)

            @block.vector
            def _(dve):
                ch = Chain("su_dve_chain")

                def go(ins):
                    ch(dve, ins)
                dve.wait_ge(s1, 1)
                go(dve.tensor_copy(srcf[:, :], banks[0][:, 0:ET]))
                go(dve.tensor_copy(dst_col[:, :], banks[0][:, ET:2 * ET]))
                go(dve.tensor_copy(nxtf[:, :], banks[0][:, 2 * ET:3 * ET]))
                go(dve.tensor_scalar(x_src[:, :], srcf[:, :], float(N - 1), None, ALU.min))
                go(dve.tensor_scalar(x_dst[:, :], dst_col[:, :], float(N - 1), None, ALU.min))
                go(dve.tensor_copy(g_dst0[:, :], dst_col[:, :]))
                go(dve.tensor_tensor(wf[:, 0, :], dst_col[:, :], nxtf[:, :], ALU.is_equal))
                go(dve.tensor_scalar(wf[:, 1, :], wf[:, 0, :], float(2 * NP), None, ALU.mult))
                go(dve.tensor_tensor(put_row[:, :], wf[:, 1, :], dst_col[:, :], ALU.add))
                go(dve.tensor_copy(wi[:, 0, :], srcf[:, :]))
                go(dve.tensor_scalar(wi[:, 1, :], wi[:, 0, :], 2, 127, ALU.logical_shift_right, ALU.bitwise_and))
                go(dve.tensor_copy(lo_f[:, :], wi[:, 1, :]))
                go(dve.tensor_scalar(wi[:, 1, :], wi[:, 0, :], 9, 2, ALU.logical_shift_right, ALU.logical_shift_left))
                go(dve.tensor_copy(wf[:, 0, :], wi[:, 1, :]))
                go(dve.tensor_scalar(wi[:, 2, :], wi[:, 0, :], 3, None, ALU.bitwise_and))
                go(dve.tensor_copy(wf[:, 1, :], wi[:, 2, :]))
                go(dve.tensor_tensor(hi_f[:, :], wf[:, 0, :], wf[:, 1, :], ALU.add))
                for k in range(3):
                    for i in range(3):
                        first = True
                        for j in range(5):
                            c = float(w121[i, j, k])
                            if abs(c) < 1e-12:
                                continue
                            if first:
                                go(dve.tensor_scalar(coef[:, :, k, i], ea[:, :, 4 + j], c, None, ALU.mult))
                            else:
                                go(dve.scalar_tensor_tensor(coef[:, :, k, i], ea[:, :, 4 + j], c, coef[:, :, k, i],
                                                            ALU.mult, ALU.add))
                            first = False
                        if first:
                            go(dve.memset(coef[:, :, k, i], 0.0))
                fan0, fan1, nb = 2 * MUL, 3 * MUL, sqrt(10.0)
                n0, n1 = sqrt(1.0 / fan0) / nb, sqrt(3.0 / fan1) / nb
                r3 = 1.0 / sqrt(3.0)
                go(dve.tensor_scalar(tp0[0:MUL, :], tp0[0:MUL, :], n0, None, ALU.mult))
                go(dve.tensor_scalar(tp0[MUL:2 * MUL, :], tp0[MUL:2 * MUL, :], n0 * r3, None, ALU.mult))
                go(dve.tensor_scalar(tp1[0:MUL, :], tp1[0:MUL, :], n1 * r3, None, ALU.mult))
                go(dve.tensor_scalar(tp1[MUL:2 * MUL, :], tp1[MUL:2 * MUL, :], n1 * r3, None, ALU.mult))
                go(dve.tensor_scalar(tp1[2 * MUL:3 * MUL, :], tp1[2 * MUL:3 * MUL, :], n1, None, ALU.mult))
                for l in range(2):
                    p = 1 + 7 * l
                    go(dve.tensor_tensor(stage[:, 0, :], wpos[:, l, :], ident[:, :], ALU.add))
                    dve.sem_inc(s2, 1)
                    dve.wait_ge(s1, p + 1)
                    go(dve.tensor_copy(aposT[:, :], banks[1][:, 0:D]))
                    dve.sem_inc(s2, 1)
                    dve.wait_ge(s1, p + 2)
                    go(dve.tensor_copy(m1[:, :], banks[2][:, 0:3 * D]))
                    go(dve.tensor_scalar(w_qkv[:, l, :], m1[:, :], cols[:, l, 0:1], None, ALU.mult))
                    go(dve.tensor_scalar(spread[:, 0, :], ones[:, :], cols[:, l, 1:2], None, ALU.mult))
                    go(dve.tensor_scalar(spread[:, 1, :], ones[:, :], cols[:, l, 2:3], cols[:, l, 3:4], ALU.mult, ALU.add))
                    go(dve.tensor_scalar(spread[:, 2, :], ones[:, :], cols[:, l, 4:5], None, ALU.mult))
                    dve.sem_inc(s2, 1)
                    dve.wait_ge(s1, p + 4)
                    go(dve.tensor_tensor(c_qkv[:, l, :], banks[3][:, 0:3 * D], bqkv[:, l, :], ALU.add))
                    go(dve.tensor_copy(u_qkv[:, l, :], banks[4][:, 0:3 * D]))
                    dve.sem_inc(s2, 1)
                    dve.wait_ge(s1, p + 5)
                    go(dve.tensor_copy(stage[:, 1:4, :], banks[5][:, 0:3 * D].rearrange("p (j d) -> p j d", j=3)))
                    dve.sem_inc(s2, 1)
                    dve.wait_ge(s1, p + 6)
                    go(dve.tensor_copy(w_vo[:, l, :], banks[6][:, 0:D]))
                    go(dve.tensor_tensor(c_vo[:, l, :], banks[6][:, D:2 * D], bo_row[:, l, :], ALU.add))
                    go(dve.tensor_copy(u_vo[:, l, :], banks[6][:, 2 * D:3 * D]))
                    dve.wait_ge(s1, p + 7)
                    go(dve.tensor_tensor(b_up[:, l, :], banks[7][:, 0:FJ], b_up_raw[:, l, :], ALU.add))
                    go(dve.tensor_scalar(w_up[:, l, :], w_up[:, l, :], cols[:, l, 5:6], None, ALU.mult))
                    dve.sem_inc(s2, 3)

        deg_seg, deg_pe = Signal("deg_seg"), Signal("deg_pe")
        deg_carry, deg_cnt = Signal("deg_carry"), Signal("deg_cnt")
        idx_set = [Signal("src_rows_set"), Signal("dst_rows_set")]

        def edge_signal(name):
            return Signal("edge_" + name)
        seg_set, agg_done, carry_set, at_set, mm_done = map(
            edge_signal, ("seg_set", "agg_done", "carry_set", "at_set", "mm_done"))
        z_set, e_set, c_set, y_set = map(edge_signal, ("z_set", "e_set", "c_set", "y_set"))
        st_set, v_set, rs_set, ln_set = map(edge_signal, ("st_set", "v_set", "rs_set", "ln_set"))
        row_set = edge_signal("row_set")
        got_src, got_dst = Transfer("edge_got_src", 0), Transfer("edge_got_dst", 0)
        put_rows = Transfer("edge_put_rows", 16)
        got_own, got_res, put_out, put_x = [Transfer("edge_" + x) for x in ("got_own", "got_res", "put_out", "put_x")]

        def p_wait(pool, s, v):
            pool.wait_ge(s, v)
            pool.nop(nofuse=True)

        def gather(pool, i, u, out, table, rows, j, free):
            p_wait(pool, *free)
            pool.tensor_copy(idx2[:, u, j:j + 1], rows[:, bass.ds(i + u, 1)]).then_inc(idx_set[j].sem, 1)
            p_wait(pool, idx_set[j].sem, idx_set[j].now(i, u))
            return pool.indirect_dma_start(
                out, None, table, bass.IndirectOffsetOnAxis(ap=idx2[:, u, j:j + 1], axis=0))

        def same_target(dve, i, u, scale):
            at = (i + u) * D
            if scale:
                dve.tensor_scalar(seg[:, u, :], dst_all[:, bass.ds(at + 1, D)], dst_col[:, bass.ds(i + u, 1)],
                                  inv_in[:, bass.ds(i + u, 1)], ALU.is_equal, ALU.mult)
            else:
                dve.tensor_scalar(seg[:, u, :], dst_all[:, bass.ds(at + 1, D)], dst_col[:, bass.ds(i + u, 1)],
                                  None, ALU.is_equal)
            return dve.tensor_scalar(cont[0:1, u, :], dst_all[0:1, bass.ds(at + 1, D)],
                                     dst_all[0:1, bass.ds(at, 1)], None, ALU.is_equal)

        one_lo = tmp("one_lo", [D, 2, D], BF16)
        one_hi = tmp("one_hi", [D, 2, HC], BF16)
        zero_b = tmp("zero_b", [D, max(HC, D)], BF16)
        carry_n = tmp("carry_n", [1, 2, 1])

        start_signals()
        with nc.Block() as block:
            @block.vector
            def _(dve):
                dve.memset(zero_b[:, :], 0.0)
                dve.memset(carry[:, :, :], 0.0)
                dve.memset(carry_n[:, :, :], 0.0)
                dve.drain()

        with nc.Block() as block:
            @block.vector
            def _(dve):
                with pairs(dve, ET) as i:
                    for u in range(2):
                        dve.wait_ge(deg_pe.sem, deg_pe.old(i, u))
                        same_target(dve, i, u, False)
                        dve.tensor_scalar(one_lo[:, u, :], iota_lo[:, :], lo_f[:, bass.ds(i + u, 1)], None, ALU.is_equal)
                        dve.tensor_scalar(one_hi[:, u, :], iota_hi[:, :], hi_f[:, bass.ds(i + u, 1)], None,
                                          ALU.is_equal).then_inc(deg_seg.sem, 1)

            @block.tensor
            def _(pe):
                hist = banks[4][:, 0:HC]
                pe.matmul(hist, zero_b[:, 0:D], zero_b[:, 0:HC], start=True, stop=False, skip_group_check=True)
                with pairs(pe, ET) as i:
                    for u in range(2):
                        pe.wait_ge(deg_seg.sem, deg_seg.now(i, u))
                        pe.wait_ge(deg_cnt.sem, deg_cnt.old(i, u))
                        pe.wait_ge(deg_carry.sem, deg_carry.last(i, u))
                        pe.matmul(hist, one_lo[:, u, :], one_hi[:, u, :], start=False, stop=False, skip_group_check=True)
                        pe.matmul(banks[u][:, 0:1], seg[:, u, :], ones[:, 0:1], start=True, stop=False)
                        pe.matmul(banks[u][:, 0:1], cont[0:1, u, :], carry_n[0:1, 1 - u, :], start=False, stop=True)
                        pe.matmul(banks[2 + u][0:1, 0:1], seg[:, u, D - 1:D], ones[:, 0:1], start=True, stop=False)
                        pe.matmul(banks[2 + u][0:1, 0:1], cont[0:1, u, D - 1:D], carry_n[0:1, 1 - u, :],
                                  start=False, stop=True).then_inc(deg_pe.sem, 1)
                pe.matmul(hist, zero_b[:, 0:D], zero_b[:, 0:HC], start=False, stop=True, skip_group_check=True)

            @block.scalar
            def _(act):
                with pairs(act, ET) as i:
                    for u in range(2):
                        act.wait_ge(deg_pe.sem, deg_pe.now(i, u))
                        act.copy(carry_n[0:1, u, :], banks[2 + u][0:1, 0:1]).then_inc(deg_carry.sem, 1)
                        act.copy(cnt[:, bass.ds(i + u, 1)], banks[u][:, 0:1]).then_inc(deg_cnt.sem, 1)
        end_phase(ET)

        sq, colsum = tmp("sq", [D, HC]), tmp("colsum", [D, 4])
        info = tmp("info", [D, CN, TPC, 4])
        info_d, info_s = tmp("info_d", [D, 2, 4]), tmp("info_s", [D, 2, 4])
        slot_row = tmp("slot_row", [D, ET])
        t1, t2, t3, t4 = sem("tab_sq"), sem("tab_total"), sem("tab_var"), sem("tab_info")
        t5, t6, t7 = sem("tab_std"), sem("tab_iota"), sem("tab_stored")
        mean_out = (E + N) / N
        primer = tmp("primer", [1, 2])
        half = tmp("half", [D, 1])
        with nc.Block() as block:
            @block.gpsimd
            def _(pool):
                for u in range(2):
                    pool.dma_start(primer[0:1, u:u + 1], t["x"][0:1, 0:1]).then_inc(put_rows.raw[u], 16)
                    pool.wait_ge(put_rows.raw[u], 16)
                pool.memset(half[:, :], 0.5)
                pool.iota(info[:, :, :, 0], [[CH, CN], [1, TPC]], base=0, channel_multiplier=TPC,
                          allow_small_or_imprecise_dtypes=True)
                pool.iota(slot_row[:, :], [[D, ET]], base=NP, channel_multiplier=1,
                          allow_small_or_imprecise_dtypes=True)
                pool.memset(info[:, :, :, 1], 1.0)
                pool.memset(info[:, :, :, 3], 0.0).then_inc(t6, 1)
                pool.wait_ge(t6, 1)
                pool.wait_ge(t3, 1)
                pool.tensor_tensor(colsum[:, 2:3], colsum[:, 1:2], half[:, :], ALU.pow).then_inc(t5, 1)

            @block.tensor
            def _(pe):
                pe.wait_ge(t1, 1)
                pe.matmul(banks[0][:, 0:1], ones[:, :], colsum[:, 0:1], start=True, stop=True).then_inc(t2, 1)

            @block.vector
            def _(dve):
                ch = Chain("tab_chain")

                def go(ins):
                    ch(dve, ins)
                go(dve.tensor_scalar(deg_node[:, :], banks[4][:, 0:HC], 1.0 - mean_out, None, ALU.add))
                go(dve.tensor_tensor(sq[:, :], deg_node[:, :], deg_node[:, :], ALU.mult))
                dve.tensor_reduce(colsum[:, 0:1], sq[:, :], AX.X, ALU.add).then_inc(t1, 1)
                dve.wait_ge(t2, 1)
                dve.tensor_scalar(colsum[:, 1:2], banks[0][:, 0:1], -(NP - N) * (1.0 - mean_out) ** 2, 1.0 / (N - 1),
                                  ALU.add, ALU.mult).then_inc(t3, 1)
                dve.wait_ge(t5, 1)
                go(dve.tensor_scalar(colsum[:, 0:1], colsum[:, 2:3], STD_EPS, None, ALU.add))
                go(dve.reciprocal(colsum[:, 3:4], colsum[:, 0:1]))
                go(dve.tensor_scalar(deg_node[:, :], deg_node[:, :], colsum[:, 3:4], None, ALU.mult))
                dve.wait_ge(t6, 1)
                dve.tensor_copy(info[:, :, :, 2], deg_node[:, :].rearrange("p (c t) -> p c t", t=TPC)).then_inc(t4, 1)

            @block.sync
            def _(sp):
                sp.wait_ge(t4, 1)
                sp.dma_start(INFO.rearrange("(c p t) f -> p c (t f)", p=D, t=TPC),
                             info[:, :, :, :].rearrange("p c t f -> p c (t f)")).then_inc(t7, 16)
                sp.wait_ge(t7, 16)

        new_info = tmp("new_info", [D, 2, 2])
        put2 = tmp("put2", [D, 2], I32)
        with nc.Block() as block:
            @block.vector
            def _(dve):
                with pairs(dve, ET) as i:
                    for u in range(2):
                        dve.wait_ge(put_rows.sem[u], put_rows.old(i))
                        dve.tensor_copy(new_info[:, u, 0:1], slot_row[:, bass.ds(i + u, 1)])
                        dve.tensor_copy(new_info[:, u, 1:2], cnt[:, bass.ds(i + u, 1)])
                        dve.tensor_scalar(put2[:, u:u + 1], put_row[:, bass.ds(i + u, 1)], 2.0, None, ALU.mult).then_inc(row_set.sem, 1)

            @block.gpsimd
            def _(pool):
                with pairs(pool, ET) as i:
                    for u in range(2):
                        p_wait(pool, row_set.sem, row_set.now(i, u))
                        pool.indirect_dma_start(INFO.rearrange("n (a b) -> (n a) b", b=2), bass.IndirectOffsetOnAxis(ap=put2[:, u:u + 1], axis=0),
                                                new_info[:, u, :], None, bounds_check=2 * NP - 1,
                                                oob_is_err=False).then_inc(put_rows.sem[u], 16)
                for u in range(2):
                    pool.wait_ge(put_rows.sem[u], put_rows.end(ET))
        end_phase(ET)
        with nc.Block() as block:
            @block.gpsimd
            def _(pool):
                with pairs(pool, ET) as i:
                    for u in range(2):
                        free = (row_set.sem, row_set.old(i, u))
                        gather(pool, i, u, info_s[:, u, :], INFO, x_src, 0, free).then_inc(got_src.sem[u], 16)
                        gather(pool, i, u, info_d[:, u, :], INFO, g_dst0, 1, free).then_inc(got_dst.sem[u], 16)

            @block.vector
            def _(dve):
                with pairs(dve, ET) as i:
                    for u in range(2):
                        dve.wait_ge(got_src.sem[u], got_src.now(i))
                        dve.wait_ge(got_dst.sem[u], got_dst.now(i))
                        dve.tensor_copy(g_src[:, bass.ds(i + u, 1)], info_s[:, u, 0:1])
                        dve.tensor_copy(deg_src[:, bass.ds(i + u, 1)], info_s[:, u, 2:3])
                        dve.tensor_copy(g_dst[:, bass.ds(i + u, 1)], info_d[:, u, 0:1])
                        dve.tensor_copy(deg_dst[:, bass.ds(i + u, 1)], info_d[:, u, 2:3])
                        dve.tensor_copy(cnt[:, bass.ds(i + u, 1)], info_d[:, u, 1:2]).then_inc(row_set.sem, 1)
                dve.wait_ge(row_set.sem, row_set.n + ET + 2)
                dve.reciprocal(inv_in[:, :], cnt[:, :])
        end_phase(ET)

        setup.close()

        nodes = ExitStack()

        def nsb(name, shape, dt=F32):
            return nodes.enter_context(nc.sbuf_tensor("sb_" + name, shape, dt))

        def node_signal(name):
            return Signal("node_" + name)
        n_pe = [node_signal(f"pe_{x}") for x in range(9)]
        n_act = [node_signal(f"act_{x}") for x in range(9)]
        n_dve = [node_signal(f"dve_{x}") for x in range(12)]
        n_pool = [node_signal(f"pool_{x}") for x in range(8)]
        n_in, n_in2 = Transfer("node_in"), Transfer("node_in2")
        n_out = [Transfer(f"node_out{x}") for x in range(4)]
        nb = [nsb(f"node_buf{x}", [D, 2, TPC, D]) for x in range(9)]
        yT = nsb("node_yT", [D, 2, TPC, D])
        nsum, nout = nsb("node_sum", [D, 2, TPC, D]), nsb("node_out", [D, 2, TPC, D])
        hT = nsb("hT", [D, 2, FJ, CH])
        nst = [nsb(f"node_stats{x}", [D, 2, TPC, 3]) for x in range(3)]
        nv = [nsb(f"node_var{x}", [D, 2, TPC]) for x in range(3)]
        nrs = [nsb(f"node_rstd{x}", [D, 2, TPC]) for x in range(3)]

        start_signals()

        def rows_of(table, c, tail=False):
            if tail:
                return table[(CN - 1) * CH:(CN - 1) * CH + TAIL_P * TPC, :].rearrange("(p t) d -> p t d", t=TPC)
            return table[bass.ds(c * CH, CH), :].rearrange("(p t) d -> p t d", t=TPC)

        def node_sync(sp, lag, loads, stores, late_loads, ragged_in, ragged_out):
            def load(which, c, u, tail=False):
                _, table, buf, tr, _ = which
                if tail and ragged_in:
                    sp.dma_start(buf[0:TAIL_P, u], rows_of(table, c, True)).then_inc(tr.sem[u], 16)
                else:
                    sp.dma_start(buf[:, u], rows_of(table, c)).then_inc(tr.sem[u], 16)

            def load_next(which, i, u, tail=False):
                for reader in which[4]:
                    sp.wait_ge(reader.sem, reader.now(i, u))
                load(which, i + (u + 2), u, tail)

            def store(which, i, u, tail=False):
                _, table, buf, tr, sig = which
                sp.wait_ge(sig.sem, sig.now(i, u))
                if tail and table is ragged_out:
                    sp.dma_start(rows_of(table, i + u, True), buf[0:TAIL_P, u]).then_inc(tr.sem[u], 16)
                else:
                    sp.dma_start(rows_of(table, i + u), buf[:, u]).then_inc(tr.sem[u], 16)

            def edge_step(i):
                for which in loads:
                    for u in range(2):
                        if 0 <= i + which[0] and i + which[0] + 2 < CN:
                            load_next(which, i + which[0], u, i + which[0] + 2 + u == CN - 1)
                for which in stores:
                    for u in range(2):
                        if 0 <= i + which[0] < CN:
                            store(which, i + which[0], u, i + which[0] + u == CN - 1)
                for which in late_loads:
                    for u in range(2):
                        if 0 <= i + which[0] and i + which[0] + 2 < CN:
                            load_next(which, i + which[0], u)

            for which in loads + late_loads:
                load(which, 0, 0)
                load(which, 1, 1)
            for i in range(-lag, 0, 2):
                edge_step(i)
            with pairs(sp, CN - 4 - lag) as i:
                for which in loads:
                    for u in range(2):
                        load_next(which, i + which[0], u)
                for which in stores:
                    for u in range(2):
                        store(which, i + which[0], u)
                for which in late_loads:
                    for u in range(2):
                        load_next(which, i + which[0], u)
            for i in range(CN - 4 - lag, CN, 2):
                edge_step(i)
            for _, _, _, tr, _ in stores:
                for u in range(2):
                    sp.wait_ge(tr.sem[u], tr.end(CN))

        def tiles_T(pe, out, src_, u):
            for k in range(TPC):
                last = pe.transpose(out[:, k * D:(k + 1) * D], src_(k), ident[:, :])
            return last

        def stats(dve, st, x, u):
            for q in range(TPC // 2):
                last = dve.bn_stats(st[:, u, 2 * q:2 * q + 2, :].rearrange("p e f -> p (e f)"),
                                    x[:, u, 2 * q:2 * q + 2, :].rearrange("p t d -> p d t"))
            return last

        def rstd(pool, i, u, st, v, r, ready, v_done, r_done):
            p_wait(pool, ready.sem, ready.now(i, u))
            pool.tensor_scalar(v[:, u, :], st[:, u, :, 2], 1.0 / D, EPS, ALU.mult, ALU.add).then_inc(v_done.sem, 1)
            p_wait(pool, v_done.sem, v_done.now(i, u))
            pool.tensor_tensor(r[:, u, :], v[:, u, :], minus_half[:, 0:TPC], ALU.pow).then_inc(r_done.sem, 1)

        def normalise(dve, out, x, st, r, u):
            for k in range(TPC):
                last = dve.tensor_scalar(out[:, u, k, :], x[:, u, k, :], st[:, u, k, 1:2], r[:, u, k:k + 1],
                                         ALU.subtract, ALU.mult)
            return last

        def flat(buf, u):
            return buf[:, u].rearrange("p t d -> p (t d)")

        with nc.Block() as block:
            @block.vector
            def _(dve):
                dve.memset(nb[0][:, :, :, :], 0.0)
                dve.memset(nb[8][:, :, :, :], 0.0)

        xin, xT, h1T, h1n, h2T, y, x1n, x2n = nb[0:8]
        with nc.Block() as block:
            @block.sync
            def _(sp):
                node_sync(sp, 0, [(0, t["x"], xin, n_in, (n_dve[0],))],
                          [(0, T1, h1n, n_out[0], n_act[3]), (0, T2, x1n, n_out[1], n_dve[2]),
                           (0, T3, x2n, n_out[2], n_pool[4])], [], True, None)

            @block.tensor
            def _(pe):
                with pairs(pe, CN) as i:
                    for u in range(2):
                        pe.wait_ge(n_in.sem[u], n_in.now(i))
                        pe.wait_ge(n_dve[0].sem, n_dve[0].old(i, u))
                        tiles_T(pe, banks[u], lambda k: xin[:, u, k, :], u).then_inc(n_pe[0].sem, 1)
                    for u in range(2):
                        pe.wait_ge(n_act[0].sem, n_act[0].now(i, u))
                        pe.wait_ge(n_act[1].sem, n_act[1].old(i, u))
                        pe.matmul(banks[2 + u], W["L0_gnn_W1_r"][:, :], flat(xT, u), start=True, stop=True).then_inc(n_pe[1].sem, 1)
                    for u in range(2):
                        pe.wait_ge(n_act[1].sem, n_act[1].now(i, u))
                        pe.wait_ge(n_act[2].sem, n_act[2].old(i, u))
                        pe.matmul(banks[6 + u], W["L0_gnn_W2_r"][:, :], flat(h1T, u), start=True, stop=True).then_inc(n_pe[2].sem, 1)
                        pe.wait_ge(n_act[3].sem, n_act[3].old(i, u))
                        tiles_T(pe, banks[4 + u], lambda k: h1T[:, u, k, :], u).then_inc(n_pe[3].sem, 1)
                    for u in range(2):
                        pe.wait_ge(n_act[2].sem, n_act[2].now(i, u))
                        tiles_T(pe, banks[u], lambda k: h2T[:, u, k, :], u).then_inc(n_pe[4].sem, 1)

            @block.scalar
            def _(act):
                with pairs(act, CN) as i:
                    for u in range(2):
                        act.wait_ge(n_pe[0].sem, n_pe[0].now(i, u))
                        act.wait_ge(n_pe[1].sem, n_pe[1].old(i, u))
                        act.copy(flat(xT, u), banks[u]).then_inc(n_act[0].sem, 1)
                    for u in range(2):
                        act.wait_ge(n_pe[1].sem, n_pe[1].now(i, u))
                        act.wait_ge(n_pe[3].sem, n_pe[3].old(i, u))
                        act.activation(flat(h1T, u), banks[2 + u], ACT.Relu, bias=b1_col[:, :]).then_inc(n_act[1].sem, 1)
                    for u in range(2):
                        act.wait_ge(n_pe[2].sem, n_pe[2].now(i, u))
                        act.wait_ge(n_pe[4].sem, n_pe[4].old(i, u))
                        act.activation(flat(h2T, u), banks[6 + u], ACT.Relu, bias=b2_col[:, :]).then_inc(n_act[2].sem, 1)
                    for u in range(2):
                        act.wait_ge(n_pe[3].sem, n_pe[3].now(i, u))
                        act.wait_ge(n_out[0].sem[u], n_out[0].old(i))
                        act.copy(flat(h1n, u), banks[4 + u]).then_inc(n_act[3].sem, 1)

            @block.vector
            def _(dve):
                with pairs(dve, CN) as i:
                    for u in range(2):
                        dve.wait_ge(n_pe[4].sem, n_pe[4].now(i, u))
                        dve.wait_ge(n_dve[2].sem, n_dve[2].old(i, u))
                        dve.tensor_tensor(flat(y, u), banks[u], flat(xin, u), ALU.add).then_inc(n_dve[0].sem, 1)
                    for u in range(2):
                        dve.wait_ge(n_dve[0].sem, n_dve[0].now(i, u))
                        dve.wait_ge(n_pool[6].sem, n_pool[6].old(i, u))
                        stats(dve, nst[0], y, u).then_inc(n_dve[1].sem, 1)
                    for u in range(2):
                        dve.wait_ge(n_pool[1].sem, n_pool[1].now(i, u))
                        dve.wait_ge(n_out[1].sem[u], n_out[1].old(i))
                        dve.wait_ge(n_pool[4].sem, n_pool[4].old(i, u))
                        normalise(dve, x1n, y, nst[0], nrs[0], u).then_inc(n_dve[2].sem, 1)

            @block.gpsimd
            def _(pool):
                with pairs(pool, CN) as i:
                    for u in range(2):
                        p_wait(pool, n_dve[2].sem, n_dve[2].old(i, u))
                        rstd(pool, i, u, nst[0], nv[0], nrs[0], n_dve[1], n_pool[0], n_pool[1])
                    for u in range(2):
                        p_wait(pool, n_pool[1].sem, n_pool[1].now(i, u))
                        pool.tensor_tensor(nv[1][:, u, :], nrs[0][:, u, :], nrs[0][:, u, :], ALU.mult).then_inc(n_pool[5].sem, 1)
                        p_wait(pool, n_pool[5].sem, n_pool[5].now(i, u))
                        pool.tensor_tensor(nv[2][:, u, :], nv[1][:, u, :], nst[0][:, u, :, 2], ALU.mult).then_inc(n_pool[6].sem, 1)
                        p_wait(pool, n_pool[6].sem, n_pool[6].now(i, u))
                        pool.tensor_scalar(nv[1][:, u, :], nv[2][:, u, :], 1.0 / D, EPS, ALU.mult, ALU.add).then_inc(n_pool[2].sem, 1)
                        p_wait(pool, n_pool[2].sem, n_pool[2].now(i, u))
                        pool.tensor_tensor(nrs[1][:, u, :], nv[1][:, u, :], minus_half[:, 0:TPC], ALU.pow).then_inc(n_pool[3].sem, 1)
                        p_wait(pool, n_pool[3].sem, n_pool[3].now(i, u))
                        p_wait(pool, n_dve[2].sem, n_dve[2].now(i, u))
                        p_wait(pool, n_out[2].sem[u], n_out[2].old(i))
                        for k in range(TPC):
                            last = pool.tensor_scalar(x2n[:, u, k, :], x1n[:, u, k, :], nrs[1][:, u, k:k + 1], None, ALU.mult)
                        last.then_inc(n_pool[4].sem, 1)
        end_phase(CN)

        def node_transformer(l):
            src_t, dst_t = (T3, T4) if l == 0 else (T4, T5)
            xin, xh, xhT, xc, tmp, yy, yb, zz, res = nb
            out_b = zz if l == 0 else nout
            with nc.Block() as block:
                @block.sync
                def _(sp):
                    node_sync(sp, 4, [(4, src_t, xin, n_in, (n_dve[1], n_pool[4]))],
                              [(0, dst_t, out_b, n_out[0], n_dve[11] if l else n_dve[7])],
                              [(0, T3, res, n_in2, (n_dve[8],))] if l else [], False, None)

                @block.tensor
                def _(pe):
                    def up(i, u):
                        for j in range(FJ):
                            if j < 2:
                                pe.wait_ge(n_act[5 + j].sem, n_act[5 + j].last(i, u))
                            else:
                                pe.wait_ge(n_act[1 + j].sem, n_act[1 + j].now(i, u))
                            pe.matmul(banks[4 + j % 2], w_up[:, l, j * D:(j + 1) * D], flat(yT, u), start=True,
                                      stop=True).then_inc(n_pe[4 + j].sem, 1)

                    def down(i, u):
                        pe.wait_ge(n_act[6].sem, n_act[6].now(i, u))
                        pe.wait_ge(n_dve[7].sem, n_dve[7].old(i, u))
                        for k in range(TPC):
                            for j in range(FJ):
                                last = pe.matmul(banks[6 + u][:, k * D:(k + 1) * D], hT[:, u, j, k * D:(k + 1) * D],
                                                 w_down[:, l, j, :], start=(j == 0), stop=(j == FJ - 1))
                        last.then_inc(n_pe[8].sem, 1)

                    def step(i, first, second, third):
                        f, s = i + 4, i + 2
                        if second:
                            pe.wait_ge(n_act[1].sem, n_act[1].now(s, 0))
                            up(s, 0)
                        if first:
                            for u in range(2):
                                pe.wait_ge(n_dve[1].sem, n_dve[1].now(f, u))
                                pe.wait_ge(n_act[1].sem, n_act[1].old(f, u))
                                tiles_T(pe, banks[u], lambda k: xh[:, u, k, :], u).then_inc(n_pe[0].sem, 1)
                        if second:
                            pe.wait_ge(n_act[1].sem, n_act[1].now(s, 1))
                            up(s, 1)
                        if first:
                            for u in range(2):
                                pe.wait_ge(n_act[0].sem, n_act[0].now(f, u))
                                pe.wait_ge(n_dve[6].sem, n_dve[6].old(f, u))
                                for k in range(TPC):
                                    last = pe.matmul(banks[2 + u][:, k * D:(k + 1) * D], xhT[:, u, k, :], w_vo[:, l, :], start=True, stop=True)
                                last.then_inc(n_pe[1].sem, 1)
                        if second:
                            down(s, 0)
                            down(s, 1)
                        if first:
                            for u in range(2):
                                pe.wait_ge(n_dve[5].sem, n_dve[5].now(f, u))
                                tiles_T(pe, banks[u], lambda k: xh[:, u, k, :], u).then_inc(n_pe[2].sem, 1)
                    skewed3(pe, CN, step)

                @block.scalar
                def _(act):
                    def hidden(i, u):
                        for j in range(FJ):
                            act.wait_ge(n_pe[4 + j].sem, n_pe[4 + j].now(i, u))
                            if j == 0:
                                act.wait_ge(n_pe[8].sem, n_pe[8].old(i, u))
                            act.activation(hT[:, u, j, :], banks[4 + j % 2], ACT.Gelu,
                                           bias=b_up[:, l, j:j + 1]).then_inc(n_act[3 + j].sem, 1)

                    def step(i, first, second, third):
                        f, s = i + 4, i + 2
                        if second:
                            hidden(s, 0)
                        if first:
                            for u in range(2):
                                act.wait_ge(n_pe[0].sem, n_pe[0].now(f, u))
                                act.wait_ge(n_pe[1].sem, n_pe[1].old(f, u))
                                act.copy(flat(xhT, u), banks[u]).then_inc(n_act[0].sem, 1)
                        if second:
                            hidden(s, 1)
                        if first:
                            for u in range(2):
                                act.wait_ge(n_pe[2].sem, n_pe[2].now(f, u))
                                act.wait_ge(n_pe[7].sem, n_pe[7].old(f, u))
                                act.copy(flat(yT, u), banks[u]).then_inc(n_act[1].sem, 1)
                    skewed3(act, CN, step)

                @block.vector
                def _(dve):
                    def step(i, first, second, third):
                        f = i + 4
                        if first:
                            for u in range(2):
                                dve.wait_ge(n_in.sem[u], n_in.now(f))
                                dve.wait_ge(n_dve[1].sem, n_dve[1].old(f, u))
                                stats(dve, nst[0], xin, u).then_inc(n_dve[0].sem, 1)
                            for u in range(2):
                                dve.wait_ge(n_pool[1].sem, n_pool[1].now(f, u))
                                dve.wait_ge(n_pe[2].sem, n_pe[2].old(f, u))
                                normalise(dve, xh, xin, nst[0], nrs[0], u).then_inc(n_dve[1].sem, 1)
                        if third:
                            for u in range(2):
                                dve.wait_ge(n_pe[8].sem, n_pe[8].now(i, u))
                                dve.wait_ge(n_pool[5].sem, n_pool[5].now(i, u))
                                if l == 0:
                                    dve.wait_ge(n_out[0].sem[u], n_out[0].old(i))
                                else:
                                    dve.wait_ge(n_dve[8].sem, n_dve[8].old(i, u))
                                dve.tensor_tensor(flat(zz, u), banks[6 + u], flat(yb, u), ALU.add).then_inc(n_dve[7].sem, 1)
                        if third and l:
                            for u in range(2):
                                dve.wait_ge(n_dve[7].sem, n_dve[7].now(i, u))
                                dve.wait_ge(n_in2.sem[u], n_in2.now(i))
                                dve.wait_ge(n_dve[11].sem, n_dve[11].old(i, u))
                                dve.tensor_tensor(flat(nsum, u), flat(zz, u), flat(res, u), ALU.add).then_inc(n_dve[8].sem, 1)
                            for u in range(2):
                                dve.wait_ge(n_dve[8].sem, n_dve[8].now(i, u))
                                stats(dve, nst[2], nsum, u).then_inc(n_dve[9].sem, 1)
                        if first:
                            for u in range(2):
                                dve.wait_ge(n_pe[1].sem, n_pe[1].now(f, u))
                                dve.wait_ge(n_dve[3].sem, n_dve[3].old(f, u))
                                for k in range(TPC):
                                    last = dve.scalar_tensor_tensor(tmp[:, u, k, :], u_vo[:, l, :], deg_node[:, bass.ds(f * TPC + (u * TPC + k), 1)],
                                                                    banks[2 + u][:, k * D:(k + 1) * D], ALU.mult, ALU.add)
                                last.then_inc(n_dve[6].sem, 1)
                            for u in range(2):
                                dve.wait_ge(n_dve[6].sem, n_dve[6].now(f, u))
                                dve.wait_ge(n_pool[4].sem, n_pool[4].now(f, u))
                                dve.wait_ge(n_pool[5].sem, n_pool[5].old(f, u))
                                dve.wait_ge(n_dve[5].sem, n_dve[5].old(f, u))
                                dve.tensor_tensor(flat(yy, u), flat(tmp, u), flat(xc, u), ALU.add).then_inc(n_dve[3].sem, 1)
                            for u in range(2):
                                dve.wait_ge(n_dve[3].sem, n_dve[3].now(f, u))
                                stats(dve, nst[1], yy, u).then_inc(n_dve[4].sem, 1)
                        if third and l:
                            for u in range(2):
                                dve.wait_ge(n_pool[7].sem, n_pool[7].now(i, u))
                                dve.wait_ge(n_out[0].sem[u], n_out[0].old(i))
                                normalise(dve, nout, nsum, nst[2], nrs[2], u).then_inc(n_dve[11].sem, 1)
                        if first:
                            for u in range(2):
                                dve.wait_ge(n_pool[3].sem, n_pool[3].now(f, u))
                                dve.wait_ge(n_pe[0].sem, n_pe[0].now(f, u))
                                normalise(dve, xh, yy, nst[1], nrs[1], u).then_inc(n_dve[5].sem, 1)
                    skewed3(dve, CN, step)

                @block.gpsimd
                def _(pool):
                    def step(i, first, second, third):
                        f, s = i + 4, i + 2
                        if first:
                            for u in range(2):
                                p_wait(pool, n_dve[1].sem, n_dve[1].old(f, u))
                                rstd(pool, f, u, nst[0], nv[0], nrs[0], n_dve[0], n_pool[0], n_pool[1])
                        if second:
                            for u in range(2):
                                p_wait(pool, n_dve[3].sem, n_dve[3].now(s, u))
                                p_wait(pool, n_dve[7].sem, n_dve[7].old(s, u))
                                pool.tensor_tensor(yb[:, u, :, :], yy[:, u, :, :],
                                                   b_down[:, l, :].unsqueeze(1).broadcast_to([D, TPC, D]), ALU.add).then_inc(n_pool[5].sem, 1)
                        if first:
                            for u in range(2):
                                p_wait(pool, n_dve[3].sem, n_dve[3].old(f, u))
                                pool.tensor_tensor(xc[:, u, :, :], xin[:, u, :, :],
                                                   c_vo[:, l, :].unsqueeze(1).broadcast_to([D, TPC, D]), ALU.add).then_inc(n_pool[4].sem, 1)
                        if third and l:
                            for u in range(2):
                                p_wait(pool, n_dve[11].sem, n_dve[11].old(i, u))
                                rstd(pool, i, u, nst[2], nv[2], nrs[2], n_dve[9], n_pool[6], n_pool[7])
                        if first:
                            for u in range(2):
                                p_wait(pool, n_dve[5].sem, n_dve[5].old(f, u))
                                rstd(pool, f, u, nst[1], nv[1], nrs[1], n_dve[4], n_pool[2], n_pool[3])
                    skewed3(pool, CN, step)
            end_phase(CN)

        node_transformer(0)
        node_transformer(1)

        xin, x_T, r0_T, r1_T, r2_T, r3_T, e_front, e_back, res = nb
        rows0, rows1, rows2, oo = yT, nsum, nout, nsb("node_result", [D, 2, TPC, D])
        m_front, m_back = nsb("node_m_front", [D, 2, TPC, D]), nsb("node_m_back", [D, 2, TPC, D])
        yy = nsb("node_yy", [D, 2, TPC, D])
        exp_done = (n_act[1], n_act[2], n_act[3], n_act[7])
        rows_done, min_done, elu_done = n_act[4:7], n_dve[4:8], n_dve[0:4]
        round_in, round_out = (x_T, r0_T, r1_T, r2_T), (r0_T, r1_T, r2_T, r3_T)
        with nc.Block() as block:
            @block.sync
            def _(sp):
                node_sync(sp, 4, [(4, T5, xin, n_in, (n_pe[0],))],
                          [(0, t["out"], oo, n_out[3], n_dve[11]), (2, T8, rows2, n_out[2], rows_done[2]),
                           (4, T6, rows0, n_out[0], rows_done[0]), (4, T7, rows1, n_out[1], rows_done[1])],
                          [(2, T5, res, n_in2, (n_dve[8],))], False, t["out"])

            @block.tensor
            def _(pe):
                def product(r, i):
                    for u in range(2):
                        if r == 0:
                            pe.wait_ge(n_act[0].sem, n_act[0].now(i, u))
                            pe.wait_ge(elu_done[1].sem, elu_done[1].old(i, u))
                        else:
                            pe.wait_ge(elu_done[r - 1].sem, elu_done[r - 1].now(i, u))
                            if r == 2:
                                pe.wait_ge(elu_done[3].sem, elu_done[3].old(i, u))
                        pe.matmul(banks[(2 if r < 2 else 6) + u], w_root[:, r, :], flat(round_in[r], u), start=True,
                                  stop=True).then_inc(n_pe[1 + r].sem, 1)

                def rows(r, i):
                    for u in range(2):
                        pe.wait_ge(elu_done[r].sem, elu_done[r].now(i, u))
                        if r == 1:
                            pe.wait_ge(rows_done[0].sem, rows_done[0].now(i, u))
                        elif r == 2:
                            pe.wait_ge(n_dve[8].sem, n_dve[8].old(i, u))
                        elif r == 3:
                            pe.wait_ge(rows_done[2].sem, rows_done[2].now(i, u))
                        tiles_T(pe, banks[(0 if r < 2 else 4) + u], lambda k: round_out[r][:, u, k, :], u).then_inc(n_pe[5 + r].sem, 1)

                def step(i, first, second, third):
                    f, s = i + 4, i + 2
                    if first:
                        for u in range(2):
                            pe.wait_ge(n_in.sem[u], n_in.now(f))
                            pe.wait_ge(rows_done[1].sem, rows_done[1].old(f, u))
                            tiles_T(pe, banks[u], lambda k: xin[:, u, k, :], u).then_inc(n_pe[0].sem, 1)
                    if second:
                        product(2, s)
                    if first:
                        product(0, f)
                    if second:
                        product(3, s)
                        rows(2, s)
                    if first:
                        product(1, f)
                    if second:
                        rows(3, s)
                    if first:
                        rows(0, f)
                        rows(1, f)
                skewed3(pe, CN, step)

            @block.scalar
            def _(act):
                def exps(r, i):
                    for u in range(2):
                        act.wait_ge(n_pe[1 + r].sem, n_pe[1 + r].now(i, u))
                        if r % 2:
                            act.wait_ge(min_done[r - 1].sem, min_done[r - 1].now(i, u))
                        else:
                            act.wait_ge(min_done[r + 1].sem, min_done[r + 1].old(i, u))
                        act.activation(flat(e_front if r < 2 else e_back, u), banks[(2 if r < 2 else 6) + u], ACT.Exp,
                                       bias=rel_col[:, r:r + 1]).then_inc(exp_done[r].sem, 1)

                def rows(r, i):
                    for u in range(2):
                        act.wait_ge(n_pe[5 + r].sem, n_pe[5 + r].now(i, u))
                        act.wait_ge(n_out[r].sem[u], n_out[r].old(i))
                        act.copy(flat((rows0, rows1, rows2)[r], u), banks[(0 if r < 2 else 4) + u]).then_inc(rows_done[r].sem, 1)

                def step(i, first, second, third):
                    f, s = i + 4, i + 2
                    if first:
                        for u in range(2):
                            act.wait_ge(n_pe[0].sem, n_pe[0].now(f, u))
                            act.wait_ge(n_pe[1].sem, n_pe[1].old(f, u))
                            act.copy(flat(x_T, u), banks[u]).then_inc(n_act[0].sem, 1)
                    if second:
                        exps(2, s)
                    if first:
                        exps(0, f)
                    if second:
                        exps(3, s)
                        rows(2, s)
                    if first:
                        exps(1, f)
                        rows(0, f)
                        rows(1, f)
                skewed3(act, CN, step)

            @block.vector
            def _(dve):
                def elu(r, i):
                    m = m_front if r < 2 else m_back
                    for u in range(2):
                        dve.wait_ge(exp_done[r].sem, exp_done[r].now(i, u))
                        if r % 2:
                            dve.wait_ge(elu_done[r - 1].sem, elu_done[r - 1].now(i, u))
                        else:
                            dve.wait_ge(elu_done[r + 1].sem, elu_done[r + 1].old(i, u))
                        dve.tensor_scalar(flat(m, u), flat(e_front if r < 2 else e_back, u), 1.0, -1.0, ALU.min,
                                          ALU.add).then_inc(min_done[r].sem, 1)
                    for u in range(2):
                        dve.wait_ge(min_done[r].sem, min_done[r].now(i, u))
                        dve.wait_ge(n_pe[5 + r].sem, n_pe[5 + r].old(i, u))
                        if r == 1:
                            dve.wait_ge(n_pe[3].sem, n_pe[3].old(i, u))
                        dve.scalar_tensor_tensor(flat(round_out[r], u), banks[(2 if r < 2 else 6) + u], rel_col[:, r:r + 1],
                                                 flat(m, u), ALU.add, ALU.max).then_inc(elu_done[r].sem, 1)

                def step(i, first, second, third):
                    f, s = i + 4, i + 2
                    if second:
                        elu(2, s)
                    if third:
                        for u in range(2):
                            dve.wait_ge(n_pool[1].sem, n_pool[1].now(i, u))
                            dve.wait_ge(n_out[3].sem[u], n_out[3].old(i))
                            normalise(dve, oo, yy, nst[0], nrs[0], u).then_inc(n_dve[11].sem, 1)
                    if first:
                        elu(0, f)
                    if second:
                        elu(3, s)
                    if first:
                        elu(1, f)
                    if second:
                        for u in range(2):
                            dve.wait_ge(n_pe[8].sem, n_pe[8].now(s, u))
                            dve.wait_ge(n_in2.sem[u], n_in2.now(s))
                            dve.wait_ge(n_dve[11].sem, n_dve[11].old(s, u))
                            dve.tensor_tensor(flat(yy, u), banks[4 + u], flat(res, u), ALU.add).then_inc(n_dve[8].sem, 1)
                        for u in range(2):
                            dve.wait_ge(n_dve[8].sem, n_dve[8].now(s, u))
                            stats(dve, nst[0], yy, u).then_inc(n_dve[9].sem, 1)
                skewed3(dve, CN, step)

            @block.gpsimd
            def _(pool):
                with pairs(pool, CN) as i:
                    for u in range(2):
                        p_wait(pool, n_dve[11].sem, n_dve[11].old(i, u))
                        rstd(pool, i, u, nst[0], nv[0], nrs[0], n_dve[9], n_pool[0], n_pool[1])
        end_phase(CN)
        nodes.close()

        msg = sb("msg", [D, 2, D])
        xd = sb("xd", [D, 2, D])
        res_e = sb("res_e", [D, 2, D])
        aT = sb("aT", [D, 2, 2 * D])
        z = sb("z", [D, 2, D])
        ex = sb("ex", [D, 2, D])
        em = sb("em", [D, 2, D])
        ye = sb("ye", [D, 2, D])
        yo = sb("yo", [D, 2, D])
        est = sb("est", [D, 2, 6])
        eag = sb("eag", [D, 2, 2])
        ev = sb("ev", [D, 2, 2])
        ers = sb("ers", [D, 2, 2])

        def slot_rows(table, c, base):
            return table[bass.ds(c * D + base, D), :]

        def edge_sync(sp, loads, stores):
            def load(c, u, which):
                table, base, buf, tr, _ = which
                sp.dma_start(buf[:, u, :], slot_rows(table, c, base)).then_inc(tr.sem[u], 16)

            def store(i, u):
                for table, base, buf, tr, sig in stores:
                    sp.wait_ge(sig.sem, sig.now(i, u))
                    sp.dma_start(slot_rows(table, i + u, base), buf[:, u, :]).then_inc(tr.sem[u], 16)
            for which in loads:
                load(0, 0, which)
                load(1, 1, which)
            with pairs(sp, ET - 2) as i:
                for which in loads:
                    for u in range(2):
                        sp.wait_ge(which[4].sem, which[4].now(i, u))
                        load(i + (u + 2), u, which)
                for u in range(2):
                    store(i, u)
            for u in range(2):
                store(ET - 2, u)
            for _, _, _, tr, _ in stores:
                for u in range(2):
                    sp.wait_ge(tr.sem[u], tr.end(ET))

        def layer_norm_stats(dve, i, u, x, made):
            dve.wait_ge(made.sem, made.now(i, u))
            dve.bn_stats(est[:, u, :], x[:, u, :]).then_inc(st_set.sem, 1)
            dve.wait_ge(st_set.sem, st_set.now(i, u))
            dve.wait_ge(ln_set.sem, ln_set.old(i, u))
            dve.nop(nofuse=True)
            dve.bn_aggr(eag[:, u, :], est[:, u, :]).then_inc(c_set.sem, 1)

        def layer_norm_rstd(pool, i, u):
            p_wait(pool, c_set.sem, c_set.now(i, u))
            p_wait(pool, ln_set.sem, ln_set.old(i, u))
            pool.tensor_scalar(ev[:, u, 0:1], eag[:, u, 1:2], EPS, None, ALU.add).then_inc(v_set.sem, 1)
            p_wait(pool, v_set.sem, v_set.now(i, u))
            pool.tensor_tensor(ers[:, u, 0:1], ev[:, u, 0:1], minus_half[:, 0:1], ALU.pow).then_inc(rs_set.sem, 1)

        def layer_norm_out(dve, i, u, x, out):
            dve.wait_ge(rs_set.sem, rs_set.now(i, u))
            return dve.tensor_scalar(out[:, u, :], x[:, u, :], eag[:, u, 0:1], ers[:, u, 0:1], ALU.subtract, ALU.mult)

        def mean_round(table, wl, wr, bias, out_t, elu, norm, residual=None, first=False, final=False):
            res_t = {"x": (XD0, 0), "t5": (T5, NP)}.get(residual)
            made = ln_set if norm else y_set
            made_buf = yo if norm else ye
            own_in = got_dst if first else got_own
            put = put_rows if final else put_out
            with nc.Block() as block:
                @block.gpsimd
                def _(pool):
                    def step(i, front, back):
                        if front:
                            f = i + 2
                            for u in range(2):
                                gather(pool, f, u, msg[:, u, :], table, x_src if first else g_src, 0,
                                       (agg_done.sem, agg_done.old(f, u))).then_inc(got_src.sem[u], 16)
                                if first:
                                    p_wait(pool, put_x.sem[u], put_x.old(f))
                                    gather(pool, f, u, xd[:, u, :], table, x_dst, 1,
                                           (agg_done.sem, agg_done.old(f, u))).then_inc(got_dst.sem[u], 16)
                        if back and norm:
                            for u in range(2):
                                layer_norm_rstd(pool, i, u)
                        if back and final:
                            for u in range(2):
                                p_wait(pool, put_rows.sem[u], put_rows.old(i))
                            pool.tensor_copy(idx2f[:, :], put_row[:, bass.ds(i, 2)]).then_inc(row_set.sem, 2)
                            p_wait(pool, row_set.sem, row_set.now(i, 1))
                            for u in range(2):
                                p_wait(pool, ln_set.sem, ln_set.now(i, u))
                                pool.indirect_dma_start(t["out"], bass.IndirectOffsetOnAxis(ap=idx2f[:, u:u + 1], axis=0),
                                                        yo[:, u, :], None, bounds_check=N - 1,
                                                        oob_is_err=False).then_inc(put_rows.sem[u], 16)
                    skewed(pool, ET, step)
                    if final:
                        for u in range(2):
                            pool.wait_ge(put_rows.sem[u], put_rows.end(ET))

                @block.sync
                def _(sp):
                    if first:
                        with pairs(sp, ET) as i:
                            for u in range(2):
                                sp.wait_ge(got_dst.sem[u], got_dst.now(i))
                                sp.dma_start(slot_rows(XD0, i + u, 0), xd[:, u, :]).then_inc(put_x.sem[u], 16)
                                sp.wait_ge(made.sem, made.now(i, u))
                                sp.dma_start(slot_rows(out_t, i + u, NP), made_buf[:, u, :]).then_inc(put_out.sem[u], 16)
                        for u in range(2):
                            sp.wait_ge(put_out.sem[u], put_out.end(ET))
                            sp.wait_ge(put_x.sem[u], put_x.end(ET))
                    else:
                        loads = [(table, NP, xd, got_own, agg_done)]
                        if residual:
                            loads.append((res_t[0], res_t[1], res_e, got_res, y_set))
                        edge_sync(sp, loads, [] if final else [(out_t, NP, made_buf, put_out, made)])

                @block.tensor
                def _(pe):
                    with pairs(pe, ET) as i:
                        for u in range(2):
                            pe.wait_ge(seg_set.sem, seg_set.now(i, u))
                            pe.wait_ge(got_src.sem[u], got_src.now(i))
                            pe.wait_ge(own_in.sem[u], own_in.now(i))
                            pe.wait_ge(at_set.sem, at_set.old(i, u))
                            pe.wait_ge(carry_set.sem, carry_set.last(i, u))
                            pe.matmul(banks[2 + u][0:1, 0:D], seg[:, u, D - 1:D], msg[:, u, :], start=True, stop=False)
                            pe.matmul(banks[2 + u][0:1, 0:D], cont[0:1, u, D - 1:D], carry[0:1, 1 - u, 0:D], start=False, stop=True)
                            pe.matmul(banks[u][:, 0:D], msg[:, u, :], seg[:, u, :], start=True, stop=False)
                            pe.matmul(banks[u][:, 0:D], carry[0:1, 1 - u, 0:D], cont[0:1, u, :], start=False, stop=True)
                            pe.transpose(banks[u][:, D:2 * D], xd[:, u, :], ident[:, :]).then_inc(agg_done.sem, 1)
                        for u in range(2):
                            pe.wait_ge(at_set.sem, at_set.now(i, u))
                            pe.wait_ge(z_set.sem, z_set.old(i, u))
                            pe.matmul(banks[4 + u][:, 0:D], aT[:, u, 0:D], wl, start=True, stop=False)
                            pe.matmul(banks[4 + u][:, 0:D], aT[:, u, D:2 * D], wr, start=False, stop=True).then_inc(mm_done.sem, 1)

                @block.scalar
                def _(act):
                    with pairs(act, ET) as i:
                        for u in range(2):
                            act.wait_ge(agg_done.sem, agg_done.now(i, u))
                            act.copy(carry[0:1, u, 0:D], banks[2 + u][0:1, 0:D]).then_inc(carry_set.sem, 1)
                            act.wait_ge(mm_done.sem, mm_done.old(i, u))
                            act.copy(aT[:, u, :], banks[u][:, 0:2 * D]).then_inc(at_set.sem, 1)
                        for u in range(2):
                            if elu:
                                act.wait_ge(row_set2.sem, row_set2.now(i, u))
                                act.wait_ge(y_set.sem, y_set.old(i, u))
                                act.activation(ex[:, u, :], em[:, u, :], ACT.Exp).then_inc(e_set.sem, 1)
                            elif not norm:
                                act.wait_ge(z_set.sem, z_set.now(i, u))
                                act.wait_ge(put_out.sem[u], put_out.old(i))
                                act.activation(ye[:, u, :], z[:, u, :], ACT.Relu).then_inc(y_set.sem, 1)

                @block.vector
                def _(dve):
                    def step(i, front, back):
                        if front:
                            for u in range(2):
                                dve.wait_ge(agg_done.sem, agg_done.old(i + 2, u))
                                same_target(dve, i + 2, u, True).then_inc(seg_set.sem, 1)
                        if not back:
                            return
                        for u in range(2):
                            dve.wait_ge(mm_done.sem, mm_done.now(i, u))
                            dve.wait_ge(y_set.sem, y_set.old(i, u))
                            dve.tensor_tensor(z[:, u, :], banks[4 + u][:, 0:D], bias, ALU.add).then_inc(z_set.sem, 1)
                            if elu:
                                dve.wait_ge(z_set.sem, z_set.now(i, u))
                                dve.tensor_scalar(em[:, u, :], z[:, u, :], 0.0, None, ALU.min).then_inc(row_set2.sem, 1)
                        for u in range(2):
                            if elu:
                                dve.wait_ge(e_set.sem, e_set.now(i, u))
                                if norm:
                                    dve.scalar_tensor_tensor(em2[:, u, :], ex[:, u, :], -1.0, z[:, u, :], ALU.add, ALU.max).then_inc(elu_set.sem, 1)
                                    dve.wait_ge(elu_set.sem, elu_set.now(i, u))
                                    dve.wait_ge(got_res.sem[u], got_res.now(i))
                                    dve.wait_ge(ln_set.sem, ln_set.old(i, u))
                                    dve.tensor_tensor(ye[:, u, :], em2[:, u, :], res_e[:, u, :], ALU.add).then_inc(y_set.sem, 1)
                                else:
                                    dve.wait_ge(put.sem[u], put.old(i))
                                    dve.scalar_tensor_tensor(ye[:, u, :], ex[:, u, :], -1.0, z[:, u, :], ALU.add, ALU.max).then_inc(y_set.sem, 1)
                            elif norm:
                                dve.wait_ge(z_set.sem, z_set.now(i, u))
                                dve.wait_ge(got_res.sem[u], got_res.now(i))
                                dve.wait_ge(ln_set.sem, ln_set.old(i, u))
                                dve.scalar_tensor_tensor(ye[:, u, :], z[:, u, :], 0.0, res_e[:, u, :], ALU.max, ALU.add).then_inc(y_set.sem, 1)
                        if norm:
                            for u in range(2):
                                layer_norm_stats(dve, i, u, ye, y_set)
                            for u in range(2):
                                dve.wait_ge(put.sem[u], put.old(i))
                                layer_norm_out(dve, i, u, ye, yo).then_inc(ln_set.sem, 1)
                    skewed(dve, ET, step)
            end_phase(ET)

        row_set2, elu_set = edge_signal("min_set"), edge_signal("elu_set")
        em2 = sb("em2", [D, 2, D])
        idx2f = sb("idx2f", [D, 2], I32)
        E3 = [edge_signal(f"more_{x}") for x in range(22)]
        start_signals()

        mean_round(t["x"], W["L0_gnn_W1_l"][:, :], W["L0_gnn_W1_r"][:, :], b1_row[:, :], T1, elu=False, norm=False, first=True)
        mean_round(T1, W["L0_gnn_W2_l"][:, :], W["L0_gnn_W2_r"][:, :], b2_row[:, :], T2, elu=False, norm=True, residual="x")

        zp = sb("zp", [D, 2, 2 * MUL + 9 * MUL])
        prod = sb("prod", [D, 2, 3, MUL, 3])
        pr1 = sb("pr1", [D, 2, MUL, 3])
        zT = sb("zT", [3 * MUL, 2, 4, D])
        (zp_done, zagg_done, zcarry, zT_set, w_done, l1_sum, prod_set) = E3[0:7]
        G0, G1 = 2 * MUL, 3 * MUL
        NZ = G0 + 3 * G1
        with nc.Block() as block:
            @block.gpsimd
            def _(pool):
                def step(i, front, back):
                    if front:
                        for u in range(2):
                            gather(pool, i + 2, u, msg[:, u, :], T2, g_src, 0,
                                   (zp_done.sem, zp_done.old(i + 2, u))).then_inc(got_src.sem[u], 16)
                    if back:
                        for u in range(2):
                            layer_norm_rstd(pool, i, u)
                skewed(pool, ET, step)

            @block.sync
            def _(sp):
                edge_sync(sp, [(T2, NP, res_e, got_res, l1_sum)], [(T3, NP, yo, put_out, ln_set)])

            @block.vector
            def _(dve):
                def tensor_product(i):
                    for u in range(2):
                        dve.wait_ge(zagg_done.sem, zagg_done.old(i, u))
                        same_target(dve, i, u, False).then_inc(seg_set.sem, 1)
                    for u in range(2):
                        a = ea[:, bass.ds(i + u, 1), :].rearrange("p o c -> p (o c)")
                        m = coef[:, bass.ds(i + u, 1), :, :].rearrange("p o k i -> p (o k) i")
                        s = msg[:, u, 0:MUL]
                        v = msg[:, u, MUL:].rearrange("p (u i) -> p u i", i=3)
                        zk = zp[:, u, G0:].rearrange("p (k g w) -> p k g w", k=3, g=3)
                        dve.wait_ge(got_src.sem[u], got_src.now(i))
                        dve.tensor_tensor(pr1[:, u, :, :], v, a[:, 1:4].unsqueeze(1).broadcast_to([D, MUL, 3]), ALU.mult)
                        for k in range(3):
                            last = dve.tensor_tensor(prod[:, u, k, :, :], v, m[:, k, :].unsqueeze(1).broadcast_to([D, MUL, 3]), ALU.mult)
                        last.then_inc(prod_set.sem, 1)
                        dve.tensor_scalar(zp[:, u, 0:MUL], s, a[:, 0:1], None, ALU.mult)
                        for k in range(3):
                            dve.tensor_scalar(zk[:, k, 0, :], s, a[:, 1 + k:2 + k], None, ALU.mult)
                            dve.tensor_scalar(zk[:, k, 1, :], v[:, :, k], a[:, 0:1], None, ALU.mult)
                        dve.wait_ge(prod_set.sem, prod_set.now(i, u))
                        dve.tensor_reduce(zp[:, u, MUL:2 * MUL], pr1[:, u, :, :], AX.X, ALU.add)
                        dve.tensor_reduce(zk[:, :, 2, :], prod[:, u, :, :, :], AX.X, ALU.add).then_inc(zp_done.sem, 1)

                def sum_and_norm(i):
                    for u in range(2):
                        dve.wait_ge(w_done.sem, w_done.now(i, u))
                        dve.wait_ge(got_res.sem[u], got_res.now(i))
                        dve.wait_ge(ln_set.sem, ln_set.old(i, u))
                        dve.tensor_tensor(ye[:, u, 0:MUL], banks[6 + u][:, 0:MUL], res_e[:, u, 0:MUL], ALU.add)
                        dve.tensor_tensor(ye[:, u, MUL:].rearrange("p (w k) -> p w k", k=3),
                                          banks[6 + u][:, MUL:4 * MUL].rearrange("p (k w) -> p w k", k=3),
                                          res_e[:, u, MUL:].rearrange("p (w k) -> p w k", k=3), ALU.add).then_inc(l1_sum.sem, 1)
                    for u in range(2):
                        layer_norm_stats(dve, i, u, ye, l1_sum)
                    for u in range(2):
                        dve.wait_ge(put_out.sem[u], put_out.old(i))
                        layer_norm_out(dve, i, u, ye, yo).then_inc(ln_set.sem, 1)

                def step(i, front, back):
                    if front:
                        tensor_product(i + 2)
                    if back:
                        sum_and_norm(i)
                skewed(dve, ET, step)

            @block.tensor
            def _(pe):
                def group(k):
                    return (0, G0) if k == 0 else (G0 + (k - 1) * G1, G1)
                with pairs(pe, ET) as i:
                    for u in range(2):
                        pe.wait_ge(zp_done.sem, zp_done.now(i, u))
                        pe.wait_ge(seg_set.sem, seg_set.now(i, u))
                        pe.wait_ge(zT_set.sem, zT_set.old(i, u))
                        pe.wait_ge(zcarry.sem, zcarry.last(i, u))
                        pe.matmul(banks[2 + u][0:1, 0:NZ], seg[:, u, D - 1:D], zp[:, u, :], start=True, stop=False)
                        pe.matmul(banks[2 + u][0:1, 0:NZ], cont[0:1, u, D - 1:D], carry[0:1, 1 - u, 0:NZ], start=False, stop=True)
                        for k in range(4):
                            at, n = group(k)
                            pe.matmul(banks[u][0:n, k * D:(k + 1) * D], zp[:, u, at:at + n], seg[:, u, :], start=True, stop=False)
                            last = pe.matmul(banks[u][0:n, k * D:(k + 1) * D], carry[0:1, 1 - u, at:at + n], cont[0:1, u, :],
                                             start=False, stop=True)
                        last.then_inc(zagg_done.sem, 1)
                    for u in range(2):
                        pe.wait_ge(zT_set.sem, zT_set.now(i, u))
                        pe.wait_ge(l1_sum.sem, l1_sum.old(i, u))
                        for k in range(4):
                            n = group(k)[1]
                            last = pe.matmul(banks[6 + u][:, k * MUL:(k + 1) * MUL], zT[0:n, u, k, :],
                                             (tp0 if k == 0 else tp1)[:, :], start=True, stop=True)
                        last.then_inc(w_done.sem, 1)

            @block.scalar
            def _(act):
                with pairs(act, ET) as i:
                    for u in range(2):
                        act.wait_ge(zagg_done.sem, zagg_done.now(i, u))
                        act.copy(carry[0:1, u, 0:NZ], banks[2 + u][0:1, 0:NZ]).then_inc(zcarry.sem, 1)
                        act.wait_ge(w_done.sem, w_done.old(i, u))
                        act.copy(zT[0:G0, u, 0, :], banks[u][0:G0, 0:D])
                        act.copy(zT[:, u, 1:4, :], banks[u][0:G1, D:4 * D].rearrange("p (k e) -> p k e", k=3)).then_inc(zT_set.sem, 1)
        end_phase(ET)

        xp = sb("xp", [D, 2, 2, D])
        raw2 = sb("raw2", [D, 2, 2, D])
        xpT = sb("xpT", [D, 2, 2, D])
        add_s = sb("add_s", [D, 2, 2 * D])
        add_d = sb("add_d", [D, 2, 3 * D])
        kv_s = sb("kv_s", [D, 2, 2 * D])
        qkv_d = sb("qkv_d", [D, 2, 3 * D])
        qk = sb("qk", [D, 2, 2, H, HD])
        att = sb("att", [D, 2, 2, H])
        att2 = sb("att2", [D, 2, 2, H])
        exa = sb("exa", [D, 2, 2, H])
        NM = D + H
        am = sb("am", [D, 2, NM])
        own = sb("own", [D, 2, NM])
        num = sb("num", [D, 2, NM])
        rden = sb("rden", [D, 2, H])
        ag = sb("ag", [D, 2, D])
        agT = sb("agT", [D, 2, D])
        xo = sb("xo", [D, 2, D])
        x2 = sb("x2", [D, 2, D])
        hE = sb("hE", [D, 2, FJ, D])
        z2 = sb("z2", [D, 2, D])
        ast2 = sb("ast2", [D, 2, 2, 3])

        def attention_round(l):
            src_t, dst_t = (T3, T4) if l == 0 else (T4, T5)
            (a_st, a_v, a_rs, a_ln, a_T, a_xT, a_mm, a_qkv, a_qk, a_att, a_exp, a_am, a_agg, a_num, a_ag, a_agt) = E3[0:16]
            (a_agT, a_wo, a_x2, a_ln2, a_t2, a_t2s) = E3[16:22]
            with nc.Block() as block:
                @block.gpsimd
                def _(pool):
                    def step(i, gathers, first, second, third, last):
                        g, f, s, q = i + 8, i + 6, i + 4, i + 2
                        if first:
                            for u in range(2):
                                p_wait(pool, a_st.sem, a_st.now(f, u))
                                p_wait(pool, a_ln.sem, a_ln.old(f, u))
                                pool.tensor_scalar(aev[:, u, :], ast2[:, u, :, 2], 1.0 / D, EPS, ALU.mult, ALU.add).then_inc(a_v.sem, 1)
                                p_wait(pool, a_v.sem, a_v.now(f, u))
                                pool.tensor_tensor(ers2[:, u, :], aev[:, u, :], minus_half[:, 0:2], ALU.pow).then_inc(a_rs.sem, 1)
                        if gathers:
                            for u in range(2):
                                gather(pool, g, u, raw2[:, u, 0, :], src_t, g_src, 0,
                                       (a_ln.sem, a_ln.old(g, u))).then_inc(got_src.sem[u], 16)
                        if second:
                            for u in range(2):
                                layer_norm_rstd(pool, s, u)
                        if third and l:
                            for u in range(2):
                                p_wait(pool, f_st.sem, f_st.now(q, u))
                                p_wait(pool, f_ln.sem, f_ln.old(q, u))
                                pool.tensor_scalar(fv[:, u, :], fag[:, u, 1:2], EPS, None, ALU.add).then_inc(f_v.sem, 1)
                                p_wait(pool, f_v.sem, f_v.now(q, u))
                                pool.tensor_tensor(frs[:, u, :], fv[:, u, :], minus_half[:, 0:1], ALU.pow).then_inc(f_rs.sem, 1)
                        if gathers:
                            for u in range(2):
                                gather(pool, g, u, raw2[:, u, 1, :], src_t, g_dst, 1,
                                       (xo_set.sem, xo_set.old(g, u))).then_inc(got_dst.sem[u], 16)
                    skewed5(pool, ET, step)

                @block.sync
                def _(sp):
                    if l == 0:
                        edge_sync(sp, [], [(dst_t, NP, z2, put_out, y_set)])
                    else:
                        edge_sync(sp, [(T3, NP, res_e, got_res, f_sum)], [(dst_t, NP, yo, put_out, f_ln)])

                @block.vector
                def _(dve):
                    def targets(i, u):
                        dve.wait_ge(a_agg.sem, a_agg.old(i, u))
                        same_target(dve, i, u, False).then_inc(seg_set.sem, 1)

                    def row_stats(i, u):
                        dve.wait_ge(got_src.sem[u], got_src.now(i))
                        dve.wait_ge(got_dst.sem[u], got_dst.now(i))
                        dve.bn_stats(ast2[:, u, :, :].rearrange("p e f -> p (e f)"),
                                     raw2[:, u, :, :].rearrange("p e d -> p d e")).then_inc(a_st.sem, 1)

                    def additions(i, u):
                        dve.wait_ge(a_qkv.sem, a_qkv.old(i, u))
                        dve.scalar_tensor_tensor(add_s[:, u, :], u_qkv[:, l, D:], deg_src[:, bass.ds(i + u, 1)],
                                                 c_qkv[:, l, D:], ALU.mult, ALU.add)
                        dve.scalar_tensor_tensor(add_d[:, u, :], u_qkv[:, l, :], deg_dst[:, bass.ds(i + u, 1)],
                                                 c_qkv[:, l, :], ALU.mult, ALU.add).then_inc(add_set.sem, 1)

                    def normed_rows(i, u):
                        dve.wait_ge(a_rs.sem, a_rs.now(i, u))
                        dve.wait_ge(a_T.sem, a_T.old(i, u))
                        for j in range(2):
                            last = dve.tensor_scalar(xp[:, u, j, :], raw2[:, u, j, :], ast2[:, u, j, 1:2], ers2[:, u, j:j + 1],
                                                     ALU.subtract, ALU.mult)
                        last.then_inc(a_ln.sem, 1)

                    def projections(i, u):
                        dve.wait_ge(a_mm.sem, a_mm.now(i, u))
                        dve.wait_ge(add_set.sem, add_set.now(i, u))
                        dve.wait_ge(a_am.sem, a_am.old(i, u))
                        dve.tensor_tensor(kv_s[:, u, :], banks[u][:, 2 * D:4 * D], add_s[:, u, :], ALU.add)
                        dve.tensor_tensor(qkv_d[:, u, :], banks[2 + u][:, 0:3 * D], add_d[:, u, :], ALU.add).then_inc(a_qkv.sem, 1)

                    def logits(i, u):
                        dve.wait_ge(a_qkv.sem, a_qkv.now(i, u))
                        q = qkv_d[:, u, 0:D]
                        dve.tensor_tensor(qk[:, u, 0].rearrange("p h d -> p (h d)"), q, kv_s[:, u, 0:D], ALU.mult)
                        dve.tensor_tensor(qk[:, u, 1].rearrange("p h d -> p (h d)"), q, qkv_d[:, u, D:2 * D], ALU.mult).then_inc(a_qk.sem, 1)

                    def logit_sums(i, u):
                        dve.wait_ge(a_qk.sem, a_qk.now(i, u))
                        dve.tensor_reduce(att[:, u, :, :], qk[:, u, :, :, :], AX.X, ALU.add).then_inc(att_sum.sem, 1)

                    def clip_above(i, u):
                        dve.wait_ge(att_sum.sem, att_sum.now(i, u))
                        dve.tensor_scalar(att2[:, u, :, :], att[:, u, :, :], HD ** -0.5, ATT_CLIP, ALU.mult, ALU.min).then_inc(att_min.sem, 1)

                    def clip_below(i, u):
                        dve.wait_ge(att_min.sem, att_min.now(i, u))
                        dve.wait_ge(a_exp.sem, a_exp.old(i, u))
                        dve.tensor_scalar(att3[:, u, :, :], att2[:, u, :, :], -ATT_CLIP, None, ALU.max).then_inc(a_att.sem, 1)

                    def weighted_values(i, u):
                        dve.wait_ge(a_exp.sem, a_exp.now(i, u))
                        dve.wait_ge(a_num.sem, a_num.old(i, u))
                        for j, (to, v) in enumerate([(am, kv_s[:, u, D:2 * D]), (own, qkv_d[:, u, 2 * D:3 * D])]):
                            dve.tensor_tensor(to[:, u, 0:D].rearrange("p (h d) -> p h d", d=HD),
                                              v.rearrange("p (h d) -> p h d", d=HD),
                                              exa[:, u, j, :].unsqueeze(2).broadcast_to([D, H, HD]), ALU.mult)
                            last = dve.tensor_copy(to[:, u, D:NM], exa[:, u, j, :])
                        last.then_inc(a_am.sem, 1)

                    def own_row(i, u):
                        dve.wait_ge(a_x2.sem, a_x2.old(i, u))
                        dve.tensor_tensor(xo[:, u, :], raw2[:, u, 1, :], bo_row[:, l, :], ALU.add).then_inc(xo_set.sem, 1)

                    def total(i, u):
                        dve.wait_ge(a_agg.sem, a_agg.now(i, u))
                        dve.wait_ge(a_am.sem, a_am.now(i, u))
                        dve.wait_ge(carry_set.sem, carry_set.now(i, u))
                        dve.wait_ge(a_ag.sem, a_ag.old(i, u))
                        dve.tensor_tensor(num[:, u, :], banks[4 + u][:, 0:NM], own[:, u, :], ALU.add).then_inc(a_num.sem, 1)

                    def inverse(i, u):
                        dve.wait_ge(a_num.sem, a_num.now(i, u))
                        dve.reciprocal(rden[:, u, :], num[:, u, D:NM]).then_inc(rden_set.sem, 1)

                    def quotient(i, u):
                        dve.wait_ge(rden_set.sem, rden_set.now(i, u))
                        dve.wait_ge(a_agt.sem, a_agt.old(i, u))
                        dve.tensor_tensor(ag[:, u, :].rearrange("p (h d) -> p h d", d=HD),
                                          num[:, u, 0:D].rearrange("p (h d) -> p h d", d=HD),
                                          rden[:, u, :].unsqueeze(2).broadcast_to([D, H, HD]), ALU.mult).then_inc(a_ag.sem, 1)

                    def residual(i, u):
                        dve.wait_ge(xo_set.sem, xo_set.now(i, u))
                        dve.wait_ge(a_wo.sem, a_wo.now(i, u))
                        dve.wait_ge(c_set.sem, c_set.old(i, u))
                        dve.wait_ge(z_set.sem, z_set.old(i, u))
                        dve.tensor_tensor(x2[:, u, :], banks[4 + u][:, 0:D], xo[:, u, :], ALU.add).then_inc(a_x2.sem, 1)

                    def mlp_input(i, u):
                        dve.wait_ge(a_t2.sem, a_t2.old(i, u))
                        dve.wait_ge(y_set.sem, y_set.old(i, u))
                        layer_norm_out(dve, i, u, x2, yln).then_inc(ln_set.sem, 1)
                        dve.tensor_tensor(z[:, u, :], x2[:, u, :], b_down[:, l, :], ALU.add).then_inc(z_set.sem, 1)

                    def mlp_output(i, u):
                        dve.wait_ge(mm_done.sem, mm_done.now(i, u))
                        dve.wait_ge(z_set.sem, z_set.now(i, u))
                        if l == 0:
                            dve.wait_ge(put_out.sem[u], put_out.old(i))
                        else:
                            dve.wait_ge(f_sum.sem, f_sum.old(i, u))
                        dve.tensor_tensor(z2[:, u, :], banks[6 + u][:, 0:D], z[:, u, :], ALU.add).then_inc(y_set.sem, 1)

                    def final_sum(i, u):
                        dve.wait_ge(y_set.sem, y_set.now(i, u))
                        dve.wait_ge(got_res.sem[u], got_res.now(i))
                        dve.wait_ge(f_ln.sem, f_ln.old(i, u))
                        dve.tensor_tensor(ye[:, u, :], z2[:, u, :], res_e[:, u, :], ALU.add).then_inc(f_sum.sem, 1)
                        dve.wait_ge(f_sum.sem, f_sum.now(i, u))
                        dve.bn_stats(fst[:, u, :], ye[:, u, :]).then_inc(f_bn.sem, 1)
                        dve.wait_ge(f_bn.sem, f_bn.now(i, u))
                        dve.nop(nofuse=True)
                        dve.bn_aggr(fag[:, u, :], fst[:, u, :]).then_inc(f_st.sem, 1)

                    def final_norm(i, u):
                        dve.wait_ge(f_rs.sem, f_rs.now(i, u))
                        dve.wait_ge(put_out.sem[u], put_out.old(i))
                        dve.tensor_scalar(yo[:, u, :], ye[:, u, :], fag[:, u, 0:1], frs[:, u, :], ALU.subtract,
                                          ALU.mult).then_inc(f_ln.sem, 1)

                    def both(stage, i):
                        for u in range(2):
                            stage(i, u)

                    def step(i, gathers, first, second, third, last):
                        f, s, q = i + 6, i + 4, i + 2
                        if third:
                            both(mlp_input, q)
                        if second:
                            both(logits, s)
                            both(logit_sums, s)
                            both(clip_above, s)
                            both(clip_below, s)
                        if last and l:
                            both(final_norm, i)
                        if first:
                            both(row_stats, f)
                        if second:
                            both(targets, s)
                            both(weighted_values, s)
                        if first:
                            both(additions, f)
                            both(normed_rows, f)
                        if second:
                            both(total, s)
                            both(inverse, s)
                            both(quotient, s)
                        if first:
                            both(projections, f)
                        if second:
                            both(residual, s)
                        if first:
                            both(own_row, f)
                        if second:
                            for u in range(2):
                                layer_norm_stats(dve, s, u, x2, a_x2)
                        if third:
                            both(mlp_output, q)
                            if l:
                                both(final_sum, q)
                    skewed5(dve, ET, step)

                @block.tensor
                def _(pe):
                    def down(i, u):
                        pe.wait_ge(g_last.sem, g_last.now(i, u))
                        for j in range(FJ):
                            end = pe.matmul(banks[6 + u][:, 0:D], hE[:, u, j, :], w_down[:, l, j, :], start=(j == 0), stop=(j == FJ - 1))
                        end.then_inc(mm_done.sem, 1)

                    def step(i, gathers, first, second, third, last):
                        f, s, q = i + 6, i + 4, i + 2
                        if third:
                            for u in range(2):
                                pe.wait_ge(ln_set.sem, ln_set.now(q, u))
                                pe.wait_ge(y_set.sem, y_set.old(q, u))
                                pe.transpose(banks[6 + u][:, 0:D], yln[:, u, :], ident[:, :]).then_inc(a_t2.sem, 1)
                            for u in range(2):
                                pe.wait_ge(a_t2s.sem, a_t2s.now(q, u))
                                for j in range(FJ):
                                    end = pe.matmul(banks[6 + u][:, j * D:(j + 1) * D], w_up[:, l, j * D:(j + 1) * D], yT[:, u, :], start=True, stop=True)
                                end.then_inc(up_done.sem, 1)
                        if second:
                            for u in range(2):
                                agg = banks[4 + u]
                                pe.wait_ge(a_am.sem, a_am.now(s, u))
                                pe.wait_ge(seg_set.sem, seg_set.now(s, u))
                                pe.wait_ge(a_x2.sem, a_x2.old(s, u))
                                pe.wait_ge(carry_set.sem, carry_set.last(s, u))
                                pe.matmul(agg[0:1, NM:2 * NM], seg[:, u, D - 1:D], am[:, u, :], start=True, stop=False)
                                pe.matmul(agg[0:1, NM:2 * NM], cont[0:1, u, D - 1:D], carry[0:1, 1 - u, 0:NM], start=False, stop=True)
                                pe.matmul(agg[:, 0:NM], seg[:, u, :], am[:, u, :], start=True, stop=False)
                                pe.matmul(agg[:, 0:NM], cont[0:1, u, :], carry[0:1, 1 - u, 0:NM], start=False, stop=True).then_inc(a_agg.sem, 1)
                        if first:
                            for u in range(2):
                                pe.wait_ge(a_ln.sem, a_ln.now(f, u))
                                pe.wait_ge(a_qkv.sem, a_qkv.old(f, u))
                                for j in range(2):
                                    end = pe.transpose(banks[u][:, j * D:(j + 1) * D], xp[:, u, j, :], ident[:, :])
                                end.then_inc(a_T.sem, 1)
                        if third:
                            down(q, 0)
                        if first:
                            for u in range(2):
                                pe.wait_ge(a_xT.sem, a_xT.now(f, u))
                                pe.matmul(banks[u][:, 2 * D:4 * D], xpT[:, u, 0, :], w_qkv[:, l, D:3 * D], start=True, stop=True)
                                pe.matmul(banks[2 + u][:, 0:3 * D], xpT[:, u, 1, :], w_qkv[:, l, :], start=True, stop=True).then_inc(a_mm.sem, 1)
                        if second:
                            for u in range(2):
                                pe.wait_ge(a_ag.sem, a_ag.now(s, u))
                                pe.transpose(banks[4 + u][:, 384:512], ag[:, u, :], ident[:, :]).then_inc(a_agt.sem, 1)
                        if third:
                            down(q, 1)
                        if second:
                            for u in range(2):
                                pe.wait_ge(a_agT.sem, a_agT.now(s, u))
                                pe.matmul(banks[4 + u][:, 0:D], agT[:, u, :], w_o[:, l, :], start=True, stop=True).then_inc(a_wo.sem, 1)
                    skewed5(pe, ET, step)

                @block.scalar
                def _(act):
                    def step(i, gathers, first, second, third, last):
                        f, s, q = i + 6, i + 4, i + 2
                        if third:
                            for u in range(2):
                                act.wait_ge(a_t2.sem, a_t2.now(q, u))
                                act.wait_ge(up_done.sem, up_done.old(q, u))
                                act.copy(yT[:, u, :], banks[6 + u][:, 0:D]).then_inc(a_t2s.sem, 1)
                        if second:
                            for u in range(2):
                                act.wait_ge(a_att.sem, a_att.now(s, u))
                                act.wait_ge(a_am.sem, a_am.old(s, u))
                                act.activation(exa[:, u, :, :], att3[:, u, :, :], ACT.Exp).then_inc(a_exp.sem, 1)
                        if third:
                            for u in range(2):
                                act.wait_ge(up_done.sem, up_done.now(q, u))
                                act.wait_ge(mm_done.sem, mm_done.old(q, u))
                                for j in range(FJ):
                                    end = act.activation(hE[:, u, j, :], banks[6 + u][:, j * D:(j + 1) * D], ACT.Gelu, bias=b_up[:, l, j:j + 1])
                                end.then_inc(g_last.sem, 1)
                        if second:
                            for u in range(2):
                                act.wait_ge(a_agg.sem, a_agg.now(s, u))
                                act.copy(carry[0:1, u, 0:NM], banks[4 + u][0:1, NM:2 * NM]).then_inc(carry_set.sem, 1)
                        if first:
                            for u in range(2):
                                act.wait_ge(a_T.sem, a_T.now(f, u))
                                act.wait_ge(a_mm.sem, a_mm.old(f, u))
                                act.copy(xpT[:, u].rearrange("p e d -> p (e d)"), banks[u][:, 0:2 * D]).then_inc(a_xT.sem, 1)
                        if second:
                            for u in range(2):
                                act.wait_ge(a_agt.sem, a_agt.now(s, u))
                                act.wait_ge(a_wo.sem, a_wo.old(s, u))
                                act.copy(agT[:, u, :], banks[4 + u][:, 384:512]).then_inc(a_agT.sem, 1)
                    skewed5(act, ET, step)
            end_phase(ET)

        ers2 = sb("ers2", [D, 2, 2])
        aev = sb("aev", [D, 2, 2])
        att3 = sb("att3", [D, 2, 2, H])
        yln, yT = sb("yln", [D, 2, D]), sb("yT", [D, 2, D])
        fst, fag, fv, frs = sb("fst", [D, 2, 6]), sb("fag", [D, 2, 2]), sb("fv", [D, 2, 1]), sb("frs", [D, 2, 1])
        names = ("add_set", "att_sum", "att_min", "rden_set", "xo_set", "g_last", "up_done", "f_sum", "f_bn", "f_st", "f_v", "f_rs", "f_ln")
        (add_set, att_sum, att_min, rden_set, xo_set, g_last, up_done, f_sum, f_bn, f_st, f_v, f_rs, f_ln) = map(edge_signal, names)
        start_signals()
        with nc.Block() as block:
            @block.vector
            def _(dve):
                dve.memset(carry[:, :, :], 0.0)
                dve.drain()
        attention_round(0)
        attention_round(1)

        def root(l):
            return w_rel[:, l, :], w_root[:, l, :], rel_row[:, l, :]
        mean_round(T5, *root(0), T6, elu=True, norm=False)
        mean_round(T6, *root(1), T7, elu=True, norm=False)
        mean_round(T7, *root(2), T8, elu=True, norm=False)
        mean_round(T8, *root(3), None, elu=True, norm=True, residual="t5", final=True)


_INS = ['x',
        'src',
        'dst',
        'edge_attr_9',
        'L0_gnn_W1_l',
        'L0_gnn_b1',
        'L0_gnn_W1_r',
        'L0_gnn_W2_l',
        'L0_gnn_b2',
        'L0_gnn_W2_r',
        'L1_gnn_w0',
        'L1_gnn_w1',
        'L1_gnn_w2',
        'L1_gnn_w3',
        'L1_gnn_w4',
        'L2_gnn_Wq',
        'L2_gnn_bq',
        'L2_gnn_Wk',
        'L2_gnn_bk',
        'L2_gnn_Wv',
        'L2_gnn_bv',
        'L2_gnn_Wo',
        'L2_gnn_bo',
        'L2_gnn_Wpos',
        'L2_gnn_bpos',
        'L2_gnn_Wdeg',
        'L2_gnn_bdeg',
        'L2_gnn_ln1_g',
        'L2_gnn_ln1_b',
        'L2_gnn_ln2_g',
        'L2_gnn_ln2_b',
        'L2_gnn_W1',
        'L2_gnn_b1',
        'L2_gnn_W2',
        'L2_gnn_b2',
        'L3_gnn_Ws_rel',
        'L3_gnn_bs_rel',
        'L3_gnn_Ws_root']


def kernel(**inputs):
    import numpy as _np
    import concourse.bacc as _bacc
    from concourse import mybir as _mybir
    from concourse.bass_utils import run_bass_kernel_spmd as _run

    nc = _bacc.Bacc("TRN2", target_bir_lowering=False, num_devices=1)
    arrays, tensors = {}, {}
    for name in _INS:
        a = _np.ascontiguousarray(inputs[name])
        arrays[f"in_{name}_dram"] = a
        tensors[name] = nc.dram_tensor(f"in_{name}_dram", a.shape, _mybir.dt.from_np(a.dtype), kind="ExternalInput").ap()
    shape = list(inputs["x"].shape)
    tensors["out"] = nc.dram_tensor("out_0_dram", shape, _mybir.dt.from_np(_np.dtype("float32")), kind="ExternalOutput").ap()
    gnn_stack(nc, tensors)
    r = _run(nc, [arrays], core_ids=[0])
    return r.results[0]["out_0_dram"]
```

```python
import concourse.bass as bass
from concourse import mybir
from contextlib import ExitStack, contextmanager
from math import factorial, sqrt
import numpy as np

F32 = mybir.dt.float32
BF16 = mybir.dt.bfloat16
I32 = mybir.dt.int32
ALU = mybir.AluOpType
ACT = mybir.ActivationFunctionType
AX = mybir.AxisListType

D = 128
TPC = 4
CH = TPC * D
H, HD = 8, 16
FF = 512
FJ = FF // D
MUL = 32
EPS = 1e-5
STD_EPS = 1e-6
ATT_CLIP = 50.0
EA = 9


def wigner_3j(l1, l2, l3):
    def f(n):
        return factorial(round(n))

    def cg(j1, m1, j2, m2, j3, m3):
        if m3 != m1 + m2:
            return 0.0
        vmin = int(max(-j1 + j2 + m3, -j1 + m1, 0))
        vmax = int(min(j2 + j3 + m1, j3 - j1 + j2, j3 + m3))
        c = ((2.0 * j3 + 1.0) * f(j3 + j1 - j2) * f(j3 - j1 + j2) * f(j1 + j2 - j3) * f(j3 + m3) * f(j3 - m3)
             / (f(j1 + j2 + j3 + 1) * f(j1 - m1) * f(j1 + m1) * f(j2 - m2) * f(j2 + m2))) ** 0.5
        s = 0
        for v in range(vmin, vmax + 1):
            s += (-1) ** (v + j2 + m2) * f(j2 + j3 + m1 - v) * f(j1 - m1 + v) / (
                f(v) * f(j3 - j1 + j2 - v) * f(j3 + m3 - v) * f(v + j1 - j2 - m3))
        return float(c * s)

    def basis(l):
        q = np.zeros((2 * l + 1, 2 * l + 1), dtype=np.complex128)
        for m in range(-l, 0):
            q[l + m, l + abs(m)] = 1 / np.sqrt(2)
            q[l + m, l - abs(m)] = -1j / np.sqrt(2)
        q[l, l] = 1
        for m in range(1, l + 1):
            q[l + m, l + abs(m)] = (-1) ** m / np.sqrt(2)
            q[l + m, l - abs(m)] = 1j * (-1) ** m / np.sqrt(2)
        return (-1j) ** l * q

    c = np.zeros((2 * l1 + 1, 2 * l2 + 1, 2 * l3 + 1))
    for m1 in range(-l1, l1 + 1):
        for m2 in range(-l2, l2 + 1):
            if abs(m1 + m2) <= l3:
                c[l1 + m1, l2 + m2, l3 + m1 + m2] = cg(l1, m1, l2, m2, l3, m1 + m2)
    out = np.real(np.einsum("ij,kl,mn,ikn->jlm", basis(l1), basis(l2), np.conj(basis(l3).T),
                            c.astype(np.complex128)))
    return out / np.linalg.norm(out)


@contextmanager
def pairs(eng, steps):
    with eng.Fori(0, steps // 2) as j:
        yield j * 2


def skewed(eng, steps, step):
    step(-2, True, False)
    with eng.Fori(0, steps // 2 - 1) as j:
        step(j * 2, True, True)
    step(steps - 2, False, True)


def skewed3(eng, steps, step):
    step(-4, True, False, False)
    step(-2, True, True, False)
    with eng.Fori(0, steps // 2 - 2) as j:
        step(j * 2, True, True, True)
    step(steps - 4, False, True, True)
    step(steps - 2, False, False, True)


def skewed5(eng, steps, step):
    for i in (-8, -6, -4, -2):
        step(i, *[i + 8 - 2 * k >= 0 for k in range(5)])
    with eng.Fori(0, steps // 2 - 4) as j:
        step(j * 2, True, True, True, True, True)
    for i in (steps - 8, steps - 6, steps - 4, steps - 2):
        step(i, *[i + 8 - 2 * k < steps for k in range(5)])


def gnn_stack(nc, t):
    N = t["x"].shape[0]
    E = t["src"].shape[0]
    CN = -(-N // CH)
    NP = CN * CH
    ET = -(-E // D)
    EP = ET * D
    TAIL_P = (N - (CN - 1) * CH) // TPC
    TAIL_E = E - (ET - 1) * D
    HC = CN * TPC
    assert N % TPC == 0 and N < NP and E < EP and ET % 2 == 0 and CN % 2 == 0 and CN >= 10 and ET >= 10 and HC <= 512

    ctx = ExitStack()
    with ctx:
        def sb(name, shape, dt=F32):
            return ctx.enter_context(nc.sbuf_tensor("sb_" + name, shape, dt))

        def sem(name):
            return ctx.enter_context(nc.semaphore(name))

        def dram(name, rows, cols, dt=F32):
            return nc.dram_tensor("scratch_" + name, [rows, cols], dt).ap()

        XD0 = dram("x_of_targets", EP, D)
        T1, T2, T3, T4, T5, T6, T7, T8 = [dram(f"table{n}", NP + EP, D) for n in range(1, 9)]
        INFO = dram("node_info", NP, 4)

        bank = [ctx.enter_context(nc.psum_tensor(f"bank{n}", [D, 512], F32)) for n in range(8)]
        banks = [b[:, :] for b in bank]

        ident = sb("ident", [D, D])
        ones = sb("ones", [D, D])
        dst_all = sb("dst_all", [D, EP + 1])
        dst_col = sb("dst_col", [D, ET])
        x_src = sb("x_src", [D, ET], I32)
        x_dst = sb("x_dst", [D, ET], I32)
        g_dst0 = sb("g_dst0", [D, ET], I32)
        g_src = sb("g_src", [D, ET], I32)
        g_dst = sb("g_dst", [D, ET], I32)
        put_row = sb("put_row", [D, ET], I32)
        inv_in = sb("inv_in", [D, ET])
        deg_src = sb("deg_src", [D, ET])
        deg_dst = sb("deg_dst", [D, ET])
        deg_node = sb("deg_node", [D, HC])
        ea = sb("ea", [D, ET, EA])
        coef = sb("coef", [D, ET, 3, 3])
        minus_half = sb("minus_half", [D, 8])
        cnt = sb("cnt", [D, ET])
        seg = sb("seg", [D, 2, D])
        cont = sb("cont", [1, 2, D])
        idx2 = sb("idx2", [D, 2, 2], I32)
        carry = sb("carry", [1, 2, 3 * D])
        W = {}
        for n in ("L0_gnn_W1_l", "L0_gnn_W1_r", "L0_gnn_W2_l", "L0_gnn_W2_r"):
            W[n] = sb("w_" + n, [D, D])
        w_rel = sb("w_rel", [D, 4, D])
        w_root = sb("w_root", [D, 4, D])
        b1_col, b2_col = sb("b1_col", [D, 1]), sb("b2_col", [D, 1])
        b1_row, b2_row = sb("b1_row", [D, D]), sb("b2_row", [D, D])
        rel_col, rel_row = sb("rel_col", [D, 4]), sb("rel_row", [D, 4, D])
        tp0, tp1 = sb("tp0", [2 * MUL, MUL]), sb("tp1", [3 * MUL, MUL])
        w_qkv = sb("w_qkv", [D, 2, 3 * D])
        c_qkv = sb("c_qkv", [D, 2, 3 * D])
        u_qkv = sb("u_qkv", [D, 2, 3 * D])
        w_o = sb("w_o", [D, 2, D])
        bo_row = sb("bo_row", [D, 2, D])
        w_vo = sb("w_vo", [D, 2, D])
        c_vo = sb("c_vo", [D, 2, D])
        u_vo = sb("u_vo", [D, 2, D])
        w_up = sb("w_up", [D, 2, FF])
        b_up = sb("b_up", [D, 2, FJ])
        w_down = sb("w_down", [D, 2, FJ, D])
        b_down = sb("b_down", [D, 2, D])

        weights_loaded = sem("setup_loaded")
        lists_loaded = sem("setup_cast_loaded")
        constants_set = sem("setup_pool")

        class Chain:
            def __init__(self, name):
                self.sem, self.n = sem(name), 0

            def __call__(self, eng, ins):
                self.n += 1
                ins.then_inc(self.sem, 1)
                eng.wait_ge(self.sem, self.n)

        signals, started = [], []

        class Signal:
            def __init__(self, name):
                self.raw, self.n, self.touched = sem(name), 0, False
                signals.append(self)

            @property
            def sem(self):
                self.touched = True
                return self.raw

            def now(self, i, u):
                return i + (self.n + u + 3)

            def last(self, i, u):
                return i + (self.n + u + 2)

            def old(self, i, u):
                return i + (self.n + u + 1)

        class Transfer:
            def __init__(self, name, start=1):
                self.start = start
                self.raw, self.n, self.touched = [sem(name + "_0"), sem(name + "_1")], 0, False
                signals.append(self)

            @property
            def sem(self):
                self.touched = True
                return self.raw

            def now(self, i):
                return i * 8 + (self.n * 8 + self.start + 16)

            def old(self, i):
                return i * 8 + (self.n * 8 + self.start)

            def end(self, steps):
                return 8 * (self.n + steps) + self.start

        def start_signals():
            with nc.Block() as block:
                @block.vector
                def _(dve):
                    for s in signals[len(started):]:
                        if isinstance(s, Signal):
                            dve.sem_inc(s.raw, 2)
                        elif s.start == 1:
                            dve.sem_inc(s.raw[0], 1)
                            dve.sem_inc(s.raw[1], 1)
                        started.append(s)

        def end_phase(steps):
            for s in signals:
                if s.touched:
                    s.n, s.touched = s.n + steps, False

        setup = ExitStack()

        def tmp(name, shape, dt=F32):
            return setup.enter_context(nc.sbuf_tensor("sb_" + name, shape, dt))

        stage = tmp("stage", [D, 6, D])
        lay = tmp("lay", [ET, 3, D])
        wpos = tmp("wpos", [D, 2, D])
        wqkv_raw = tmp("wqkv_raw", [D, 2, 3 * D])
        cols = tmp("cols", [D, 2, 8])
        bqkv = tmp("bqkv", [D, 2, 3 * D])
        aposT = tmp("aposT", [D, D])
        m1 = tmp("m1", [D, 3 * D])
        spread = tmp("spread", [D, 3, D])
        b_up_raw = tmp("b_up_raw", [D, 2, FJ])
        n_ld = [0]
        ea_cleared, pads_set = sem("ea_cleared"), sem("pads_set")

        def row_bc(v):
            return v.rearrange("(a n) -> a n", a=1).broadcast_to([D, v.shape[0]])

        def col_of(v):
            return v.rearrange("(n a) -> n a", a=1)

        with nc.Block() as block:
            @block.sync
            def _(sp):
                def ld(out, in_):
                    sp.dma_start(out, in_).then_inc(weights_loaded, 16)
                    n_ld[0] += 16
                for n in ("L0_gnn_W1_l", "L0_gnn_W1_r", "L0_gnn_W2_l", "L0_gnn_W2_r"):
                    ld(W[n][:, :], t[n])
                ld(b1_col[:, :], col_of(t["L0_gnn_b1"]))
                ld(b2_col[:, :], col_of(t["L0_gnn_b2"]))
                ld(b1_row[:, :], row_bc(t["L0_gnn_b1"]))
                ld(b2_row[:, :], row_bc(t["L0_gnn_b2"]))
                ld(w_rel[:, :, :], t["L3_gnn_Ws_rel"].rearrange("l a b -> a l b"))
                ld(w_root[:, :, :], t["L3_gnn_Ws_root"].rearrange("l a b -> a l b"))
                for l in range(4):
                    ld(rel_col[:, l:l + 1], col_of(t["L3_gnn_bs_rel"][l, :]))
                    ld(rel_row[:, l, :], row_bc(t["L3_gnn_bs_rel"][l, :]))
                for k, (tile, at) in enumerate([(tp0, 0), (tp1, 0), (tp1, MUL), (tp0, MUL), (tp1, 2 * MUL)]):
                    ld(tile[at:at + MUL, :], t[f"L1_gnn_w{k}"].rearrange("u a w -> u (a w)"))
                for l in range(2):
                    ld(wpos[:, l, :], t["L2_gnn_Wpos"][l, :, :])
                    for j, n in enumerate("qkv"):
                        ld(wqkv_raw[:, l, j * D:(j + 1) * D], t[f"L2_gnn_W{n}"][l, :, :])
                        ld(bqkv[:, l, j * D:(j + 1) * D], row_bc(t[f"L2_gnn_b{n}"][l, :]))
                    for j, v in enumerate([t["L2_gnn_ln1_g"][l, :], t["L2_gnn_ln1_b"][l, :], t["L2_gnn_bpos"][l, :],
                                           t["L2_gnn_bdeg"][l, :], t["L2_gnn_Wdeg"][l, 0, :],
                                           t["L2_gnn_ln2_g"][l, :], t["L2_gnn_ln2_b"][l, :]]):
                        ld(cols[:, l, j:j + 1], col_of(v))
                    ld(w_o[:, l, :], t["L2_gnn_Wo"][l, :, :])
                    ld(bo_row[:, l, :], row_bc(t["L2_gnn_bo"][l, :]))
                    ld(w_up[:, l, :], t["L2_gnn_W1"][l, :, :])
                    ld(w_down[:, l, :, :], t["L2_gnn_W2"][l, :, :].rearrange("(j p) n -> p j n", p=D))
                    for j in range(FJ):
                        ld(b_up_raw[:, l, j:j + 1], col_of(t["L2_gnn_b1"][l, j * D:(j + 1) * D]))
                    ld(b_down[:, l, :], row_bc(t["L2_gnn_b2"][l, :]))
                sp.wait_ge(ea_cleared, 1)
                ld(ea[:, 0:ET - 1, :], t["edge_attr_9"][0:(ET - 1) * D, :].rearrange("(s p) c -> p s c", p=D))
                ld(ea[0:TAIL_E, ET - 1, :], t["edge_attr_9"][(ET - 1) * D:E, :])
                sp.wait_ge(weights_loaded, n_ld[0])

            @block.gpsimd
            def _(pool):
                pool.memset(ident[:, :], 0.0).then_inc(constants_set, 1)
                pool.wait_ge(constants_set, 1)
                pool.affine_select(out=ident[:, :], in_=ident[:, :], compare_op=ALU.not_equal, fill=1.0,
                                   base=0, pattern=[[-1, D]], channel_multiplier=1).then_inc(constants_set, 1)
                pool.memset(ones[:, :], 1.0).then_inc(constants_set, 1)
                pool.memset(minus_half[:, :], -0.5).then_inc(constants_set, 1)
                pool.wait_ge(pads_set, 1)
                n = 0
                for j, (v, o) in enumerate([(t["src"], 0), (t["dst"], 0), (t["dst"], 1)]):
                    full = (ET - 1) * D
                    pool.dma_start(lay[0:ET - 1, j, :], v[o:o + full].rearrange("(s p) -> s p", p=D)).then_inc(lists_loaded, 16)
                    pool.dma_start(lay[ET - 1:ET, j, 0:TAIL_E - o],
                                   v[full + o:E].rearrange("(s p) -> s p", s=1)).then_inc(lists_loaded, 16)
                    n += 32
                pool.dma_start(dst_all[:, 1:1 + E], row_bc(t["dst"])).then_inc(lists_loaded, 16)
                pool.wait_ge(lists_loaded, n + 16)

            @block.vector
            def _(dve):
                dve.memset(ea[:, ET - 1, :], 0.0).then_inc(ea_cleared, 1)
                dve.memset(lay[:, 0, :], float(NP))
                dve.memset(lay[:, 1, :], float(NP - 1))
                dve.memset(lay[:, 2, :], float(NP - 1))
                dve.memset(dst_all[:, 0:1], -1.0)
                dve.memset(dst_all[:, 1 + E:], float(NP - 1)).then_inc(pads_set, 1)

        pe_folds, dve_folds = sem("setup_pe_folds"), sem("setup_dve_folds")
        srcf = tmp("srcf", [D, ET])
        nxtf = tmp("nxtf", [D, ET])
        lo_f, hi_f = tmp("lo_f", [D, ET]), tmp("hi_f", [D, ET])
        wi = tmp("wi", [D, 3, ET], I32)
        wf = tmp("wf", [D, 3, ET])
        iota_lo, iota_hi = tmp("iota_lo", [D, D]), tmp("iota_hi", [D, HC])
        w121 = wigner_3j(1, 2, 1)

        with nc.Block() as block:
            @block.gpsimd
            def _(pool):
                pool.iota(iota_lo[:, :], [[1, D]], base=0, channel_multiplier=0,
                          allow_small_or_imprecise_dtypes=True)
                pool.iota(iota_hi[:, :], [[1, HC]], base=0, channel_multiplier=0,
                          allow_small_or_imprecise_dtypes=True)

            @block.tensor
            def _(pe):
                ch = [0]

                def done(ins):
                    ch[0] += 1
                    ins.then_inc(pe_folds, 1)
                for j in range(3):
                    last = pe.transpose(banks[0][:, j * ET:(j + 1) * ET], lay[:, j, :], ident[0:ET, 0:ET])
                done(last)
                for l in range(2):
                    v = 8 * l
                    pe.wait_ge(dve_folds, v + 1)
                    done(pe.transpose(banks[1][:, 0:D], stage[:, 0, :], ident[:, :]))
                    pe.wait_ge(dve_folds, v + 2)
                    done(pe.matmul(banks[2][:, 0:3 * D], aposT[:, :], wqkv_raw[:, l, :], start=True, stop=True))
                    pe.wait_ge(dve_folds, v + 3)
                    pe.matmul(banks[3][:, 0:3 * D], spread[:, 0, :], m1[:, :], start=True, stop=False)
                    done(pe.matmul(banks[3][:, 0:3 * D], spread[:, 1, :], wqkv_raw[:, l, :], start=False, stop=True))
                    done(pe.matmul(banks[4][:, 0:3 * D], spread[:, 2, :], wqkv_raw[:, l, :], start=True, stop=True))
                    pe.wait_ge(dve_folds, v + 4)
                    for j, src_ in enumerate([w_qkv[:, l, 2 * D:3 * D], c_qkv[:, l, 2 * D:3 * D], u_qkv[:, l, 2 * D:3 * D]]):
                        last = pe.transpose(banks[5][:, j * D:(j + 1) * D], src_, ident[:, :])
                    done(last)
                    pe.wait_ge(dve_folds, v + 5)
                    for j in range(3):
                        last = pe.matmul(banks[6][:, j * D:(j + 1) * D], stage[:, 1 + j, :], w_o[:, l, :], start=True, stop=True)
                    done(last)
                    for j in range(FJ):
                        last = pe.matmul(banks[7][:, j:j + 1], w_up[:, l, j * D:(j + 1) * D], cols[:, l, 6:7], start=True, stop=True)
                    done(last)

            @block.vector
            def _(dve):
                ch = Chain("su_dve_chain")

                def go(ins):
                    ch(dve, ins)
                dve.wait_ge(pe_folds, 1)
                go(dve.tensor_copy(srcf[:, :], banks[0][:, 0:ET]))
                go(dve.tensor_copy(dst_col[:, :], banks[0][:, ET:2 * ET]))
                go(dve.tensor_copy(nxtf[:, :], banks[0][:, 2 * ET:3 * ET]))
                go(dve.tensor_scalar(x_src[:, :], srcf[:, :], float(N - 1), None, ALU.min))
                go(dve.tensor_scalar(x_dst[:, :], dst_col[:, :], float(N - 1), None, ALU.min))
                go(dve.tensor_copy(g_dst0[:, :], dst_col[:, :]))
                go(dve.tensor_tensor(wf[:, 0, :], dst_col[:, :], nxtf[:, :], ALU.is_equal))
                go(dve.tensor_scalar(wf[:, 1, :], wf[:, 0, :], float(2 * NP), None, ALU.mult))
                go(dve.tensor_tensor(put_row[:, :], wf[:, 1, :], dst_col[:, :], ALU.add))
                go(dve.tensor_copy(wi[:, 0, :], srcf[:, :]))
                go(dve.tensor_scalar(wi[:, 1, :], wi[:, 0, :], 2, 127, ALU.logical_shift_right, ALU.bitwise_and))
                go(dve.tensor_copy(lo_f[:, :], wi[:, 1, :]))
                go(dve.tensor_scalar(wi[:, 1, :], wi[:, 0, :], 9, 2, ALU.logical_shift_right, ALU.logical_shift_left))
                go(dve.tensor_copy(wf[:, 0, :], wi[:, 1, :]))
                go(dve.tensor_scalar(wi[:, 2, :], wi[:, 0, :], 3, None, ALU.bitwise_and))
                go(dve.tensor_copy(wf[:, 1, :], wi[:, 2, :]))
                go(dve.tensor_tensor(hi_f[:, :], wf[:, 0, :], wf[:, 1, :], ALU.add))
                for k in range(3):
                    for i in range(3):
                        first = True
                        for j in range(5):
                            c = float(w121[i, j, k])
                            if abs(c) < 1e-12:
                                continue
                            if first:
                                go(dve.tensor_scalar(coef[:, :, k, i], ea[:, :, 4 + j], c, None, ALU.mult))
                            else:
                                go(dve.scalar_tensor_tensor(coef[:, :, k, i], ea[:, :, 4 + j], c, coef[:, :, k, i],
                                                            ALU.mult, ALU.add))
                            first = False
                        if first:
                            go(dve.memset(coef[:, :, k, i], 0.0))
                fan0, fan1, nb = 2 * MUL, 3 * MUL, sqrt(10.0)
                n0, n1 = sqrt(1.0 / fan0) / nb, sqrt(3.0 / fan1) / nb
                r3 = 1.0 / sqrt(3.0)
                go(dve.tensor_scalar(tp0[0:MUL, :], tp0[0:MUL, :], n0, None, ALU.mult))
                go(dve.tensor_scalar(tp0[MUL:2 * MUL, :], tp0[MUL:2 * MUL, :], n0 * r3, None, ALU.mult))
                go(dve.tensor_scalar(tp1[0:MUL, :], tp1[0:MUL, :], n1 * r3, None, ALU.mult))
                go(dve.tensor_scalar(tp1[MUL:2 * MUL, :], tp1[MUL:2 * MUL, :], n1 * r3, None, ALU.mult))
                go(dve.tensor_scalar(tp1[2 * MUL:3 * MUL, :], tp1[2 * MUL:3 * MUL, :], n1, None, ALU.mult))
                for l in range(2):
                    p = 1 + 7 * l
                    go(dve.tensor_tensor(stage[:, 0, :], wpos[:, l, :], ident[:, :], ALU.add))
                    dve.sem_inc(dve_folds, 1)
                    dve.wait_ge(pe_folds, p + 1)
                    go(dve.tensor_copy(aposT[:, :], banks[1][:, 0:D]))
                    dve.sem_inc(dve_folds, 1)
                    dve.wait_ge(pe_folds, p + 2)
                    go(dve.tensor_copy(m1[:, :], banks[2][:, 0:3 * D]))
                    go(dve.tensor_scalar(w_qkv[:, l, :], m1[:, :], cols[:, l, 0:1], None, ALU.mult))
                    go(dve.tensor_scalar(spread[:, 0, :], ones[:, :], cols[:, l, 1:2], None, ALU.mult))
                    go(dve.tensor_scalar(spread[:, 1, :], ones[:, :], cols[:, l, 2:3], cols[:, l, 3:4], ALU.mult, ALU.add))
                    go(dve.tensor_scalar(spread[:, 2, :], ones[:, :], cols[:, l, 4:5], None, ALU.mult))
                    dve.sem_inc(dve_folds, 1)
                    dve.wait_ge(pe_folds, p + 4)
                    go(dve.tensor_tensor(c_qkv[:, l, :], banks[3][:, 0:3 * D], bqkv[:, l, :], ALU.add))
                    go(dve.tensor_copy(u_qkv[:, l, :], banks[4][:, 0:3 * D]))
                    dve.sem_inc(dve_folds, 1)
                    dve.wait_ge(pe_folds, p + 5)
                    go(dve.tensor_copy(stage[:, 1:4, :], banks[5][:, 0:3 * D].rearrange("p (j d) -> p j d", j=3)))
                    dve.sem_inc(dve_folds, 1)
                    dve.wait_ge(pe_folds, p + 6)
                    go(dve.tensor_copy(w_vo[:, l, :], banks[6][:, 0:D]))
                    go(dve.tensor_tensor(c_vo[:, l, :], banks[6][:, D:2 * D], bo_row[:, l, :], ALU.add))
                    go(dve.tensor_copy(u_vo[:, l, :], banks[6][:, 2 * D:3 * D]))
                    dve.wait_ge(pe_folds, p + 7)
                    go(dve.tensor_tensor(b_up[:, l, :], banks[7][:, 0:FJ], b_up_raw[:, l, :], ALU.add))
                    go(dve.tensor_scalar(w_up[:, l, :], w_up[:, l, :], cols[:, l, 5:6], None, ALU.mult))
                    dve.sem_inc(dve_folds, 3)

        deg_seg, deg_pe = Signal("deg_seg"), Signal("deg_pe")
        deg_carry, deg_cnt = Signal("deg_carry"), Signal("deg_cnt")
        idx_set = [Signal("src_rows_set"), Signal("dst_rows_set")]

        def edge_signal(name):
            return Signal("edge_" + name)
        seg_set, agg_done, carry_set, at_set, mm_done = map(
            edge_signal, ("seg_set", "agg_done", "carry_set", "at_set", "mm_done"))
        z_set, e_set, c_set, y_set = map(edge_signal, ("z_set", "e_set", "c_set", "y_set"))
        st_set, v_set, rs_set, ln_set = map(edge_signal, ("st_set", "v_set", "rs_set", "ln_set"))
        row_set = edge_signal("row_set")
        got_src, got_dst = Transfer("edge_got_src", 0), Transfer("edge_got_dst", 0)
        put_rows = Transfer("edge_put_rows", 16)
        got_own, got_res, put_out, put_x = [Transfer("edge_" + x) for x in ("got_own", "got_res", "put_out", "put_x")]

        def p_wait(pool, s, v):
            pool.wait_ge(s, v)
            pool.nop(nofuse=True)

        def gather(pool, i, u, out, table, rows, j, free):
            p_wait(pool, *free)
            pool.tensor_copy(idx2[:, u, j:j + 1], rows[:, bass.ds(i + u, 1)]).then_inc(idx_set[j].sem, 1)
            p_wait(pool, idx_set[j].sem, idx_set[j].now(i, u))
            return pool.indirect_dma_start(
                out, None, table, bass.IndirectOffsetOnAxis(ap=idx2[:, u, j:j + 1], axis=0))

        def same_target(dve, i, u, scale):
            at = (i + u) * D
            if scale:
                dve.tensor_scalar(seg[:, u, :], dst_all[:, bass.ds(at + 1, D)], dst_col[:, bass.ds(i + u, 1)],
                                  inv_in[:, bass.ds(i + u, 1)], ALU.is_equal, ALU.mult)
            else:
                dve.tensor_scalar(seg[:, u, :], dst_all[:, bass.ds(at + 1, D)], dst_col[:, bass.ds(i + u, 1)],
                                  None, ALU.is_equal)
            return dve.tensor_scalar(cont[0:1, u, :], dst_all[0:1, bass.ds(at + 1, D)],
                                     dst_all[0:1, bass.ds(at, 1)], None, ALU.is_equal)

        one_lo = tmp("one_lo", [D, 2, D], BF16)
        one_hi = tmp("one_hi", [D, 2, HC], BF16)
        zero_b = tmp("zero_b", [D, max(HC, D)], BF16)
        carry_n = tmp("carry_n", [1, 2, 1])

        start_signals()
        with nc.Block() as block:
            @block.vector
            def _(dve):
                dve.memset(zero_b[:, :], 0.0)
                dve.memset(carry[:, :, :], 0.0)
                dve.memset(carry_n[:, :, :], 0.0)
                dve.drain()

        with nc.Block() as block:
            @block.vector
            def _(dve):
                with pairs(dve, ET) as i:
                    for u in range(2):
                        dve.wait_ge(deg_pe.sem, deg_pe.old(i, u))
                        same_target(dve, i, u, False)
                        dve.tensor_scalar(one_lo[:, u, :], iota_lo[:, :], lo_f[:, bass.ds(i + u, 1)], None, ALU.is_equal)
                        dve.tensor_scalar(one_hi[:, u, :], iota_hi[:, :], hi_f[:, bass.ds(i + u, 1)], None,
                                          ALU.is_equal).then_inc(deg_seg.sem, 1)

            @block.tensor
            def _(pe):
                hist = banks[4][:, 0:HC]
                pe.matmul(hist, zero_b[:, 0:D], zero_b[:, 0:HC], start=True, stop=False, skip_group_check=True)
                with pairs(pe, ET) as i:
                    for u in range(2):
                        pe.wait_ge(deg_seg.sem, deg_seg.now(i, u))
                        pe.wait_ge(deg_cnt.sem, deg_cnt.old(i, u))
                        pe.wait_ge(deg_carry.sem, deg_carry.last(i, u))
                        pe.matmul(hist, one_lo[:, u, :], one_hi[:, u, :], start=False, stop=False, skip_group_check=True)
                        pe.matmul(banks[u][:, 0:1], seg[:, u, :], ones[:, 0:1], start=True, stop=False)
                        pe.matmul(banks[u][:, 0:1], cont[0:1, u, :], carry_n[0:1, 1 - u, :], start=False, stop=True)
                        pe.matmul(banks[2 + u][0:1, 0:1], seg[:, u, D - 1:D], ones[:, 0:1], start=True, stop=False)
                        pe.matmul(banks[2 + u][0:1, 0:1], cont[0:1, u, D - 1:D], carry_n[0:1, 1 - u, :],
                                  start=False, stop=True).then_inc(deg_pe.sem, 1)
                pe.matmul(hist, zero_b[:, 0:D], zero_b[:, 0:HC], start=False, stop=True, skip_group_check=True)

            @block.scalar
            def _(act):
                with pairs(act, ET) as i:
                    for u in range(2):
                        act.wait_ge(deg_pe.sem, deg_pe.now(i, u))
                        act.copy(carry_n[0:1, u, :], banks[2 + u][0:1, 0:1]).then_inc(deg_carry.sem, 1)
                        act.copy(cnt[:, bass.ds(i + u, 1)], banks[u][:, 0:1]).then_inc(deg_cnt.sem, 1)
        end_phase(ET)

        sq, colsum = tmp("sq", [D, HC]), tmp("colsum", [D, 4])
        info = tmp("info", [D, CN, TPC, 4])
        info_d, info_s = tmp("info_d", [D, 2, 4]), tmp("info_s", [D, 2, 4])
        slot_row = tmp("slot_row", [D, ET])
        squares_summed, total_done, variance_set, info_set = sem("tab_sq"), sem("tab_total"), sem("tab_var"), sem("tab_info")
        std_set, numbers_set, info_stored = sem("tab_std"), sem("tab_iota"), sem("tab_stored")
        mean_out = (E + N) / N
        primer = tmp("primer", [1, 2])
        half = tmp("half", [D, 1])
        with nc.Block() as block:
            @block.gpsimd
            def _(pool):
                for u in range(2):
                    pool.dma_start(primer[0:1, u:u + 1], t["x"][0:1, 0:1]).then_inc(put_rows.raw[u], 16)
                    pool.wait_ge(put_rows.raw[u], 16)
                pool.memset(half[:, :], 0.5)
                pool.iota(info[:, :, :, 0], [[CH, CN], [1, TPC]], base=0, channel_multiplier=TPC,
                          allow_small_or_imprecise_dtypes=True)
                pool.iota(slot_row[:, :], [[D, ET]], base=NP, channel_multiplier=1,
                          allow_small_or_imprecise_dtypes=True)
                pool.memset(info[:, :, :, 1], 1.0)
                pool.memset(info[:, :, :, 3], 0.0).then_inc(numbers_set, 1)
                pool.wait_ge(numbers_set, 1)
                pool.wait_ge(variance_set, 1)
                pool.tensor_tensor(colsum[:, 2:3], colsum[:, 1:2], half[:, :], ALU.pow).then_inc(std_set, 1)

            @block.tensor
            def _(pe):
                pe.wait_ge(squares_summed, 1)
                pe.matmul(banks[0][:, 0:1], ones[:, :], colsum[:, 0:1], start=True, stop=True).then_inc(total_done, 1)

            @block.vector
            def _(dve):
                ch = Chain("tab_chain")

                def go(ins):
                    ch(dve, ins)
                go(dve.tensor_scalar(deg_node[:, :], banks[4][:, 0:HC], 1.0 - mean_out, None, ALU.add))
                go(dve.tensor_tensor(sq[:, :], deg_node[:, :], deg_node[:, :], ALU.mult))
                dve.tensor_reduce(colsum[:, 0:1], sq[:, :], AX.X, ALU.add).then_inc(squares_summed, 1)
                dve.wait_ge(total_done, 1)
                dve.tensor_scalar(colsum[:, 1:2], banks[0][:, 0:1], -(NP - N) * (1.0 - mean_out) ** 2, 1.0 / (N - 1),
                                  ALU.add, ALU.mult).then_inc(variance_set, 1)
                dve.wait_ge(std_set, 1)
                go(dve.tensor_scalar(colsum[:, 0:1], colsum[:, 2:3], STD_EPS, None, ALU.add))
                go(dve.reciprocal(colsum[:, 3:4], colsum[:, 0:1]))
                go(dve.tensor_scalar(deg_node[:, :], deg_node[:, :], colsum[:, 3:4], None, ALU.mult))
                dve.wait_ge(numbers_set, 1)
                dve.tensor_copy(info[:, :, :, 2], deg_node[:, :].rearrange("p (c t) -> p c t", t=TPC)).then_inc(info_set, 1)

            @block.sync
            def _(sp):
                sp.wait_ge(info_set, 1)
                sp.dma_start(INFO.rearrange("(c p t) f -> p c (t f)", p=D, t=TPC),
                             info[:, :, :, :].rearrange("p c t f -> p c (t f)")).then_inc(info_stored, 16)
                sp.wait_ge(info_stored, 16)

        new_info = tmp("new_info", [D, 2, 2])
        put2 = tmp("put2", [D, 2], I32)
        with nc.Block() as block:
            @block.vector
            def _(dve):
                with pairs(dve, ET) as i:
                    for u in range(2):
                        dve.wait_ge(put_rows.sem[u], put_rows.old(i))
                        dve.tensor_copy(new_info[:, u, 0:1], slot_row[:, bass.ds(i + u, 1)])
                        dve.tensor_copy(new_info[:, u, 1:2], cnt[:, bass.ds(i + u, 1)])
                        dve.tensor_scalar(put2[:, u:u + 1], put_row[:, bass.ds(i + u, 1)], 2.0, None, ALU.mult).then_inc(row_set.sem, 1)

            @block.gpsimd
            def _(pool):
                with pairs(pool, ET) as i:
                    for u in range(2):
                        p_wait(pool, row_set.sem, row_set.now(i, u))
                        pool.indirect_dma_start(INFO.rearrange("n (a b) -> (n a) b", b=2), bass.IndirectOffsetOnAxis(ap=put2[:, u:u + 1], axis=0),
                                                new_info[:, u, :], None, bounds_check=2 * NP - 1,
                                                oob_is_err=False).then_inc(put_rows.sem[u], 16)
                for u in range(2):
                    pool.wait_ge(put_rows.sem[u], put_rows.end(ET))
        end_phase(ET)
        with nc.Block() as block:
            @block.gpsimd
            def _(pool):
                with pairs(pool, ET) as i:
                    for u in range(2):
                        free = (row_set.sem, row_set.old(i, u))
                        gather(pool, i, u, info_s[:, u, :], INFO, x_src, 0, free).then_inc(got_src.sem[u], 16)
                        gather(pool, i, u, info_d[:, u, :], INFO, g_dst0, 1, free).then_inc(got_dst.sem[u], 16)

            @block.vector
            def _(dve):
                with pairs(dve, ET) as i:
                    for u in range(2):
                        dve.wait_ge(got_src.sem[u], got_src.now(i))
                        dve.wait_ge(got_dst.sem[u], got_dst.now(i))
                        dve.tensor_copy(g_src[:, bass.ds(i + u, 1)], info_s[:, u, 0:1])
                        dve.tensor_copy(deg_src[:, bass.ds(i + u, 1)], info_s[:, u, 2:3])
                        dve.tensor_copy(g_dst[:, bass.ds(i + u, 1)], info_d[:, u, 0:1])
                        dve.tensor_copy(deg_dst[:, bass.ds(i + u, 1)], info_d[:, u, 2:3])
                        dve.tensor_copy(cnt[:, bass.ds(i + u, 1)], info_d[:, u, 1:2]).then_inc(row_set.sem, 1)
                dve.wait_ge(row_set.sem, row_set.n + ET + 2)
                dve.reciprocal(inv_in[:, :], cnt[:, :])
        end_phase(ET)

        setup.close()

        nodes = ExitStack()

        def nsb(name, shape, dt=F32):
            return nodes.enter_context(nc.sbuf_tensor("sb_" + name, shape, dt))

        def node_signal(name):
            return Signal("node_" + name)
        n_pe = [node_signal(f"pe_{x}") for x in range(9)]
        n_act = [node_signal(f"act_{x}") for x in range(9)]
        n_dve = [node_signal(f"dve_{x}") for x in range(12)]
        n_pool = [node_signal(f"pool_{x}") for x in range(8)]
        n_in, n_in2 = Transfer("node_in"), Transfer("node_in2")
        n_out = [Transfer(f"node_out{x}") for x in range(4)]
        nb = [nsb(f"node_buf{x}", [D, 2, TPC, D]) for x in range(9)]
        yT = nsb("node_yT", [D, 2, TPC, D])
        nsum, nout = nsb("node_sum", [D, 2, TPC, D]), nsb("node_out", [D, 2, TPC, D])
        hT = nsb("hT", [D, 2, FJ, CH])
        nst = [nsb(f"node_stats{x}", [D, 2, TPC, 3]) for x in range(3)]
        nv = [nsb(f"node_var{x}", [D, 2, TPC]) for x in range(3)]
        nrs = [nsb(f"node_rstd{x}", [D, 2, TPC]) for x in range(3)]

        start_signals()

        def rows_of(table, c, tail=False):
            if tail:
                return table[(CN - 1) * CH:(CN - 1) * CH + TAIL_P * TPC, :].rearrange("(p t) d -> p t d", t=TPC)
            return table[bass.ds(c * CH, CH), :].rearrange("(p t) d -> p t d", t=TPC)

        def node_sync(sp, lag, loads, stores, late_loads, ragged_in, ragged_out):
            def load(which, c, u, tail=False):
                _, table, buf, tr, _ = which
                if tail and ragged_in:
                    sp.dma_start(buf[0:TAIL_P, u], rows_of(table, c, True)).then_inc(tr.sem[u], 16)
                else:
                    sp.dma_start(buf[:, u], rows_of(table, c)).then_inc(tr.sem[u], 16)

            def load_next(which, i, u, tail=False):
                for reader in which[4]:
                    sp.wait_ge(reader.sem, reader.now(i, u))
                load(which, i + (u + 2), u, tail)

            def store(which, i, u, tail=False):
                _, table, buf, tr, sig = which
                sp.wait_ge(sig.sem, sig.now(i, u))
                if tail and table is ragged_out:
                    sp.dma_start(rows_of(table, i + u, True), buf[0:TAIL_P, u]).then_inc(tr.sem[u], 16)
                else:
                    sp.dma_start(rows_of(table, i + u), buf[:, u]).then_inc(tr.sem[u], 16)

            def edge_step(i):
                for which in loads:
                    for u in range(2):
                        if 0 <= i + which[0] and i + which[0] + 2 < CN:
                            load_next(which, i + which[0], u, i + which[0] + 2 + u == CN - 1)
                for which in stores:
                    for u in range(2):
                        if 0 <= i + which[0] < CN:
                            store(which, i + which[0], u, i + which[0] + u == CN - 1)
                for which in late_loads:
                    for u in range(2):
                        if 0 <= i + which[0] and i + which[0] + 2 < CN:
                            load_next(which, i + which[0], u)

            for which in loads + late_loads:
                load(which, 0, 0)
                load(which, 1, 1)
            for i in range(-lag, 0, 2):
                edge_step(i)
            with pairs(sp, CN - 4 - lag) as i:
                for which in loads:
                    for u in range(2):
                        load_next(which, i + which[0], u)
                for which in stores:
                    for u in range(2):
                        store(which, i + which[0], u)
                for which in late_loads:
                    for u in range(2):
                        load_next(which, i + which[0], u)
            for i in range(CN - 4 - lag, CN, 2):
                edge_step(i)
            for _, _, _, tr, _ in stores:
                for u in range(2):
                    sp.wait_ge(tr.sem[u], tr.end(CN))

        def tiles_T(pe, out, src_, u):
            for k in range(TPC):
                last = pe.transpose(out[:, k * D:(k + 1) * D], src_(k), ident[:, :])
            return last

        def stats(dve, st, x, u):
            for q in range(TPC // 2):
                last = dve.bn_stats(st[:, u, 2 * q:2 * q + 2, :].rearrange("p e f -> p (e f)"),
                                    x[:, u, 2 * q:2 * q + 2, :].rearrange("p t d -> p d t"))
            return last

        def rstd(pool, i, u, st, v, r, ready, v_done, r_done):
            p_wait(pool, ready.sem, ready.now(i, u))
            pool.tensor_scalar(v[:, u, :], st[:, u, :, 2], 1.0 / D, EPS, ALU.mult, ALU.add).then_inc(v_done.sem, 1)
            p_wait(pool, v_done.sem, v_done.now(i, u))
            pool.tensor_tensor(r[:, u, :], v[:, u, :], minus_half[:, 0:TPC], ALU.pow).then_inc(r_done.sem, 1)

        def normalise(dve, out, x, st, r, u):
            for k in range(TPC):
                last = dve.tensor_scalar(out[:, u, k, :], x[:, u, k, :], st[:, u, k, 1:2], r[:, u, k:k + 1],
                                         ALU.subtract, ALU.mult)
            return last

        def flat(buf, u):
            return buf[:, u].rearrange("p t d -> p (t d)")

        with nc.Block() as block:
            @block.vector
            def _(dve):
                dve.memset(nb[0][:, :, :, :], 0.0)
                dve.memset(nb[8][:, :, :, :], 0.0)

        xin, xT, h1T, h1n, h2T, y, x1n, x2n = nb[0:8]
        n_x_turned, n_product1, n_product2 = n_pe[0], n_pe[1], n_pe[2]
        n_h1_turned, n_h2_turned, n_xT_set = n_pe[3], n_pe[4], n_act[0]
        n_h1T_set, n_h2T_set, n_h1_set = n_act[1], n_act[2], n_act[3]
        n_sum_set, n_stats_set, n_ln_set = n_dve[0], n_dve[1], n_dve[2]
        n_var_set, n_rstd_set, n_var2_set = n_pool[0], n_pool[1], n_pool[2]
        n_rstd2_set, n_twice_set, n_rstd_squared = n_pool[3], n_pool[4], n_pool[5]
        n_ln_squares = n_pool[6]
        with nc.Block() as block:
            @block.sync
            def _(sp):
                node_sync(sp, 2, [(2, t["x"], xin, n_in, (n_sum_set,))],
                          [(2, T1, h1n, n_out[0], n_h1_set), (2, T2, x1n, n_out[1], n_ln_set),
                           (0, T3, x2n, n_out[2], n_twice_set)], [], True, None)

            @block.tensor
            def _(pe):
                with pairs(pe, CN) as i:
                    for u in range(2):
                        pe.wait_ge(n_in.sem[u], n_in.now(i))
                        pe.wait_ge(n_sum_set.sem, n_sum_set.old(i, u))
                        tiles_T(pe, banks[u], lambda k: xin[:, u, k, :], u).then_inc(n_x_turned.sem, 1)
                    for u in range(2):
                        pe.wait_ge(n_xT_set.sem, n_xT_set.now(i, u))
                        pe.wait_ge(n_h1T_set.sem, n_h1T_set.old(i, u))
                        pe.matmul(banks[2 + u], W["L0_gnn_W1_r"][:, :], flat(xT, u), start=True, stop=True).then_inc(n_product1.sem, 1)
                    for u in range(2):
                        pe.wait_ge(n_h1T_set.sem, n_h1T_set.now(i, u))
                        pe.wait_ge(n_h2T_set.sem, n_h2T_set.old(i, u))
                        pe.matmul(banks[6 + u], W["L0_gnn_W2_r"][:, :], flat(h1T, u), start=True, stop=True).then_inc(n_product2.sem, 1)
                        pe.wait_ge(n_h1_set.sem, n_h1_set.old(i, u))
                        tiles_T(pe, banks[4 + u], lambda k: h1T[:, u, k, :], u).then_inc(n_h1_turned.sem, 1)
                    for u in range(2):
                        pe.wait_ge(n_h2T_set.sem, n_h2T_set.now(i, u))
                        tiles_T(pe, banks[u], lambda k: h2T[:, u, k, :], u).then_inc(n_h2_turned.sem, 1)

            @block.scalar
            def _(act):
                with pairs(act, CN) as i:
                    for u in range(2):
                        act.wait_ge(n_x_turned.sem, n_x_turned.now(i, u))
                        act.wait_ge(n_product1.sem, n_product1.old(i, u))
                        act.copy(flat(xT, u), banks[u]).then_inc(n_xT_set.sem, 1)
                    for u in range(2):
                        act.wait_ge(n_product1.sem, n_product1.now(i, u))
                        act.wait_ge(n_h1_turned.sem, n_h1_turned.old(i, u))
                        act.activation(flat(h1T, u), banks[2 + u], ACT.Relu, bias=b1_col[:, :]).then_inc(n_h1T_set.sem, 1)
                    for u in range(2):
                        act.wait_ge(n_product2.sem, n_product2.now(i, u))
                        act.wait_ge(n_h2_turned.sem, n_h2_turned.old(i, u))
                        act.activation(flat(h2T, u), banks[6 + u], ACT.Relu, bias=b2_col[:, :]).then_inc(n_h2T_set.sem, 1)
                    for u in range(2):
                        act.wait_ge(n_h1_turned.sem, n_h1_turned.now(i, u))
                        act.wait_ge(n_out[0].sem[u], n_out[0].old(i))
                        act.copy(flat(h1n, u), banks[4 + u]).then_inc(n_h1_set.sem, 1)

            @block.vector
            def _(dve):
                def step(i, front, back):
                    f = i + 2
                    if front:
                        for u in range(2):
                            dve.wait_ge(n_h2_turned.sem, n_h2_turned.now(f, u))
                            dve.wait_ge(n_ln_set.sem, n_ln_set.old(f, u))
                            dve.tensor_tensor(flat(y, u), banks[u], flat(xin, u), ALU.add).then_inc(n_sum_set.sem, 1)
                        for u in range(2):
                            dve.wait_ge(n_sum_set.sem, n_sum_set.now(f, u))
                            dve.wait_ge(n_ln_squares.sem, n_ln_squares.old(f, u))
                            stats(dve, nst[0], y, u).then_inc(n_stats_set.sem, 1)
                    if back:
                        for u in range(2):
                            dve.wait_ge(n_rstd2_set.sem, n_rstd2_set.now(i, u))
                            dve.wait_ge(n_out[2].sem[u], n_out[2].old(i))
                            for k in range(TPC):
                                last = dve.tensor_scalar(x2n[:, u, k, :], x1n[:, u, k, :], nrs[1][:, u, k:k + 1], None, ALU.mult)
                            last.then_inc(n_twice_set.sem, 1)
                    if front:
                        for u in range(2):
                            dve.wait_ge(n_rstd_set.sem, n_rstd_set.now(f, u))
                            dve.wait_ge(n_out[1].sem[u], n_out[1].old(f))
                            dve.wait_ge(n_twice_set.sem, n_twice_set.old(f, u))
                            normalise(dve, x1n, y, nst[0], nrs[0], u).then_inc(n_ln_set.sem, 1)
                skewed(dve, CN, step)

            @block.gpsimd
            def _(pool):
                with pairs(pool, CN) as i:
                    for u in range(2):
                        p_wait(pool, n_ln_set.sem, n_ln_set.old(i, u))
                        rstd(pool, i, u, nst[0], nv[0], nrs[0], n_stats_set, n_var_set, n_rstd_set)
                    for u in range(2):
                        p_wait(pool, n_rstd_set.sem, n_rstd_set.now(i, u))
                        pool.tensor_tensor(nv[1][:, u, :], nrs[0][:, u, :], nrs[0][:, u, :], ALU.mult).then_inc(n_rstd_squared.sem, 1)
                    for u in range(2):
                        p_wait(pool, n_rstd_squared.sem, n_rstd_squared.now(i, u))
                        pool.tensor_tensor(nv[2][:, u, :], nv[1][:, u, :], nst[0][:, u, :, 2], ALU.mult).then_inc(n_ln_squares.sem, 1)
                    for u in range(2):
                        p_wait(pool, n_ln_squares.sem, n_ln_squares.now(i, u))
                        pool.tensor_scalar(nv[1][:, u, :], nv[2][:, u, :], 1.0 / D, EPS, ALU.mult, ALU.add).then_inc(n_var2_set.sem, 1)
                    for u in range(2):
                        p_wait(pool, n_var2_set.sem, n_var2_set.now(i, u))
                        p_wait(pool, n_twice_set.sem, n_twice_set.old(i, u))
                        pool.tensor_tensor(nrs[1][:, u, :], nv[1][:, u, :], minus_half[:, 0:TPC], ALU.pow).then_inc(n_rstd2_set.sem, 1)
        end_phase(CN)

        def node_transformer(l):
            src_t, dst_t = (T3, T4) if l == 0 else (T4, T5)
            xin, xh, xhT, xc, tmp, yy, yb, zz, res = nb
            out_b = zz if l == 0 else nout
            n_ln1_turned, n_vo_done, n_ln2_turned = n_pe[0], n_pe[1], n_pe[2]
            n_down_done, n_up_done, n_ln1T_set = n_pe[8], n_pe[4:8], n_act[0]
            n_ln2T_set, n_hidden_set, n_stats1_set = n_act[1], n_act[3:7], n_dve[0]
            n_ln1_set, n_attended, n_stats2_set = n_dve[1], n_dve[3], n_dve[4]
            n_ln2_set, n_degree_added, n_mlp_added = n_dve[5], n_dve[6], n_dve[7]
            n_residual_added, n_stats3_set, n_result_set = n_dve[8], n_dve[9], n_dve[11]
            n_var1_set, n_rstd1_set, n_var2_set = n_pool[0], n_pool[1], n_pool[2]
            n_rstd2_set, n_bias_added, n_mlp_bias_added = n_pool[3], n_pool[4], n_pool[5]
            n_var3_set, n_rstd3_set = n_pool[6], n_pool[7]
            with nc.Block() as block:
                @block.sync
                def _(sp):
                    node_sync(sp, 4, [(4, src_t, xin, n_in, (n_ln1_set, n_bias_added))],
                              [(0, dst_t, out_b, n_out[0], n_result_set if l else n_mlp_added)],
                              [(0, T3, res, n_in2, (n_residual_added,))] if l else [], False, None)

                @block.tensor
                def _(pe):
                    def up(i, u):
                        for j in range(FJ):
                            if j < 2:
                                pe.wait_ge(n_hidden_set[2 + j].sem, n_hidden_set[2 + j].last(i, u))
                            else:
                                pe.wait_ge(n_hidden_set[j - 2].sem, n_hidden_set[j - 2].now(i, u))
                            pe.matmul(banks[4 + j % 2], w_up[:, l, j * D:(j + 1) * D], flat(yT, u), start=True,
                                      stop=True).then_inc(n_up_done[j].sem, 1)

                    def down(i, u):
                        pe.wait_ge(n_hidden_set[3].sem, n_hidden_set[3].now(i, u))
                        pe.wait_ge(n_mlp_added.sem, n_mlp_added.old(i, u))
                        for k in range(TPC):
                            for j in range(FJ):
                                last = pe.matmul(banks[6 + u][:, k * D:(k + 1) * D], hT[:, u, j, k * D:(k + 1) * D],
                                                 w_down[:, l, j, :], start=(j == 0), stop=(j == FJ - 1))
                        last.then_inc(n_down_done.sem, 1)

                    def step(i, first, second, third):
                        f, s = i + 4, i + 2
                        if second:
                            pe.wait_ge(n_ln2T_set.sem, n_ln2T_set.now(s, 0))
                            up(s, 0)
                        if first:
                            for u in range(2):
                                pe.wait_ge(n_ln1_set.sem, n_ln1_set.now(f, u))
                                pe.wait_ge(n_ln2T_set.sem, n_ln2T_set.old(f, u))
                                tiles_T(pe, banks[u], lambda k: xh[:, u, k, :], u).then_inc(n_ln1_turned.sem, 1)
                        if second:
                            pe.wait_ge(n_ln2T_set.sem, n_ln2T_set.now(s, 1))
                            up(s, 1)
                        if first:
                            for u in range(2):
                                pe.wait_ge(n_ln1T_set.sem, n_ln1T_set.now(f, u))
                                pe.wait_ge(n_degree_added.sem, n_degree_added.old(f, u))
                                for k in range(TPC):
                                    last = pe.matmul(banks[2 + u][:, k * D:(k + 1) * D], xhT[:, u, k, :], w_vo[:, l, :], start=True, stop=True)
                                last.then_inc(n_vo_done.sem, 1)
                        if second:
                            down(s, 0)
                            down(s, 1)
                        if first:
                            for u in range(2):
                                pe.wait_ge(n_ln2_set.sem, n_ln2_set.now(f, u))
                                tiles_T(pe, banks[u], lambda k: xh[:, u, k, :], u).then_inc(n_ln2_turned.sem, 1)
                    skewed3(pe, CN, step)

                @block.scalar
                def _(act):
                    def hidden(i, u):
                        for j in range(FJ):
                            act.wait_ge(n_up_done[j].sem, n_up_done[j].now(i, u))
                            if j == 0:
                                act.wait_ge(n_down_done.sem, n_down_done.old(i, u))
                            act.activation(hT[:, u, j, :], banks[4 + j % 2], ACT.Gelu,
                                           bias=b_up[:, l, j:j + 1]).then_inc(n_hidden_set[j].sem, 1)

                    def step(i, first, second, third):
                        f, s = i + 4, i + 2
                        if second:
                            hidden(s, 0)
                        if first:
                            for u in range(2):
                                act.wait_ge(n_ln1_turned.sem, n_ln1_turned.now(f, u))
                                act.wait_ge(n_vo_done.sem, n_vo_done.old(f, u))
                                act.copy(flat(xhT, u), banks[u]).then_inc(n_ln1T_set.sem, 1)
                        if second:
                            hidden(s, 1)
                        if first:
                            for u in range(2):
                                act.wait_ge(n_ln2_turned.sem, n_ln2_turned.now(f, u))
                                act.wait_ge(n_up_done[3].sem, n_up_done[3].old(f, u))
                                act.copy(flat(yT, u), banks[u]).then_inc(n_ln2T_set.sem, 1)
                    skewed3(act, CN, step)

                @block.vector
                def _(dve):
                    def step(i, first, second, third):
                        f = i + 4
                        if first:
                            for u in range(2):
                                dve.wait_ge(n_in.sem[u], n_in.now(f))
                                dve.wait_ge(n_ln1_set.sem, n_ln1_set.old(f, u))
                                stats(dve, nst[0], xin, u).then_inc(n_stats1_set.sem, 1)
                            for u in range(2):
                                dve.wait_ge(n_rstd1_set.sem, n_rstd1_set.now(f, u))
                                dve.wait_ge(n_ln2_turned.sem, n_ln2_turned.old(f, u))
                                normalise(dve, xh, xin, nst[0], nrs[0], u).then_inc(n_ln1_set.sem, 1)
                        if third:
                            for u in range(2):
                                dve.wait_ge(n_down_done.sem, n_down_done.now(i, u))
                                dve.wait_ge(n_mlp_bias_added.sem, n_mlp_bias_added.now(i, u))
                                if l == 0:
                                    dve.wait_ge(n_out[0].sem[u], n_out[0].old(i))
                                else:
                                    dve.wait_ge(n_residual_added.sem, n_residual_added.old(i, u))
                                dve.tensor_tensor(flat(zz, u), banks[6 + u], flat(yb, u), ALU.add).then_inc(n_mlp_added.sem, 1)
                        if third and l:
                            for u in range(2):
                                dve.wait_ge(n_mlp_added.sem, n_mlp_added.now(i, u))
                                dve.wait_ge(n_in2.sem[u], n_in2.now(i))
                                dve.wait_ge(n_result_set.sem, n_result_set.old(i, u))
                                dve.tensor_tensor(flat(nsum, u), flat(zz, u), flat(res, u), ALU.add).then_inc(n_residual_added.sem, 1)
                            for u in range(2):
                                dve.wait_ge(n_residual_added.sem, n_residual_added.now(i, u))
                                stats(dve, nst[2], nsum, u).then_inc(n_stats3_set.sem, 1)
                        if first:
                            for u in range(2):
                                dve.wait_ge(n_vo_done.sem, n_vo_done.now(f, u))
                                dve.wait_ge(n_attended.sem, n_attended.old(f, u))
                                for k in range(TPC):
                                    last = dve.scalar_tensor_tensor(tmp[:, u, k, :], u_vo[:, l, :], deg_node[:, bass.ds(f * TPC + (u * TPC + k), 1)],
                                                                    banks[2 + u][:, k * D:(k + 1) * D], ALU.mult, ALU.add)
                                last.then_inc(n_degree_added.sem, 1)
                            for u in range(2):
                                dve.wait_ge(n_degree_added.sem, n_degree_added.now(f, u))
                                dve.wait_ge(n_bias_added.sem, n_bias_added.now(f, u))
                                dve.wait_ge(n_mlp_bias_added.sem, n_mlp_bias_added.old(f, u))
                                dve.wait_ge(n_ln2_set.sem, n_ln2_set.old(f, u))
                                dve.tensor_tensor(flat(yy, u), flat(tmp, u), flat(xc, u), ALU.add).then_inc(n_attended.sem, 1)
                            for u in range(2):
                                dve.wait_ge(n_attended.sem, n_attended.now(f, u))
                                stats(dve, nst[1], yy, u).then_inc(n_stats2_set.sem, 1)
                        if third and l:
                            for u in range(2):
                                dve.wait_ge(n_rstd3_set.sem, n_rstd3_set.now(i, u))
                                dve.wait_ge(n_out[0].sem[u], n_out[0].old(i))
                                normalise(dve, nout, nsum, nst[2], nrs[2], u).then_inc(n_result_set.sem, 1)
                        if first:
                            for u in range(2):
                                dve.wait_ge(n_rstd2_set.sem, n_rstd2_set.now(f, u))
                                dve.wait_ge(n_ln1_turned.sem, n_ln1_turned.now(f, u))
                                normalise(dve, xh, yy, nst[1], nrs[1], u).then_inc(n_ln2_set.sem, 1)
                    skewed3(dve, CN, step)

                @block.gpsimd
                def _(pool):
                    def step(i, first, second, third):
                        f, s = i + 4, i + 2
                        if first:
                            for u in range(2):
                                p_wait(pool, n_ln1_set.sem, n_ln1_set.old(f, u))
                                rstd(pool, f, u, nst[0], nv[0], nrs[0], n_stats1_set, n_var1_set, n_rstd1_set)
                        if second:
                            for u in range(2):
                                p_wait(pool, n_attended.sem, n_attended.now(s, u))
                                p_wait(pool, n_mlp_added.sem, n_mlp_added.old(s, u))
                                pool.tensor_tensor(yb[:, u, :, :], yy[:, u, :, :],
                                                   b_down[:, l, :].unsqueeze(1).broadcast_to([D, TPC, D]), ALU.add).then_inc(n_mlp_bias_added.sem, 1)
                        if first:
                            for u in range(2):
                                p_wait(pool, n_attended.sem, n_attended.old(f, u))
                                pool.tensor_tensor(xc[:, u, :, :], xin[:, u, :, :],
                                                   c_vo[:, l, :].unsqueeze(1).broadcast_to([D, TPC, D]), ALU.add).then_inc(n_bias_added.sem, 1)
                        if third and l:
                            for u in range(2):
                                p_wait(pool, n_result_set.sem, n_result_set.old(i, u))
                                rstd(pool, i, u, nst[2], nv[2], nrs[2], n_stats3_set, n_var3_set, n_rstd3_set)
                        if first:
                            for u in range(2):
                                p_wait(pool, n_ln2_set.sem, n_ln2_set.old(f, u))
                                rstd(pool, f, u, nst[1], nv[1], nrs[1], n_stats2_set, n_var2_set, n_rstd2_set)
                    skewed3(pool, CN, step)
            end_phase(CN)

        node_transformer(0)
        node_transformer(1)

        xin, x_T, r0_T, r1_T, r2_T, r3_T, e_front, e_back, res = nb
        rows0, rows1, rows2, oo = yT, nsum, nout, nsb("node_result", [D, 2, TPC, D])
        m_front, m_back = nsb("node_m_front", [D, 2, TPC, D]), nsb("node_m_back", [D, 2, TPC, D])
        yy = nsb("node_yy", [D, 2, TPC, D])
        exp_done = (n_act[1], n_act[2], n_act[3], n_act[7])
        rows_done, min_done, elu_done = n_act[4:7], n_dve[4:8], n_dve[0:4]
        n_x_turned, n_product, n_rows_turned = n_pe[0], n_pe[1:5], n_pe[5:9]
        n_xT_set, n_sum_set, n_stats_set = n_act[0], n_dve[8], n_dve[9]
        n_result_set, n_var_set, n_rstd_set = n_dve[11], n_pool[0], n_pool[1]
        round_in, round_out = (x_T, r0_T, r1_T, r2_T), (r0_T, r1_T, r2_T, r3_T)
        with nc.Block() as block:
            @block.sync
            def _(sp):
                node_sync(sp, 4, [(4, T5, xin, n_in, (n_x_turned,))],
                          [(0, t["out"], oo, n_out[3], n_result_set), (2, T8, rows2, n_out[2], rows_done[2]),
                           (4, T6, rows0, n_out[0], rows_done[0]), (4, T7, rows1, n_out[1], rows_done[1])],
                          [(2, T5, res, n_in2, (n_sum_set,))], False, t["out"])

            @block.tensor
            def _(pe):
                def product(r, i):
                    for u in range(2):
                        if r == 0:
                            pe.wait_ge(n_xT_set.sem, n_xT_set.now(i, u))
                            pe.wait_ge(elu_done[1].sem, elu_done[1].old(i, u))
                        else:
                            pe.wait_ge(elu_done[r - 1].sem, elu_done[r - 1].now(i, u))
                            if r == 2:
                                pe.wait_ge(elu_done[3].sem, elu_done[3].old(i, u))
                        pe.matmul(banks[(2 if r < 2 else 6) + u], w_root[:, r, :], flat(round_in[r], u), start=True,
                                  stop=True).then_inc(n_product[r].sem, 1)

                def rows(r, i):
                    for u in range(2):
                        pe.wait_ge(elu_done[r].sem, elu_done[r].now(i, u))
                        if r == 1:
                            pe.wait_ge(rows_done[0].sem, rows_done[0].now(i, u))
                        elif r == 2:
                            pe.wait_ge(n_sum_set.sem, n_sum_set.old(i, u))
                        elif r == 3:
                            pe.wait_ge(rows_done[2].sem, rows_done[2].now(i, u))
                        tiles_T(pe, banks[(0 if r < 2 else 4) + u], lambda k: round_out[r][:, u, k, :], u).then_inc(n_rows_turned[r].sem, 1)

                def step(i, first, second, third):
                    f, s = i + 4, i + 2
                    if first:
                        for u in range(2):
                            pe.wait_ge(n_in.sem[u], n_in.now(f))
                            pe.wait_ge(rows_done[1].sem, rows_done[1].old(f, u))
                            tiles_T(pe, banks[u], lambda k: xin[:, u, k, :], u).then_inc(n_x_turned.sem, 1)
                    if second:
                        product(2, s)
                    if first:
                        product(0, f)
                    if second:
                        product(3, s)
                        rows(2, s)
                    if first:
                        product(1, f)
                    if second:
                        rows(3, s)
                    if first:
                        rows(0, f)
                        rows(1, f)
                skewed3(pe, CN, step)

            @block.scalar
            def _(act):
                def exps(r, i):
                    for u in range(2):
                        act.wait_ge(n_product[r].sem, n_product[r].now(i, u))
                        if r % 2:
                            act.wait_ge(min_done[r - 1].sem, min_done[r - 1].now(i, u))
                        else:
                            act.wait_ge(min_done[r + 1].sem, min_done[r + 1].old(i, u))
                        act.activation(flat(e_front if r < 2 else e_back, u), banks[(2 if r < 2 else 6) + u], ACT.Exp,
                                       bias=rel_col[:, r:r + 1]).then_inc(exp_done[r].sem, 1)

                def rows(r, i):
                    for u in range(2):
                        act.wait_ge(n_rows_turned[r].sem, n_rows_turned[r].now(i, u))
                        act.wait_ge(n_out[r].sem[u], n_out[r].old(i))
                        act.copy(flat((rows0, rows1, rows2)[r], u), banks[(0 if r < 2 else 4) + u]).then_inc(rows_done[r].sem, 1)

                def step(i, first, second, third):
                    f, s = i + 4, i + 2
                    if first:
                        for u in range(2):
                            act.wait_ge(n_x_turned.sem, n_x_turned.now(f, u))
                            act.wait_ge(n_product[0].sem, n_product[0].old(f, u))
                            act.copy(flat(x_T, u), banks[u]).then_inc(n_xT_set.sem, 1)
                    if second:
                        exps(2, s)
                    if first:
                        exps(0, f)
                    if second:
                        exps(3, s)
                        rows(2, s)
                    if first:
                        exps(1, f)
                        rows(0, f)
                        rows(1, f)
                skewed3(act, CN, step)

            @block.vector
            def _(dve):
                def elu(r, i):
                    m = m_front if r < 2 else m_back
                    for u in range(2):
                        dve.wait_ge(exp_done[r].sem, exp_done[r].now(i, u))
                        if r % 2:
                            dve.wait_ge(elu_done[r - 1].sem, elu_done[r - 1].now(i, u))
                        else:
                            dve.wait_ge(elu_done[r + 1].sem, elu_done[r + 1].old(i, u))
                        dve.tensor_scalar(flat(m, u), flat(e_front if r < 2 else e_back, u), 1.0, -1.0, ALU.min,
                                          ALU.add).then_inc(min_done[r].sem, 1)
                    for u in range(2):
                        dve.wait_ge(min_done[r].sem, min_done[r].now(i, u))
                        dve.wait_ge(n_rows_turned[r].sem, n_rows_turned[r].old(i, u))
                        if r == 1:
                            dve.wait_ge(n_product[2].sem, n_product[2].old(i, u))
                        dve.scalar_tensor_tensor(flat(round_out[r], u), banks[(2 if r < 2 else 6) + u], rel_col[:, r:r + 1],
                                                 flat(m, u), ALU.add, ALU.max).then_inc(elu_done[r].sem, 1)

                def step(i, first, second, third):
                    f, s = i + 4, i + 2
                    if second:
                        elu(2, s)
                    if third:
                        for u in range(2):
                            dve.wait_ge(n_rstd_set.sem, n_rstd_set.now(i, u))
                            dve.wait_ge(n_out[3].sem[u], n_out[3].old(i))
                            normalise(dve, oo, yy, nst[0], nrs[0], u).then_inc(n_result_set.sem, 1)
                    if first:
                        elu(0, f)
                    if second:
                        elu(3, s)
                    if first:
                        elu(1, f)
                    if second:
                        for u in range(2):
                            dve.wait_ge(n_rows_turned[3].sem, n_rows_turned[3].now(s, u))
                            dve.wait_ge(n_in2.sem[u], n_in2.now(s))
                            dve.wait_ge(n_result_set.sem, n_result_set.old(s, u))
                            dve.tensor_tensor(flat(yy, u), banks[4 + u], flat(res, u), ALU.add).then_inc(n_sum_set.sem, 1)
                        for u in range(2):
                            dve.wait_ge(n_sum_set.sem, n_sum_set.now(s, u))
                            stats(dve, nst[0], yy, u).then_inc(n_stats_set.sem, 1)
                skewed3(dve, CN, step)

            @block.gpsimd
            def _(pool):
                with pairs(pool, CN) as i:
                    for u in range(2):
                        p_wait(pool, n_result_set.sem, n_result_set.old(i, u))
                        rstd(pool, i, u, nst[0], nv[0], nrs[0], n_stats_set, n_var_set, n_rstd_set)
        end_phase(CN)
        nodes.close()

        msg = sb("msg", [D, 2, D])
        xd = sb("xd", [D, 2, D])
        res_e = sb("res_e", [D, 2, D])
        aT = sb("aT", [D, 2, 2 * D])
        z = sb("z", [D, 2, D])
        ex = sb("ex", [D, 2, D])
        em = sb("em", [D, 2, D])
        ye = sb("ye", [D, 2, D])
        yo = sb("yo", [D, 2, D])
        est = sb("est", [D, 2, 6])
        eag = sb("eag", [D, 2, 2])
        ev = sb("ev", [D, 2, 2])
        ers = sb("ers", [D, 2, 2])

        def slot_rows(table, c, base):
            return table[bass.ds(c * D + base, D), :]

        def edge_sync(sp, loads, stores):
            def load(c, u, which):
                table, base, buf, tr, _ = which
                sp.dma_start(buf[:, u, :], slot_rows(table, c, base)).then_inc(tr.sem[u], 16)

            def store(i, u):
                for table, base, buf, tr, sig in stores:
                    sp.wait_ge(sig.sem, sig.now(i, u))
                    sp.dma_start(slot_rows(table, i + u, base), buf[:, u, :]).then_inc(tr.sem[u], 16)
            for which in loads:
                load(0, 0, which)
                load(1, 1, which)
            with pairs(sp, ET - 2) as i:
                for which in loads:
                    for u in range(2):
                        sp.wait_ge(which[4].sem, which[4].now(i, u))
                        load(i + (u + 2), u, which)
                for u in range(2):
                    store(i, u)
            for u in range(2):
                store(ET - 2, u)
            for _, _, _, tr, _ in stores:
                for u in range(2):
                    sp.wait_ge(tr.sem[u], tr.end(ET))

        def layer_norm_stats(dve, i, u, x, made):
            dve.wait_ge(made.sem, made.now(i, u))
            dve.bn_stats(est[:, u, :], x[:, u, :]).then_inc(st_set.sem, 1)
            dve.wait_ge(st_set.sem, st_set.now(i, u))
            dve.wait_ge(ln_set.sem, ln_set.old(i, u))
            dve.nop(nofuse=True)
            dve.bn_aggr(eag[:, u, :], est[:, u, :]).then_inc(c_set.sem, 1)

        def layer_norm_rstd(pool, i, u):
            p_wait(pool, c_set.sem, c_set.now(i, u))
            p_wait(pool, ln_set.sem, ln_set.old(i, u))
            pool.tensor_scalar(ev[:, u, 0:1], eag[:, u, 1:2], EPS, None, ALU.add).then_inc(v_set.sem, 1)
            p_wait(pool, v_set.sem, v_set.now(i, u))
            pool.tensor_tensor(ers[:, u, 0:1], ev[:, u, 0:1], minus_half[:, 0:1], ALU.pow).then_inc(rs_set.sem, 1)

        def layer_norm_out(dve, i, u, x, out):
            dve.wait_ge(rs_set.sem, rs_set.now(i, u))
            return dve.tensor_scalar(out[:, u, :], x[:, u, :], eag[:, u, 0:1], ers[:, u, 0:1], ALU.subtract, ALU.mult)

        def mean_round(table, wl, wr, bias, out_t, elu, norm, residual=None, first=False, final=False):
            res_t = {"x": (XD0, 0), "t5": (T5, NP)}.get(residual)
            made = ln_set if norm else y_set
            made_buf = yo if norm else ye
            own_in = got_dst if first else got_own
            put = put_rows if final else put_out
            with nc.Block() as block:
                @block.gpsimd
                def _(pool):
                    def step(i, front, back):
                        if front:
                            f = i + 2
                            for u in range(2):
                                gather(pool, f, u, msg[:, u, :], table, x_src if first else g_src, 0,
                                       (agg_done.sem, agg_done.old(f, u))).then_inc(got_src.sem[u], 16)
                                if first:
                                    p_wait(pool, put_x.sem[u], put_x.old(f))
                                    gather(pool, f, u, xd[:, u, :], table, x_dst, 1,
                                           (agg_done.sem, agg_done.old(f, u))).then_inc(got_dst.sem[u], 16)
                        if back and norm:
                            for u in range(2):
                                layer_norm_rstd(pool, i, u)
                        if back and final:
                            for u in range(2):
                                p_wait(pool, put_rows.sem[u], put_rows.old(i))
                            pool.tensor_copy(idx2f[:, :], put_row[:, bass.ds(i, 2)]).then_inc(row_set.sem, 2)
                            p_wait(pool, row_set.sem, row_set.now(i, 1))
                            for u in range(2):
                                p_wait(pool, ln_set.sem, ln_set.now(i, u))
                                pool.indirect_dma_start(t["out"], bass.IndirectOffsetOnAxis(ap=idx2f[:, u:u + 1], axis=0),
                                                        yo[:, u, :], None, bounds_check=N - 1,
                                                        oob_is_err=False).then_inc(put_rows.sem[u], 16)
                    skewed(pool, ET, step)
                    if final:
                        for u in range(2):
                            pool.wait_ge(put_rows.sem[u], put_rows.end(ET))

                @block.sync
                def _(sp):
                    if first:
                        def step(i, front, back):
                            if front:
                                for u in range(2):
                                    sp.wait_ge(got_dst.sem[u], got_dst.now(i + 2))
                                    sp.dma_start(slot_rows(XD0, i + (u + 2), 0), xd[:, u, :]).then_inc(put_x.sem[u], 16)
                            if back:
                                for u in range(2):
                                    sp.wait_ge(made.sem, made.now(i, u))
                                    sp.dma_start(slot_rows(out_t, i + u, NP), made_buf[:, u, :]).then_inc(put_out.sem[u], 16)
                        skewed(sp, ET, step)
                        for u in range(2):
                            sp.wait_ge(put_out.sem[u], put_out.end(ET))
                            sp.wait_ge(put_x.sem[u], put_x.end(ET))
                    else:
                        loads = [(table, NP, xd, got_own, agg_done)]
                        if residual:
                            loads.append((res_t[0], res_t[1], res_e, got_res, y_set))
                        edge_sync(sp, loads, [] if final else [(out_t, NP, made_buf, put_out, made)])

                @block.tensor
                def _(pe):
                    with pairs(pe, ET) as i:
                        for u in range(2):
                            pe.wait_ge(seg_set.sem, seg_set.now(i, u))
                            pe.wait_ge(got_src.sem[u], got_src.now(i))
                            pe.wait_ge(own_in.sem[u], own_in.now(i))
                            pe.wait_ge(at_set.sem, at_set.old(i, u))
                            pe.wait_ge(carry_set.sem, carry_set.last(i, u))
                            pe.matmul(banks[2 + u][0:1, 0:D], seg[:, u, D - 1:D], msg[:, u, :], start=True, stop=False)
                            pe.matmul(banks[2 + u][0:1, 0:D], cont[0:1, u, D - 1:D], carry[0:1, 1 - u, 0:D], start=False, stop=True)
                            pe.matmul(banks[u][:, 0:D], msg[:, u, :], seg[:, u, :], start=True, stop=False)
                            pe.matmul(banks[u][:, 0:D], carry[0:1, 1 - u, 0:D], cont[0:1, u, :], start=False, stop=True)
                            pe.transpose(banks[u][:, D:2 * D], xd[:, u, :], ident[:, :]).then_inc(agg_done.sem, 1)
                        for u in range(2):
                            pe.wait_ge(at_set.sem, at_set.now(i, u))
                            pe.wait_ge(z_set.sem, z_set.old(i, u))
                            pe.matmul(banks[4 + u][:, 0:D], aT[:, u, 0:D], wl, start=True, stop=False)
                            pe.matmul(banks[4 + u][:, 0:D], aT[:, u, D:2 * D], wr, start=False, stop=True).then_inc(mm_done.sem, 1)

                @block.scalar
                def _(act):
                    with pairs(act, ET) as i:
                        for u in range(2):
                            act.wait_ge(agg_done.sem, agg_done.now(i, u))
                            act.copy(carry[0:1, u, 0:D], banks[2 + u][0:1, 0:D]).then_inc(carry_set.sem, 1)
                            act.wait_ge(mm_done.sem, mm_done.old(i, u))
                            act.copy(aT[:, u, :], banks[u][:, 0:2 * D]).then_inc(at_set.sem, 1)
                        for u in range(2):
                            if elu:
                                act.wait_ge(row_set2.sem, row_set2.now(i, u))
                                act.wait_ge(y_set.sem, y_set.old(i, u))
                                act.activation(ex[:, u, :], em[:, u, :], ACT.Exp).then_inc(e_set.sem, 1)
                            elif not norm:
                                act.wait_ge(z_set.sem, z_set.now(i, u))
                                act.wait_ge(put_out.sem[u], put_out.old(i))
                                act.activation(ye[:, u, :], z[:, u, :], ACT.Relu).then_inc(y_set.sem, 1)

                @block.vector
                def _(dve):
                    def step(i, front, back):
                        if front:
                            for u in range(2):
                                dve.wait_ge(agg_done.sem, agg_done.old(i + 2, u))
                                same_target(dve, i + 2, u, True).then_inc(seg_set.sem, 1)
                        if not back:
                            return
                        for u in range(2):
                            dve.wait_ge(mm_done.sem, mm_done.now(i, u))
                            dve.wait_ge(y_set.sem, y_set.old(i, u))
                            dve.tensor_tensor(z[:, u, :], banks[4 + u][:, 0:D], bias, ALU.add).then_inc(z_set.sem, 1)
                            if elu:
                                dve.wait_ge(z_set.sem, z_set.now(i, u))
                                dve.tensor_scalar(em[:, u, :], z[:, u, :], 0.0, None, ALU.min).then_inc(row_set2.sem, 1)
                        for u in range(2):
                            if elu:
                                dve.wait_ge(e_set.sem, e_set.now(i, u))
                                if norm:
                                    dve.scalar_tensor_tensor(em2[:, u, :], ex[:, u, :], -1.0, z[:, u, :], ALU.add, ALU.max).then_inc(elu_set.sem, 1)
                                    dve.wait_ge(elu_set.sem, elu_set.now(i, u))
                                    dve.wait_ge(got_res.sem[u], got_res.now(i))
                                    dve.wait_ge(ln_set.sem, ln_set.old(i, u))
                                    dve.tensor_tensor(ye[:, u, :], em2[:, u, :], res_e[:, u, :], ALU.add).then_inc(y_set.sem, 1)
                                else:
                                    dve.wait_ge(put.sem[u], put.old(i))
                                    dve.scalar_tensor_tensor(ye[:, u, :], ex[:, u, :], -1.0, z[:, u, :], ALU.add, ALU.max).then_inc(y_set.sem, 1)
                            elif norm:
                                dve.wait_ge(z_set.sem, z_set.now(i, u))
                                dve.wait_ge(got_res.sem[u], got_res.now(i))
                                dve.wait_ge(ln_set.sem, ln_set.old(i, u))
                                dve.scalar_tensor_tensor(ye[:, u, :], z[:, u, :], 0.0, res_e[:, u, :], ALU.max, ALU.add).then_inc(y_set.sem, 1)
                        if norm:
                            for u in range(2):
                                layer_norm_stats(dve, i, u, ye, y_set)
                            for u in range(2):
                                dve.wait_ge(put.sem[u], put.old(i))
                                layer_norm_out(dve, i, u, ye, yo).then_inc(ln_set.sem, 1)
                    skewed(dve, ET, step)
            end_phase(ET)

        row_set2, elu_set = edge_signal("min_set"), edge_signal("elu_set")
        em2 = sb("em2", [D, 2, D])
        idx2f = sb("idx2f", [D, 2], I32)
        product_signals = ("rows_made", "rows_summed", "rows_carried", "sums_set", "weighted", "sum_made", "products_set")
        (zp_done, zagg_done, zcarry, zT_set, w_done, l1_sum, prod_set) = [edge_signal(x) for x in product_signals]
        attention_signals = ("stats_set", "var_set", "rstd_set", "ln1_set", "ln1_turned", "ln1T_set", "qkv_done", "qkv_set",
                             "qk_set", "logits_set", "exp_set", "values_set", "summed", "sum_set", "quotient_set",
                             "quotient_turned", "quotientT_set", "out_done", "residual_set", "ln2_turned", "ln2T_set")
        (a_st, a_v, a_rs, a_ln, a_T, a_xT, a_mm, a_qkv, a_qk, a_att, a_exp, a_am, a_agg, a_num, a_ag,
         a_agt, a_agT, a_wo, a_x2, a_t2, a_t2s) = [edge_signal("attention_" + x) for x in attention_signals]
        start_signals()

        mean_round(t["x"], W["L0_gnn_W1_l"][:, :], W["L0_gnn_W1_r"][:, :], b1_row[:, :], T1, elu=False, norm=False, first=True)
        mean_round(T1, W["L0_gnn_W2_l"][:, :], W["L0_gnn_W2_r"][:, :], b2_row[:, :], T2, elu=False, norm=True, residual="x")

        zp = sb("zp", [D, 2, 2 * MUL + 9 * MUL])
        prod = sb("prod", [D, 2, 3, MUL, 3])
        pr1 = sb("pr1", [D, 2, MUL, 3])
        zT = sb("zT", [3 * MUL, 2, 4, D])
        G0, G1 = 2 * MUL, 3 * MUL
        NZ = G0 + 3 * G1
        with nc.Block() as block:
            @block.gpsimd
            def _(pool):
                def step(i, front, back):
                    if front:
                        for u in range(2):
                            gather(pool, i + 2, u, msg[:, u, :], T2, g_src, 0,
                                   (zp_done.sem, zp_done.old(i + 2, u))).then_inc(got_src.sem[u], 16)
                    if back:
                        for u in range(2):
                            layer_norm_rstd(pool, i, u)
                skewed(pool, ET, step)

            @block.sync
            def _(sp):
                edge_sync(sp, [(T2, NP, res_e, got_res, l1_sum)], [(T3, NP, yo, put_out, ln_set)])

            @block.vector
            def _(dve):
                def tensor_product(i):
                    for u in range(2):
                        dve.wait_ge(zagg_done.sem, zagg_done.old(i, u))
                        same_target(dve, i, u, False).then_inc(seg_set.sem, 1)
                    for u in range(2):
                        a = ea[:, bass.ds(i + u, 1), :].rearrange("p o c -> p (o c)")
                        m = coef[:, bass.ds(i + u, 1), :, :].rearrange("p o k i -> p (o k) i")
                        s = msg[:, u, 0:MUL]
                        v = msg[:, u, MUL:].rearrange("p (u i) -> p u i", i=3)
                        zk = zp[:, u, G0:].rearrange("p (k g w) -> p k g w", k=3, g=3)
                        dve.wait_ge(got_src.sem[u], got_src.now(i))
                        dve.tensor_tensor(pr1[:, u, :, :], v, a[:, 1:4].unsqueeze(1).broadcast_to([D, MUL, 3]), ALU.mult)
                        for k in range(3):
                            last = dve.tensor_tensor(prod[:, u, k, :, :], v, m[:, k, :].unsqueeze(1).broadcast_to([D, MUL, 3]), ALU.mult)
                        last.then_inc(prod_set.sem, 1)
                        dve.tensor_scalar(zp[:, u, 0:MUL], s, a[:, 0:1], None, ALU.mult)
                        for k in range(3):
                            dve.tensor_scalar(zk[:, k, 0, :], s, a[:, 1 + k:2 + k], None, ALU.mult)
                            dve.tensor_scalar(zk[:, k, 1, :], v[:, :, k], a[:, 0:1], None, ALU.mult)
                        dve.wait_ge(prod_set.sem, prod_set.now(i, u))
                        dve.tensor_reduce(zp[:, u, MUL:2 * MUL], pr1[:, u, :, :], AX.X, ALU.add)
                        dve.tensor_reduce(zk[:, :, 2, :], prod[:, u, :, :, :], AX.X, ALU.add).then_inc(zp_done.sem, 1)

                def sum_and_norm(i):
                    for u in range(2):
                        dve.wait_ge(w_done.sem, w_done.now(i, u))
                        dve.wait_ge(got_res.sem[u], got_res.now(i))
                        dve.wait_ge(ln_set.sem, ln_set.old(i, u))
                        dve.tensor_tensor(ye[:, u, 0:MUL], banks[6 + u][:, 0:MUL], res_e[:, u, 0:MUL], ALU.add)
                        dve.tensor_tensor(ye[:, u, MUL:].rearrange("p (w k) -> p w k", k=3),
                                          banks[6 + u][:, MUL:4 * MUL].rearrange("p (k w) -> p w k", k=3),
                                          res_e[:, u, MUL:].rearrange("p (w k) -> p w k", k=3), ALU.add).then_inc(l1_sum.sem, 1)
                    for u in range(2):
                        layer_norm_stats(dve, i, u, ye, l1_sum)
                    for u in range(2):
                        dve.wait_ge(put_out.sem[u], put_out.old(i))
                        layer_norm_out(dve, i, u, ye, yo).then_inc(ln_set.sem, 1)

                def step(i, front, back):
                    if front:
                        tensor_product(i + 2)
                    if back:
                        sum_and_norm(i)
                skewed(dve, ET, step)

            @block.tensor
            def _(pe):
                def group(k):
                    return (0, G0) if k == 0 else (G0 + (k - 1) * G1, G1)
                with pairs(pe, ET) as i:
                    for u in range(2):
                        pe.wait_ge(zp_done.sem, zp_done.now(i, u))
                        pe.wait_ge(seg_set.sem, seg_set.now(i, u))
                        pe.wait_ge(zT_set.sem, zT_set.old(i, u))
                        pe.wait_ge(zcarry.sem, zcarry.last(i, u))
                        pe.matmul(banks[2 + u][0:1, 0:NZ], seg[:, u, D - 1:D], zp[:, u, :], start=True, stop=False)
                        pe.matmul(banks[2 + u][0:1, 0:NZ], cont[0:1, u, D - 1:D], carry[0:1, 1 - u, 0:NZ], start=False, stop=True)
                        for k in range(4):
                            at, n = group(k)
                            pe.matmul(banks[u][0:n, k * D:(k + 1) * D], zp[:, u, at:at + n], seg[:, u, :], start=True, stop=False)
                            last = pe.matmul(banks[u][0:n, k * D:(k + 1) * D], carry[0:1, 1 - u, at:at + n], cont[0:1, u, :],
                                             start=False, stop=True)
                        last.then_inc(zagg_done.sem, 1)
                    for u in range(2):
                        pe.wait_ge(zT_set.sem, zT_set.now(i, u))
                        pe.wait_ge(l1_sum.sem, l1_sum.old(i, u))
                        for k in range(4):
                            n = group(k)[1]
                            last = pe.matmul(banks[6 + u][:, k * MUL:(k + 1) * MUL], zT[0:n, u, k, :],
                                             (tp0 if k == 0 else tp1)[:, :], start=True, stop=True)
                        last.then_inc(w_done.sem, 1)

            @block.scalar
            def _(act):
                with pairs(act, ET) as i:
                    for u in range(2):
                        act.wait_ge(zagg_done.sem, zagg_done.now(i, u))
                        act.copy(carry[0:1, u, 0:NZ], banks[2 + u][0:1, 0:NZ]).then_inc(zcarry.sem, 1)
                        act.wait_ge(w_done.sem, w_done.old(i, u))
                        act.copy(zT[0:G0, u, 0, :], banks[u][0:G0, 0:D])
                        act.copy(zT[:, u, 1:4, :], banks[u][0:G1, D:4 * D].rearrange("p (k e) -> p k e", k=3)).then_inc(zT_set.sem, 1)
        end_phase(ET)

        xp = sb("xp", [D, 2, 2, D])
        raw2 = sb("raw2", [D, 2, 2, D])
        xpT = sb("xpT", [D, 2, 2, D])
        add_s = sb("add_s", [D, 2, 2 * D])
        add_d = sb("add_d", [D, 2, 3 * D])
        kv_s = sb("kv_s", [D, 2, 2 * D])
        qkv_d = sb("qkv_d", [D, 2, 3 * D])
        qk = sb("qk", [D, 2, 2, H, HD])
        att = sb("att", [D, 2, 2, H])
        att2 = sb("att2", [D, 2, 2, H])
        exa = sb("exa", [D, 2, 2, H])
        NM = D + H
        am = sb("am", [D, 2, NM])
        own = sb("own", [D, 2, NM])
        num = sb("num", [D, 2, NM])
        rden = sb("rden", [D, 2, H])
        ag = sb("ag", [D, 2, D])
        agT = sb("agT", [D, 2, D])
        xo = sb("xo", [D, 2, D])
        x2 = sb("x2", [D, 2, D])
        hE = sb("hE", [D, 2, FJ, D])
        z2 = sb("z2", [D, 2, D])
        ast2 = sb("ast2", [D, 2, 2, 3])

        def attention_round(l):
            src_t, dst_t = (T3, T4) if l == 0 else (T4, T5)
            with nc.Block() as block:
                @block.gpsimd
                def _(pool):
                    def step(i, gathers, first, second, third, last):
                        g, f, s, q = i + 8, i + 6, i + 4, i + 2
                        if first:
                            for u in range(2):
                                p_wait(pool, a_st.sem, a_st.now(f, u))
                                p_wait(pool, a_ln.sem, a_ln.old(f, u))
                                pool.tensor_scalar(aev[:, u, :], ast2[:, u, :, 2], 1.0 / D, EPS, ALU.mult, ALU.add).then_inc(a_v.sem, 1)
                                p_wait(pool, a_v.sem, a_v.now(f, u))
                                pool.tensor_tensor(ers2[:, u, :], aev[:, u, :], minus_half[:, 0:2], ALU.pow).then_inc(a_rs.sem, 1)
                        if gathers:
                            for u in range(2):
                                gather(pool, g, u, raw2[:, u, 0, :], src_t, g_src, 0,
                                       (a_ln.sem, a_ln.old(g, u))).then_inc(got_src.sem[u], 16)
                        if second:
                            for u in range(2):
                                layer_norm_rstd(pool, s, u)
                        if third and l:
                            for u in range(2):
                                p_wait(pool, f_st.sem, f_st.now(q, u))
                                p_wait(pool, f_ln.sem, f_ln.old(q, u))
                                pool.tensor_scalar(fv[:, u, :], fag[:, u, 1:2], EPS, None, ALU.add).then_inc(f_v.sem, 1)
                                p_wait(pool, f_v.sem, f_v.now(q, u))
                                pool.tensor_tensor(frs[:, u, :], fv[:, u, :], minus_half[:, 0:1], ALU.pow).then_inc(f_rs.sem, 1)
                        if gathers:
                            for u in range(2):
                                gather(pool, g, u, raw2[:, u, 1, :], src_t, g_dst, 1,
                                       (xo_set.sem, xo_set.old(g, u))).then_inc(got_dst.sem[u], 16)
                    skewed5(pool, ET, step)

                @block.sync
                def _(sp):
                    if l == 0:
                        edge_sync(sp, [], [(dst_t, NP, z2, put_out, y_set)])
                    else:
                        edge_sync(sp, [(T3, NP, res_e, got_res, f_sum)], [(dst_t, NP, yo, put_out, f_ln)])

                @block.vector
                def _(dve):
                    def targets(i, u):
                        dve.wait_ge(a_agg.sem, a_agg.old(i, u))
                        same_target(dve, i, u, False).then_inc(seg_set.sem, 1)

                    def row_stats(i, u):
                        dve.wait_ge(got_src.sem[u], got_src.now(i))
                        dve.wait_ge(got_dst.sem[u], got_dst.now(i))
                        dve.bn_stats(ast2[:, u, :, :].rearrange("p e f -> p (e f)"),
                                     raw2[:, u, :, :].rearrange("p e d -> p d e")).then_inc(a_st.sem, 1)

                    def additions(i, u):
                        dve.wait_ge(a_qkv.sem, a_qkv.old(i, u))
                        dve.scalar_tensor_tensor(add_s[:, u, :], u_qkv[:, l, D:], deg_src[:, bass.ds(i + u, 1)],
                                                 c_qkv[:, l, D:], ALU.mult, ALU.add)
                        dve.scalar_tensor_tensor(add_d[:, u, :], u_qkv[:, l, :], deg_dst[:, bass.ds(i + u, 1)],
                                                 c_qkv[:, l, :], ALU.mult, ALU.add).then_inc(add_set.sem, 1)

                    def normed_rows(i, u):
                        dve.wait_ge(a_rs.sem, a_rs.now(i, u))
                        dve.wait_ge(a_T.sem, a_T.old(i, u))
                        for j in range(2):
                            last = dve.tensor_scalar(xp[:, u, j, :], raw2[:, u, j, :], ast2[:, u, j, 1:2], ers2[:, u, j:j + 1],
                                                     ALU.subtract, ALU.mult)
                        last.then_inc(a_ln.sem, 1)

                    def projections(i, u):
                        dve.wait_ge(a_mm.sem, a_mm.now(i, u))
                        dve.wait_ge(add_set.sem, add_set.now(i, u))
                        dve.wait_ge(a_am.sem, a_am.old(i, u))
                        dve.tensor_tensor(kv_s[:, u, :], banks[u][:, 2 * D:4 * D], add_s[:, u, :], ALU.add)
                        dve.tensor_tensor(qkv_d[:, u, :], banks[2 + u][:, 0:3 * D], add_d[:, u, :], ALU.add).then_inc(a_qkv.sem, 1)

                    def logits(i, u):
                        dve.wait_ge(a_qkv.sem, a_qkv.now(i, u))
                        q = qkv_d[:, u, 0:D]
                        dve.tensor_tensor(qk[:, u, 0].rearrange("p h d -> p (h d)"), q, kv_s[:, u, 0:D], ALU.mult)
                        dve.tensor_tensor(qk[:, u, 1].rearrange("p h d -> p (h d)"), q, qkv_d[:, u, D:2 * D], ALU.mult).then_inc(a_qk.sem, 1)

                    def logit_sums(i, u):
                        dve.wait_ge(a_qk.sem, a_qk.now(i, u))
                        dve.tensor_reduce(att[:, u, :, :], qk[:, u, :, :, :], AX.X, ALU.add).then_inc(att_sum.sem, 1)

                    def clip_above(i, u):
                        dve.wait_ge(att_sum.sem, att_sum.now(i, u))
                        dve.tensor_scalar(att2[:, u, :, :], att[:, u, :, :], HD ** -0.5, ATT_CLIP, ALU.mult, ALU.min).then_inc(att_min.sem, 1)

                    def clip_below(i, u):
                        dve.wait_ge(att_min.sem, att_min.now(i, u))
                        dve.wait_ge(a_exp.sem, a_exp.old(i, u))
                        dve.tensor_scalar(att3[:, u, :, :], att2[:, u, :, :], -ATT_CLIP, None, ALU.max).then_inc(a_att.sem, 1)

                    def weighted_values(i, u):
                        dve.wait_ge(a_exp.sem, a_exp.now(i, u))
                        dve.wait_ge(a_num.sem, a_num.old(i, u))
                        for j, (to, v) in enumerate([(am, kv_s[:, u, D:2 * D]), (own, qkv_d[:, u, 2 * D:3 * D])]):
                            dve.tensor_tensor(to[:, u, 0:D].rearrange("p (h d) -> p h d", d=HD),
                                              v.rearrange("p (h d) -> p h d", d=HD),
                                              exa[:, u, j, :].unsqueeze(2).broadcast_to([D, H, HD]), ALU.mult)
                            last = dve.tensor_copy(to[:, u, D:NM], exa[:, u, j, :])
                        last.then_inc(a_am.sem, 1)

                    def own_row(i, u):
                        dve.wait_ge(a_x2.sem, a_x2.old(i, u))
                        dve.tensor_tensor(xo[:, u, :], raw2[:, u, 1, :], bo_row[:, l, :], ALU.add).then_inc(xo_set.sem, 1)

                    def total(i, u):
                        dve.wait_ge(a_agg.sem, a_agg.now(i, u))
                        dve.wait_ge(a_am.sem, a_am.now(i, u))
                        dve.wait_ge(carry_set.sem, carry_set.now(i, u))
                        dve.wait_ge(a_ag.sem, a_ag.old(i, u))
                        dve.tensor_tensor(num[:, u, :], banks[4 + u][:, 0:NM], own[:, u, :], ALU.add).then_inc(a_num.sem, 1)

                    def inverse(i, u):
                        dve.wait_ge(a_num.sem, a_num.now(i, u))
                        dve.reciprocal(rden[:, u, :], num[:, u, D:NM]).then_inc(rden_set.sem, 1)

                    def quotient(i, u):
                        dve.wait_ge(rden_set.sem, rden_set.now(i, u))
                        dve.wait_ge(a_agt.sem, a_agt.old(i, u))
                        dve.tensor_tensor(ag[:, u, :].rearrange("p (h d) -> p h d", d=HD),
                                          num[:, u, 0:D].rearrange("p (h d) -> p h d", d=HD),
                                          rden[:, u, :].unsqueeze(2).broadcast_to([D, H, HD]), ALU.mult).then_inc(a_ag.sem, 1)

                    def residual(i, u):
                        dve.wait_ge(xo_set.sem, xo_set.now(i, u))
                        dve.wait_ge(a_wo.sem, a_wo.now(i, u))
                        dve.wait_ge(c_set.sem, c_set.old(i, u))
                        dve.wait_ge(z_set.sem, z_set.old(i, u))
                        dve.tensor_tensor(x2[:, u, :], banks[4 + u][:, 0:D], xo[:, u, :], ALU.add).then_inc(a_x2.sem, 1)

                    def mlp_input(i, u):
                        dve.wait_ge(a_t2.sem, a_t2.old(i, u))
                        dve.wait_ge(y_set.sem, y_set.old(i, u))
                        layer_norm_out(dve, i, u, x2, yln).then_inc(ln_set.sem, 1)
                        dve.tensor_tensor(z[:, u, :], x2[:, u, :], b_down[:, l, :], ALU.add).then_inc(z_set.sem, 1)

                    def mlp_output(i, u):
                        dve.wait_ge(mm_done.sem, mm_done.now(i, u))
                        dve.wait_ge(z_set.sem, z_set.now(i, u))
                        if l == 0:
                            dve.wait_ge(put_out.sem[u], put_out.old(i))
                        else:
                            dve.wait_ge(f_sum.sem, f_sum.old(i, u))
                        dve.tensor_tensor(z2[:, u, :], banks[6 + u][:, 0:D], z[:, u, :], ALU.add).then_inc(y_set.sem, 1)

                    def final_sum(i, u):
                        dve.wait_ge(y_set.sem, y_set.now(i, u))
                        dve.wait_ge(got_res.sem[u], got_res.now(i))
                        dve.wait_ge(f_ln.sem, f_ln.old(i, u))
                        dve.tensor_tensor(ye[:, u, :], z2[:, u, :], res_e[:, u, :], ALU.add).then_inc(f_sum.sem, 1)
                        dve.wait_ge(f_sum.sem, f_sum.now(i, u))
                        dve.bn_stats(fst[:, u, :], ye[:, u, :]).then_inc(f_bn.sem, 1)
                        dve.wait_ge(f_bn.sem, f_bn.now(i, u))
                        dve.nop(nofuse=True)
                        dve.bn_aggr(fag[:, u, :], fst[:, u, :]).then_inc(f_st.sem, 1)

                    def final_norm(i, u):
                        dve.wait_ge(f_rs.sem, f_rs.now(i, u))
                        dve.wait_ge(put_out.sem[u], put_out.old(i))
                        dve.tensor_scalar(yo[:, u, :], ye[:, u, :], fag[:, u, 0:1], frs[:, u, :], ALU.subtract,
                                          ALU.mult).then_inc(f_ln.sem, 1)

                    def both(stage, i):
                        for u in range(2):
                            stage(i, u)

                    def step(i, gathers, first, second, third, last):
                        f, s, q = i + 6, i + 4, i + 2
                        if third:
                            both(mlp_input, q)
                        if second:
                            both(logits, s)
                            both(logit_sums, s)
                            both(clip_above, s)
                            both(clip_below, s)
                        if last and l:
                            both(final_norm, i)
                        if first:
                            both(row_stats, f)
                        if second:
                            both(targets, s)
                            both(weighted_values, s)
                        if first:
                            both(additions, f)
                            both(normed_rows, f)
                        if second:
                            both(total, s)
                            both(inverse, s)
                            both(quotient, s)
                        if first:
                            both(projections, f)
                        if second:
                            both(residual, s)
                        if first:
                            both(own_row, f)
                        if second:
                            for u in range(2):
                                layer_norm_stats(dve, s, u, x2, a_x2)
                        if third:
                            both(mlp_output, q)
                            if l:
                                both(final_sum, q)
                    skewed5(dve, ET, step)

                @block.tensor
                def _(pe):
                    def down(i, u):
                        pe.wait_ge(g_last.sem, g_last.now(i, u))
                        for j in range(FJ):
                            end = pe.matmul(banks[6 + u][:, 0:D], hE[:, u, j, :], w_down[:, l, j, :], start=(j == 0), stop=(j == FJ - 1))
                        end.then_inc(mm_done.sem, 1)

                    def step(i, gathers, first, second, third, last):
                        f, s, q = i + 6, i + 4, i + 2
                        if third:
                            for u in range(2):
                                pe.wait_ge(ln_set.sem, ln_set.now(q, u))
                                pe.wait_ge(y_set.sem, y_set.old(q, u))
                                pe.transpose(banks[6 + u][:, 0:D], yln[:, u, :], ident[:, :]).then_inc(a_t2.sem, 1)
                            for u in range(2):
                                pe.wait_ge(a_t2s.sem, a_t2s.now(q, u))
                                for j in range(FJ):
                                    end = pe.matmul(banks[6 + u][:, j * D:(j + 1) * D], w_up[:, l, j * D:(j + 1) * D], yT[:, u, :], start=True, stop=True)
                                end.then_inc(up_done.sem, 1)
                        if second:
                            for u in range(2):
                                agg = banks[4 + u]
                                pe.wait_ge(a_am.sem, a_am.now(s, u))
                                pe.wait_ge(seg_set.sem, seg_set.now(s, u))
                                pe.wait_ge(a_x2.sem, a_x2.old(s, u))
                                pe.wait_ge(carry_set.sem, carry_set.last(s, u))
                                pe.matmul(agg[0:1, NM:2 * NM], seg[:, u, D - 1:D], am[:, u, :], start=True, stop=False)
                                pe.matmul(agg[0:1, NM:2 * NM], cont[0:1, u, D - 1:D], carry[0:1, 1 - u, 0:NM], start=False, stop=True)
                                pe.matmul(agg[:, 0:NM], seg[:, u, :], am[:, u, :], start=True, stop=False)
                                pe.matmul(agg[:, 0:NM], cont[0:1, u, :], carry[0:1, 1 - u, 0:NM], start=False, stop=True).then_inc(a_agg.sem, 1)
                        if first:
                            for u in range(2):
                                pe.wait_ge(a_ln.sem, a_ln.now(f, u))
                                pe.wait_ge(a_qkv.sem, a_qkv.old(f, u))
                                for j in range(2):
                                    end = pe.transpose(banks[u][:, j * D:(j + 1) * D], xp[:, u, j, :], ident[:, :])
                                end.then_inc(a_T.sem, 1)
                        if third:
                            down(q, 0)
                        if first:
                            for u in range(2):
                                pe.wait_ge(a_xT.sem, a_xT.now(f, u))
                                pe.matmul(banks[u][:, 2 * D:4 * D], xpT[:, u, 0, :], w_qkv[:, l, D:3 * D], start=True, stop=True)
                                pe.matmul(banks[2 + u][:, 0:3 * D], xpT[:, u, 1, :], w_qkv[:, l, :], start=True, stop=True).then_inc(a_mm.sem, 1)
                        if second:
                            for u in range(2):
                                pe.wait_ge(a_ag.sem, a_ag.now(s, u))
                                pe.transpose(banks[4 + u][:, 384:512], ag[:, u, :], ident[:, :]).then_inc(a_agt.sem, 1)
                        if third:
                            down(q, 1)
                        if second:
                            for u in range(2):
                                pe.wait_ge(a_agT.sem, a_agT.now(s, u))
                                pe.matmul(banks[4 + u][:, 0:D], agT[:, u, :], w_o[:, l, :], start=True, stop=True).then_inc(a_wo.sem, 1)
                    skewed5(pe, ET, step)

                @block.scalar
                def _(act):
                    def step(i, gathers, first, second, third, last):
                        f, s, q = i + 6, i + 4, i + 2
                        if third:
                            for u in range(2):
                                act.wait_ge(a_t2.sem, a_t2.now(q, u))
                                act.wait_ge(up_done.sem, up_done.old(q, u))
                                act.copy(yT[:, u, :], banks[6 + u][:, 0:D]).then_inc(a_t2s.sem, 1)
                        if second:
                            for u in range(2):
                                act.wait_ge(a_att.sem, a_att.now(s, u))
                                act.wait_ge(a_am.sem, a_am.old(s, u))
                                act.activation(exa[:, u, :, :], att3[:, u, :, :], ACT.Exp).then_inc(a_exp.sem, 1)
                        if third:
                            for u in range(2):
                                act.wait_ge(up_done.sem, up_done.now(q, u))
                                act.wait_ge(mm_done.sem, mm_done.old(q, u))
                                for j in range(FJ):
                                    end = act.activation(hE[:, u, j, :], banks[6 + u][:, j * D:(j + 1) * D], ACT.Gelu, bias=b_up[:, l, j:j + 1])
                                end.then_inc(g_last.sem, 1)
                        if second:
                            for u in range(2):
                                act.wait_ge(a_agg.sem, a_agg.now(s, u))
                                act.copy(carry[0:1, u, 0:NM], banks[4 + u][0:1, NM:2 * NM]).then_inc(carry_set.sem, 1)
                        if first:
                            for u in range(2):
                                act.wait_ge(a_T.sem, a_T.now(f, u))
                                act.wait_ge(a_mm.sem, a_mm.old(f, u))
                                act.copy(xpT[:, u].rearrange("p e d -> p (e d)"), banks[u][:, 0:2 * D]).then_inc(a_xT.sem, 1)
                        if second:
                            for u in range(2):
                                act.wait_ge(a_agt.sem, a_agt.now(s, u))
                                act.wait_ge(a_wo.sem, a_wo.old(s, u))
                                act.copy(agT[:, u, :], banks[4 + u][:, 384:512]).then_inc(a_agT.sem, 1)
                    skewed5(act, ET, step)
            end_phase(ET)

        ers2 = sb("ers2", [D, 2, 2])
        aev = sb("aev", [D, 2, 2])
        att3 = sb("att3", [D, 2, 2, H])
        yln, yT = sb("yln", [D, 2, D]), sb("yT", [D, 2, D])
        fst, fag, fv, frs = sb("fst", [D, 2, 6]), sb("fag", [D, 2, 2]), sb("fv", [D, 2, 1]), sb("frs", [D, 2, 1])
        names = ("add_set", "att_sum", "att_min", "rden_set", "xo_set", "g_last", "up_done", "f_sum", "f_bn", "f_st", "f_v", "f_rs", "f_ln")
        (add_set, att_sum, att_min, rden_set, xo_set, g_last, up_done, f_sum, f_bn, f_st, f_v, f_rs, f_ln) = map(edge_signal, names)
        start_signals()
        with nc.Block() as block:
            @block.vector
            def _(dve):
                dve.memset(carry[:, :, :], 0.0)
                dve.drain()
        attention_round(0)
        attention_round(1)

        def root(l):
            return w_rel[:, l, :], w_root[:, l, :], rel_row[:, l, :]
        mean_round(T5, *root(0), T6, elu=True, norm=False)
        mean_round(T6, *root(1), T7, elu=True, norm=False)
        mean_round(T7, *root(2), T8, elu=True, norm=False)
        mean_round(T8, *root(3), None, elu=True, norm=True, residual="t5", final=True)


_INS = ['x',
        'src',
        'dst',
        'edge_attr_9',
        'L0_gnn_W1_l',
        'L0_gnn_b1',
        'L0_gnn_W1_r',
        'L0_gnn_W2_l',
        'L0_gnn_b2',
        'L0_gnn_W2_r',
        'L1_gnn_w0',
        'L1_gnn_w1',
        'L1_gnn_w2',
        'L1_gnn_w3',
        'L1_gnn_w4',
        'L2_gnn_Wq',
        'L2_gnn_bq',
        'L2_gnn_Wk',
        'L2_gnn_bk',
        'L2_gnn_Wv',
        'L2_gnn_bv',
        'L2_gnn_Wo',
        'L2_gnn_bo',
        'L2_gnn_Wpos',
        'L2_gnn_bpos',
        'L2_gnn_Wdeg',
        'L2_gnn_bdeg',
        'L2_gnn_ln1_g',
        'L2_gnn_ln1_b',
        'L2_gnn_ln2_g',
        'L2_gnn_ln2_b',
        'L2_gnn_W1',
        'L2_gnn_b1',
        'L2_gnn_W2',
        'L2_gnn_b2',
        'L3_gnn_Ws_rel',
        'L3_gnn_bs_rel',
        'L3_gnn_Ws_root']


def kernel(**inputs):
    import numpy as _np
    import concourse.bacc as _bacc
    from concourse import mybir as _mybir
    from concourse.bass_utils import run_bass_kernel_spmd as _run

    nc = _bacc.Bacc("TRN2", target_bir_lowering=False, num_devices=1)
    arrays, tensors = {}, {}
    for name in _INS:
        a = _np.ascontiguousarray(inputs[name])
        arrays[f"in_{name}_dram"] = a
        tensors[name] = nc.dram_tensor(f"in_{name}_dram", a.shape, _mybir.dt.from_np(a.dtype), kind="ExternalInput").ap()
    shape = list(inputs["x"].shape)
    tensors["out"] = nc.dram_tensor("out_0_dram", shape, _mybir.dt.from_np(_np.dtype("float32")), kind="ExternalOutput").ap()
    gnn_stack(nc, tensors)
    r = _run(nc, [arrays], core_ids=[0])
    return r.results[0]["out_0_dram"]
```
